# Optimizing a Trainium2 kernel written in Bass

```python
import numpy as np
import jax
import jax.numpy as jnp

def _softmax(x, axis=-1):
    return jax.nn.softmax(x, axis=axis)

def _gelu(x):
    return jax.nn.gelu(x, approximate=True)

def _silu(x):
    return jax.nn.silu(x)

def _sigmoid(x):
    return jax.nn.sigmoid(x)

def _layernorm(x, axis=-1, eps=1e-05):
    m = jnp.mean(x, axis=axis, keepdims=True)
    v = jnp.var(x, axis=axis, keepdims=True)
    return (x - m) / jnp.sqrt(v + eps)

def _scatter_add(tgt, idx, src, axis=0):
    return tgt.at[idx].add(src)

def _segment_sum(src, seg, n):
    return jax.ops.segment_sum(src, seg, n)
kernel_name = 'mk_adaln_d1_jaxref_r4_dd6f08'

def setup_inputs(seed: int=0):
    np.random.seed(seed)
    _w = jnp.asarray

    def _L0_attn_setup():
        import jax, jax.numpy as jnp
        import numpy as np
        D_MODEL = 256
        N_HEADS = 16
        key = jax.random.key(seed)
        kx, kw, kb = jax.random.split(key, 3)
        x = jax.random.normal(kx, (2, 512, D_MODEL), dtype=jnp.float32)
        W = jax.random.normal(kw, (3 * D_MODEL, D_MODEL), dtype=jnp.float32) / np.sqrt(D_MODEL)
        b = jax.random.normal(kb, (3 * D_MODEL,), dtype=jnp.float32) * 0.02
        return {'x': x, 'W': W, 'b': b}
    _L0_attn_in = _L0_attn_setup()

    def _L0_ffn_setup():
        import jax, jax.numpy as jnp
        import numpy as np
        B, T, C = (2, 512, 256)
        H, D = (16, 64)
        CR = 8
        R = C // CR
        ROPE = D // 2
        NOPE = D - ROPE
        E, K, I, S = (8, 2, 128, 1)
        THETA = 100000.0
        EPS = 1e-05

        def _rmsnorm(x, w):
            rms = jnp.sqrt(jnp.mean(x * x, axis=-1, keepdims=True) + EPS)
            return w * (x / rms)

        def _rope(xh):
            d = xh.shape[-1]
            t = jnp.arange(xh.shape[2], dtype=jnp.float32)
            freqs = 1.0 / THETA ** (jnp.arange(0, d, 2, dtype=jnp.float32) / d)
            ang = jnp.outer(t, freqs)
            cos, sin = (jnp.cos(ang), jnp.sin(ang))
            xr = xh.reshape(xh.shape[:-1] + (d // 2, 2))
            x0, x1 = (xr[..., 0], xr[..., 1])
            rot = jnp.stack([x0 * cos - x1 * sin, x0 * sin + x1 * cos], axis=-1)
            return rot.reshape(xh.shape)

        def _attention(x, Wq, Wkva, Wkvb, Wo):
            b, t, _ = x.shape
            q = (x @ Wq).reshape(b, t, H, D).transpose(0, 2, 1, 3)
            ckv = x @ Wkva
            kv_latent, k_rope = (ckv[:, :, :R], ckv[:, :, R:])
            kv = (kv_latent @ Wkvb).reshape(b, t, H, NOPE).transpose(0, 2, 1, 3)
            k_rope = jnp.broadcast_to(k_rope[:, None, :, :], (b, H, t, ROPE))
            q_nope, q_rope = (q[..., :NOPE], q[..., NOPE:])
            q = jnp.concatenate([q_nope, _rope(q_rope)], axis=-1)
            k = jnp.concatenate([kv, _rope(k_rope)], axis=-1)
            v = jnp.concatenate([kv, jnp.zeros_like(k_rope)], axis=-1)
            att = jnp.einsum('bhqd,bhkd->bhqk', q, k) / jnp.sqrt(jnp.float32(D))
            mask = jnp.tril(jnp.ones((t, t), dtype=bool))
            att = jnp.where(mask, att, jnp.float32(-jnp.inf))
            att = jax.nn.softmax(att, axis=-1)
            y = jnp.einsum('bhqk,bhkd->bhqd', att, v)
            y = y.transpose(0, 2, 1, 3).reshape(b, t, H * D)
            return y @ Wo

        def _experts(x_flat, Wg, Wu, Wd):
            g = jax.nn.silu(jnp.einsum('nc,eci->nei', x_flat, Wg))
            u = jnp.einsum('nc,eci->nei', x_flat, Wu)
            return jnp.einsum('nei,eic->nec', g * u, Wd)

        def _moe(x, Wgate, expert_bias, Wg, Wu, Wd, sWg, sWu, sWd):
            b, t, c = x.shape
            xf = x.reshape(-1, c)
            shared = jnp.mean(_experts(xf, sWg, sWu, sWd), axis=1)
            logits = xf @ Wgate + expert_bias
            probs = jax.nn.softmax(logits, axis=-1)
            topk_p, topk_i = jax.lax.top_k(probs, K)
            topk_p = topk_p / jnp.sum(topk_p, axis=-1, keepdims=True)
            comb = jnp.sum(jax.nn.one_hot(topk_i, E, dtype=xf.dtype) * topk_p[..., None], axis=1)
            routed = jnp.einsum('ne,nec->nc', comb, _experts(xf, Wg, Wu, Wd))
            return (shared + routed).reshape(b, t, c)
        key = jax.random.key(seed)
        ks = jax.random.split(key, 16)
        w = lambda k, shp: jax.random.normal(k, shp, dtype=jnp.float32) * 0.02
        return {'x': jax.random.normal(ks[0], (B, T, C), dtype=jnp.float32), 'w_ln1': jnp.ones((C,), jnp.float32), 'Wq': w(ks[1], (C, H * D)), 'Wkva': w(ks[2], (C, R + ROPE)), 'Wkvb': w(ks[3], (R, H * NOPE)), 'Wo': w(ks[4], (H * D, C)), 'w_ln2': jnp.ones((C,), jnp.float32), 'Wgate': w(ks[5], (C, E)), 'expert_bias': jnp.zeros((E,), jnp.float32), 'Wg': w(ks[6], (E, C, I)), 'Wu': w(ks[7], (E, C, I)), 'Wd': w(ks[8], (E, I, C)), 'sWg': w(ks[9], (S, C, I)), 'sWu': w(ks[10], (S, C, I)), 'sWd': w(ks[11], (S, I, C))}
    _L0_ffn_in = _L0_ffn_setup()
    _L0_c = _w((lambda *s: np.random.randn(*s).astype(np.float32) * 0.05)(2, 256))
    _L0_wmod = _w((lambda *s: np.random.randn(*s).astype(np.float32) * 0.05)(256, 6 * 256) * 256 ** (-0.5))
    _d = {'L0_attn_x': _L0_attn_in['x'], 'L0_attn_W': _L0_attn_in['W'], 'L0_attn_b': _L0_attn_in['b'], 'L0_ffn_w_ln1': _L0_ffn_in['w_ln1'], 'L0_ffn_Wq': _L0_ffn_in['Wq'], 'L0_ffn_Wkva': _L0_ffn_in['Wkva'], 'L0_ffn_Wkvb': _L0_ffn_in['Wkvb'], 'L0_ffn_Wo': _L0_ffn_in['Wo'], 'L0_ffn_w_ln2': _L0_ffn_in['w_ln2'], 'L0_ffn_Wgate': _L0_ffn_in['Wgate'], 'L0_ffn_expert_bias': _L0_ffn_in['expert_bias'], 'L0_ffn_Wg': _L0_ffn_in['Wg'], 'L0_ffn_Wu': _L0_ffn_in['Wu'], 'L0_ffn_Wd': _L0_ffn_in['Wd'], 'L0_ffn_sWg': _L0_ffn_in['sWg'], 'L0_ffn_sWu': _L0_ffn_in['sWu'], 'L0_ffn_sWd': _L0_ffn_in['sWd'], 'L0_c': _L0_c, 'L0_wmod': _L0_wmod}
    _x0 = _d['L0_attn_x']
    _d['L0_attn_x'] = jax.random.normal(jax.random.fold_in(jax.random.key(seed), 1), (2, 2048, 256), dtype=_x0.dtype)
    del _x0
    return _d

def reference(L0_attn_x, L0_attn_W, L0_attn_b, L0_ffn_w_ln1, L0_ffn_Wq, L0_ffn_Wkva, L0_ffn_Wkvb, L0_ffn_Wo, L0_ffn_w_ln2, L0_ffn_Wgate, L0_ffn_expert_bias, L0_ffn_Wg, L0_ffn_Wu, L0_ffn_Wd, L0_ffn_sWg, L0_ffn_sWu, L0_ffn_sWd, L0_c, L0_wmod):

    def _L0_attn_ref(x, W, b):
        import jax, jax.numpy as jnp
        import numpy as np
        D_MODEL = 256
        N_HEADS = 16
        B, S, D = x.shape
        H = N_HEADS
        hd = D // H
        qkv = x @ W.T + b
        q, k, v = jnp.split(qkv, 3, axis=-1)
        split_heads = lambda t: t.reshape(B, S, H, hd).transpose(0, 2, 1, 3)
        q, k, v = map(split_heads, (q, k, v))
        scores = jnp.einsum('bhqd,bhkd->bhqk', q, k)
        causal = jnp.tril(jnp.ones((S, S), dtype=bool))
        scores = jnp.where(causal, scores, -jnp.inf)
        attn = jax.nn.softmax(scores, axis=-1)
        out = jnp.einsum('bhqk,bhkd->bhqd', attn, v)
        out = out.transpose(0, 2, 1, 3).reshape(B, S, D)
        return x + out

    def _L0_ffn_ref(x, w_ln1, Wq, Wkva, Wkvb, Wo, w_ln2, Wgate, expert_bias, Wg, Wu, Wd, sWg, sWu, sWd):
        import jax, jax.numpy as jnp
        import numpy as np
        B, T, C = (2, 512, 256)
        H, D = (16, 64)
        CR = 8
        R = C // CR
        ROPE = D // 2
        NOPE = D - ROPE
        E, K, I, S = (8, 2, 128, 1)
        THETA = 100000.0
        EPS = 1e-05

        def _rmsnorm(x, w):
            rms = jnp.sqrt(jnp.mean(x * x, axis=-1, keepdims=True) + EPS)
            return w * (x / rms)

        def _rope(xh):
            d = xh.shape[-1]
            t = jnp.arange(xh.shape[2], dtype=jnp.float32)
            freqs = 1.0 / THETA ** (jnp.arange(0, d, 2, dtype=jnp.float32) / d)
            ang = jnp.outer(t, freqs)
            cos, sin = (jnp.cos(ang), jnp.sin(ang))
            xr = xh.reshape(xh.shape[:-1] + (d // 2, 2))
            x0, x1 = (xr[..., 0], xr[..., 1])
            rot = jnp.stack([x0 * cos - x1 * sin, x0 * sin + x1 * cos], axis=-1)
            return rot.reshape(xh.shape)

        def _attention(x, Wq, Wkva, Wkvb, Wo):
            b, t, _ = x.shape
            q = (x @ Wq).reshape(b, t, H, D).transpose(0, 2, 1, 3)
            ckv = x @ Wkva
            kv_latent, k_rope = (ckv[:, :, :R], ckv[:, :, R:])
            kv = (kv_latent @ Wkvb).reshape(b, t, H, NOPE).transpose(0, 2, 1, 3)
            k_rope = jnp.broadcast_to(k_rope[:, None, :, :], (b, H, t, ROPE))
            q_nope, q_rope = (q[..., :NOPE], q[..., NOPE:])
            q = jnp.concatenate([q_nope, _rope(q_rope)], axis=-1)
            k = jnp.concatenate([kv, _rope(k_rope)], axis=-1)
            v = jnp.concatenate([kv, jnp.zeros_like(k_rope)], axis=-1)
            att = jnp.einsum('bhqd,bhkd->bhqk', q, k) / jnp.sqrt(jnp.float32(D))
            mask = jnp.tril(jnp.ones((t, t), dtype=bool))
            att = jnp.where(mask, att, jnp.float32(-jnp.inf))
            att = jax.nn.softmax(att, axis=-1)
            y = jnp.einsum('bhqk,bhkd->bhqd', att, v)
            y = y.transpose(0, 2, 1, 3).reshape(b, t, H * D)
            return y @ Wo

        def _experts(x_flat, Wg, Wu, Wd):
            g = jax.nn.silu(jnp.einsum('nc,eci->nei', x_flat, Wg))
            u = jnp.einsum('nc,eci->nei', x_flat, Wu)
            return jnp.einsum('nei,eic->nec', g * u, Wd)

        def _moe(x, Wgate, expert_bias, Wg, Wu, Wd, sWg, sWu, sWd):
            b, t, c = x.shape
            xf = x.reshape(-1, c)
            shared = jnp.mean(_experts(xf, sWg, sWu, sWd), axis=1)
            logits = xf @ Wgate + expert_bias
            probs = jax.nn.softmax(logits, axis=-1)
            topk_p, topk_i = jax.lax.top_k(probs, K)
            topk_p = topk_p / jnp.sum(topk_p, axis=-1, keepdims=True)
            comb = jnp.sum(jax.nn.one_hot(topk_i, E, dtype=xf.dtype) * topk_p[..., None], axis=1)
            routed = jnp.einsum('ne,nec->nc', comb, _experts(xf, Wg, Wu, Wd))
            return (shared + routed).reshape(b, t, c)
        x = x + _attention(_rmsnorm(x, w_ln1), Wq, Wkva, Wkvb, Wo)
        residual = x
        xn = _rmsnorm(x, w_ln2)
        x_out = _moe(xn, Wgate, expert_bias, Wg, Wu, Wd, sWg, sWu, sWd)
        return residual + x_out
    x = L0_attn_x
    mod = (_silu(L0_c) @ L0_wmod).reshape(L0_c.shape[0], 6, 1, -1)
    sa, ca, ga, sb, cb, gb = (mod[:, 0], mod[:, 1], mod[:, 2], mod[:, 3], mod[:, 4], mod[:, 5])
    ga = (2 * (ga >= 0) - 1) * jnp.maximum(jnp.abs(ga), 0.25)
    gb = (2 * (gb >= 0) - 1) * jnp.maximum(jnp.abs(gb), 0.25)
    h = _layernorm(x, axis=-1) * (1 + ca) + sa
    x = x + ga * _L0_attn_ref(h, L0_attn_W, L0_attn_b)
    h = _layernorm(x, axis=-1) * (1 + cb) + sb
    x = x + gb * _L0_ffn_ref(h, L0_ffn_w_ln1, L0_ffn_Wq, L0_ffn_Wkva, L0_ffn_Wkvb, L0_ffn_Wo, L0_ffn_w_ln2, L0_ffn_Wgate, L0_ffn_expert_bias, L0_ffn_Wg, L0_ffn_Wu, L0_ffn_Wd, L0_ffn_sWg, L0_ffn_sWu, L0_ffn_sWd)
    return x

_drawn_inputs = setup_inputs


def setup_inputs(seed=0):
    import zlib

    import numpy as np

    out = dict(_drawn_inputs(seed))
    spreads = {'L0_ffn_w_ln1': (1.0, 0.6), 'L0_ffn_w_ln2': (1.0, 0.6), 'L0_ffn_expert_bias': (0.0, 0.8)}
    factors = {'L0_attn_b': 5.309,
     'L0_ffn_Wq': 8.0,
     'L0_ffn_Wkva': 8.0,
     'L0_ffn_Wkvb': 8.0,
     'L0_ffn_Wo': 8.0,
     'L0_ffn_Wgate': 8.0,
     'L0_ffn_Wg': 8.0,
     'L0_ffn_Wu': 8.0,
     'L0_ffn_Wd': 8.0,
     'L0_ffn_sWg': 8.0,
     'L0_ffn_sWu': 8.0,
     'L0_ffn_sWd': 8.0}
    for name, (base, spread) in spreads.items():
        noise = np.random.default_rng([zlib.crc32(name.encode()), seed]).standard_normal(out[name].shape)
        drawn = base * np.exp(spread * noise) if base else spread * noise
        out[name] = jnp.asarray(drawn.astype(out[name].dtype))
    for name, factor in factors.items():
        out[name] = (out[name] * factor).astype(out[name].dtype)
    return out
```

```python
import numpy as np
import concourse.bass as bass
from concourse import mybir
from concourse.alu_op_type import AluOpType as ALU
from contextlib import ExitStack

FP32 = mybir.dt.float32
F32R = mybir.dt.float32r
BF16 = mybir.dt.bfloat16
ACT = mybir.ActivationFunctionType
AX = mybir.AxisListType

B, T, C = 2, 2048, 256
P = 128
KT = C // P
GT = 512
NTILE = GT // P
NGRP = T // GT
HEADS = 16
HG = 4
NG = B * HEADS // HG
HD1 = C // HEADS
HD2, ROPE, LAT = 64, 32, 32
E, I = 8, 128
EPS = 1e-5
NEG = -1e30


def rope_tables():
    freqs = (np.float32(1.0) / np.float32(100000.0) ** (np.arange(0, ROPE, 2, dtype=np.float32) / np.float32(ROPE))).astype(np.float32)
    ang = np.outer(freqs, np.arange(T, dtype=np.float32)).astype(np.float32)
    cos, sin = np.cos(ang).astype(np.float32), np.sin(ang).astype(np.float32)
    return np.concatenate([cos, cos]), np.concatenate([-sin, sin])



def modulation(nc, d, m):
    with ExitStack() as ctx:
        sb = lambda n, s, t=FP32: ctx.enter_context(nc.sbuf_tensor(n, s, t))
        sem = lambda n: nc.alloc_semaphore(n)
        cT, cE = sb("cT", [P, KT, B]), sb("cE", [P, KT, B])
        cB = sb("cB", [P, KT, B, P])
        wmod = sb("wmod", [P, KT, 6 * C])
        size, sign = sb("ga_size", [P, B, C]), sb("ga_sign", [P, B, C])
        ps = ctx.enter_context(nc.psum_tensor("ps_mod", [P, 6, 512], FP32))
        loaded, c_exp, c_ready, mod_psum, mod_read, chain = (
            sem(n) for n in ("mod_loaded", "mod_c_exp", "mod_c_ready", "mod_psum", "mod_read", "mod_chain"))
        block = ctx.enter_context(nc.Block())
        LOADS = 8

        @block.sync
        def _(sp):
            sp.dma_start(cT[:, :, :], d["cT"].rearrange("(k p) b -> p k b", p=P)).then_inc(loaded, 16)
            sp.dma_start(wmod[:, :, :], d["wmod"].rearrange("(k p) n -> p k n", p=P)).then_inc(loaded, 16)
            sp.dma_start(m.eye[:, :], d["eye"]).then_inc(loaded, 16)
            sp.dma_start(m.causal[:, :], d["causal"]).then_inc(loaded, 16)
            sp.dma_start(m.bqk[:, :], d["bqk"]).then_inc(loaded, 16)
            sp.dma_start(m.bv[:, :], d["bv"].rearrange("(a n) -> a n", a=1).broadcast_to([P, C])).then_inc(loaded, 16)
            sp.dma_start(m.wln[:, :, :], d["wln"]).then_inc(loaded, 16)
            sp.dma_start(m.ebias[:, :], d["ebias"].rearrange("(a n) -> a n", a=1).broadcast_to([P, E])).then_inc(loaded, 16)

        @block.scalar
        def _(act):
            act.wait_ge(loaded, 16 * LOADS)
            act.activation(cE[:, :, :], cT[:, :, :], ACT.Exp, scale=-1.0).then_inc(c_exp, 1)

        @block.tensor
        def _(pe):
            pe.wait_ge(c_ready, 1)
            for b in range(B):
                for n in range(3):
                    for k in range(KT):
                        mm = pe.matmul(ps[:, 3 * b + n, :], cB[:, k, b, :], wmod[:, k, 512 * n:512 * n + 512],
                                       start=(k == 0), stop=(k == KT - 1))
                    mm.then_inc(mod_psum, 1)

        @block.vector
        def _(dve):
            done = [0]

            def link(ins):
                done[0] += 1
                ins.then_inc(chain, 1)
                dve.wait_ge(chain, done[0])

            dve.wait_ge(c_exp, 1)
            dve.tensor_copy(m.eye16[:, :], m.eye[:, :])
            dve.tensor_copy(m.after16[:, :], m.causal[:, GT - P:GT])
            link(dve.tensor_scalar(cE[:, :, :], cE[:, :, :], 1.0, None, ALU.add))
            link(dve.reciprocal(cE[:, :, :], cE[:, :, :]))
            link(dve.tensor_tensor(cT[:, :, :], cT[:, :, :], cE[:, :, :], ALU.mult))
            dve.tensor_copy(cB[:, :, :, :], cT[:, :, :].unsqueeze(3).broadcast_to([P, KT, B, P])).then_inc(c_ready, 1)
            for b in range(B):
                for n in range(3):
                    dve.wait_ge(mod_psum, 3 * b + n + 1)
                    dve.tensor_copy(m.mod[:, b, 2 * n:2 * n + 2, :],
                                    ps[:, 3 * b + n, :].rearrange("p (a c) -> p a c", a=2)).then_inc(mod_read, 1)
            dve.wait_ge(mod_read, 6)
            for v in (1, 4):
                link(dve.tensor_scalar(m.mod[:, :, v, :], m.mod[:, :, v, :], 1.0, None, ALU.add))
            for v in (2, 5):
                link(dve.tensor_scalar(sign[:, :, :], m.mod[:, :, v, :], 0.0, 2.0, ALU.is_ge, ALU.mult))
                link(dve.tensor_scalar(size[:, :, :], m.mod[:, :, v, :], -1.0, None, ALU.mult))
                link(dve.tensor_tensor(size[:, :, :], size[:, :, :], m.mod[:, :, v, :], ALU.max))
                link(dve.tensor_scalar(size[:, :, :], size[:, :, :], 0.25, None, ALU.max))
                link(dve.scalar_tensor_tensor(out=m.mod[:, :, v, :], in0=sign[:, :, :], scalar=-1.0, in1=size[:, :, :],
                                              op0=ALU.add, op1=ALU.mult))


def product3(pe, out, hi, lo, x_hi, x_lo, first, last, **kw):
    pe.matmul(out, lo, x_hi, start=first, stop=False, **kw)
    pe.matmul(out, hi, x_lo, start=False, stop=False, **kw)
    return pe.matmul(out, hi, x_hi, start=False, stop=last, **kw)


def split_weights(nc, name, jobs):
    with ExitStack() as ctx:
        sem = lambda n: nc.alloc_semaphore(name + n)
        loaded = [sem(f"_loaded{n}") for n in range(len(jobs))]
        high = sem("_high")
        block = ctx.enter_context(nc.Block())

        @block.sync
        def _(sp):
            for n, (loads, stage, hi, lo) in enumerate(jobs):
                for src, place in loads:
                    sp.dma_start(place, src).then_inc(loaded[n], 16)

        @block.scalar
        def _(act):
            for n, (loads, stage, hi, lo) in enumerate(jobs):
                act.wait_ge(loaded[n], 16 * len(loads))
                act.activation(hi, stage, ACT.Copy).then_inc(high, 1)

        @block.vector
        def _(dve):
            for n, (loads, stage, hi, lo) in enumerate(jobs):
                dve.wait_ge(high, n + 1)
                dve.tensor_tensor(lo, stage, hi, ALU.subtract)


def project1(nc, d, m):
    with ExitStack() as ctx:
        sb = lambda n, s, t=FP32: ctx.enter_context(nc.sbuf_tensor("p1_" + n, s, t))
        sem = lambda n: nc.alloc_semaphore("p1_" + n)
        sems = lambda n: [sem(f"{n}{b}") for b in range(2)]
        w_st = sb("w_st", [P, KT, 3 * C])
        w_hi, w_lo = sb("w_hi", [P, KT, 3 * C], F32R), sb("w_lo", [P, KT, 3 * C], F32R)
        split_weights(nc, "p1_w", [([(d["wT"].rearrange("(k p) n -> p k n", p=P), w_st[:, :, :])], w_st[:, :, :], w_hi[:, :, :], w_lo[:, :, :])])
        x = sb("x", [P, B, NTILE, C])
        h = sb("h", [P, B, NTILE, C])
        u = sb("u", [P, B, NTILE, C])
        stats, mv = sb("stats", [P, B, NTILE, 6]), sb("mv", [P, B, NTILE, 2])
        sd, rstd = sb("sd", [P, B, NTILE]), sb("rstd", [P, B, NTILE])
        hT_hi, hT_lo = sb("hT_hi", [P, B, KT, GT], F32R), sb("hT_lo", [P, B, KT, GT], F32R)
        qk_hi, qk_lo = sb("qk_hi", [P, 2, GT], F32R), sb("qk_lo", [P, 2, GT], F32R)
        pT = ctx.enter_context(nc.psum_tensor("p1_pT", [P, KT, GT], FP32))
        pQK = ctx.enter_context(nc.psum_tensor("p1_pQK", [P, 2, GT], FP32))
        pV = ctx.enter_context(nc.psum_tensor("p1_pV", [P, 2, 2, C], FP32))
        x_loaded, var_ready, sd_ready, h_ready, u_ready, u_stored = (
            sems(n) for n in ("x_loaded", "var_ready", "sd_ready", "h_ready", "u_ready", "u_stored"))
        hT_used = sems("hT_used")
        t_psum, hi_ready, lo_ready = sem("t_psum"), sem("hi_ready"), sem("lo_ready")
        qk_psum, qk_hi_ready, qk_lo_ready, qk_stored = (sems(n) for n in ("qk_psum", "qk_hi_ready", "qk_lo_ready", "qk_stored"))
        v_psum, v_read = sems("v_psum"), sems("v_read")
        stats_ready, norm_ready, ga_h, passed = sem("stats_ready"), sem("norm_ready"), sem("ga_h"), sem("passed")
        block = ctx.enter_context(nc.Block())
        x_v = d["x"].rearrange("b (i t p) c -> b i p t c", t=NTILE, p=P)
        u_v = d["u1"].rearrange("b (i t p) c -> b i p t c", t=NTILE, p=P)
        use = lambda i, b, n: 4 * i + 2 * b + n // 2

        @block.sync
        def _(sp):
            with sp.Fori(0, NGRP) as i:
                for b in range(B):
                    sp.wait_ge(u_ready[b], i)
                    sp.dma_start(x[:, b], x_v[b, bass.ds(i, 1)].rearrange("a p t c -> (a p) t c")).then_inc(x_loaded[b], 16)
                for b in range(B):
                    for n in range(4):
                        r = n % 2
                        sp.wait_ge(qk_lo_ready[r], use(i, b, n) + 1)
                        row = b * C + P * r
                        for s, half in enumerate((qk_hi, qk_lo)):
                            sp.dma_start(d["qk1"][n // 2, s, row:row + P, bass.ds(i * GT, GT)],
                                         half[:, r, :].bitcast(FP32)).then_inc(qk_stored[r], 16)
                    sp.wait_ge(u_ready[b], i + 1)
                    sp.dma_start(u_v[b, bass.ds(i, 1)].rearrange("a p t c -> (a p) t c"), u[:, b]).then_inc(u_stored[b], 16)
            for b in range(B):
                sp.wait_ge(u_stored[b], 16 * NGRP)
                sp.wait_ge(qk_stored[b], 16 * 2 * 4 * NGRP)

        @block.gpsimd
        def _(pool):
            with pool.Fori(0, NGRP) as i:
                for b in range(B):
                    ga = m.mod[:, b, 2, :].unsqueeze(1).broadcast_to([P, NTILE, C])
                    pool.wait_ge(h_ready[b], i + 1)
                    pool.wait_ge(u_stored[b], 16 * i)
                    pool.tensor_tensor(u[:, b], h[:, b], ga, ALU.mult).then_inc(ga_h, 1)
                    pool.wait_ge(ga_h, 2 * i + b + 1)
                    pool.tensor_tensor(u[:, b], u[:, b], x[:, b], ALU.add).then_inc(u_ready[b], 1)

        @block.scalar
        def _(act):
            with act.Fori(0, NGRP) as i:
                for b in range(B):
                    act.wait_ge(var_ready[b], i + 1)
                    act.activation(sd[:, b], mv[:, b, :, 1], ACT.Sqrt).then_inc(sd_ready[b], 1)
                for b in range(B):
                    act.wait_ge(hT_used[b], i)
                    for k in range(KT):
                        act.wait_ge(t_psum, 4 * i + 2 * b + k + 1)
                        act.activation(hT_hi[:, b, k, :], pT[:, k, :], ACT.Copy).then_inc(hi_ready, 1)
                    for n in range(4):
                        r = n % 2
                        act.wait_ge(qk_psum[r], use(i, b, n) + 1)
                        act.wait_ge(qk_stored[r], 32 * use(i, b, n))
                        act.activation(qk_hi[:, r, :], pQK[:, r, :], ACT.Identity, bias=m.bqk[:, n:n + 1]).then_inc(qk_hi_ready[r], 1)

        @block.vector
        def _(dve):
            with dve.Fori(0, NGRP) as i:
                for b in range(B):
                    dve.wait_ge(x_loaded[b], 16 * (i + 1))
                    for t in range(NTILE):
                        last = dve.bn_stats(stats[:, b, t, :], x[:, b, t, :])
                    last.then_inc(stats_ready, 1)
                    dve.wait_ge(stats_ready, 6 * i + 3 * b + 1)
                    dve.sem_inc(passed, 1)
                    for t in range(NTILE):
                        last = dve.bn_aggr(mv[:, b, t, :], stats[:, b, t, :])
                    last.then_inc(stats_ready, 1)
                    dve.wait_ge(stats_ready, 6 * i + 3 * b + 2)
                    dve.tensor_scalar(mv[:, b, :, 1], mv[:, b, :, 1], EPS, None, ALU.add).then_inc(var_ready[b], 1)
                    dve.wait_ge(sd_ready[b], i + 1)
                    dve.reciprocal(rstd[:, b], sd[:, b]).then_inc(stats_ready, 1)
                    dve.wait_ge(stats_ready, 6 * i + 3 * b + 3)
                    dve.wait_ge(u_ready[b], i)
                    for t in range(NTILE):
                        last = dve.tensor_scalar(h[:, b, t, :], x[:, b, t, :], mv[:, b, t, 0:1], rstd[:, b, t:t + 1],
                                                 ALU.subtract, ALU.mult)
                    last.then_inc(norm_ready, 1)
                    dve.wait_ge(norm_ready, 4 * i + 2 * b + 1)
                    dve.tensor_tensor(h[:, b], h[:, b], m.mod[:, b, 1, :].unsqueeze(1).broadcast_to([P, NTILE, C]),
                                      ALU.mult).then_inc(norm_ready, 1)
                    dve.wait_ge(norm_ready, 4 * i + 2 * b + 2)
                    dve.tensor_tensor(h[:, b], h[:, b], m.mod[:, b, 0, :].unsqueeze(1).broadcast_to([P, NTILE, C]),
                                      ALU.add).then_inc(h_ready[b], 1)
                for b in range(B):
                    for k in range(KT):
                        dve.wait_ge(hi_ready, 4 * i + 2 * b + k + 1)
                        dve.tensor_tensor(hT_lo[:, b, k, :], pT[:, k, :], hT_hi[:, b, k, :], ALU.subtract).then_inc(lo_ready, 1)
                    for n in range(4):
                        r = n % 2
                        dve.wait_ge(qk_hi_ready[r], use(i, b, n) + 1)
                        dve.scalar_tensor_tensor(out=qk_lo[:, r, :], in0=pQK[:, r, :], scalar=m.bqk[:, n:n + 1],
                                                 in1=qk_hi[:, r, :], op0=ALU.add, op1=ALU.subtract).then_inc(qk_lo_ready[r], 1)
                    for half in range(2):
                        dve.wait_ge(v_psum[half], 2 * i + b + 1)
                        dst = m.v1[:, 4 * b:4 * b + 4, bass.ds(i * NTILE + 2 * half, 2), :].rearrange("p g t f -> p t g f")
                        dve.tensor_tensor(dst, pV[:, half].rearrange("p t (g f) -> p t g f", g=4),
                                          m.bv[:, :].rearrange("p (g f) -> p g f", g=4).unsqueeze(1).broadcast_to([P, 2, 4, C // 4]),
                                          ALU.add).then_inc(v_read[half], 1)

        @block.tensor
        def _(pe):
            with pe.Fori(0, NGRP) as i:
                for b in range(B):
                    pe.wait_ge(h_ready[b], i + 1)
                    pe.wait_ge(lo_ready, 4 * i + 2 * b)
                    for k in range(KT):
                        for t in range(NTILE):
                            mm = pe.transpose(pT[:, k, P * t:P * t + P], h[:, b, t, P * k:P * k + P], m.eye[:, :])
                        mm.then_inc(t_psum, 1)
                    pe.wait_ge(lo_ready, 4 * i + 2 * b + 2)
                    for n in range(4):
                        r = n % 2
                        pe.wait_ge(qk_lo_ready[r], use(i, b, n))
                        for k in range(KT):
                            mm = product3(pe, pQK[:, r, :], w_hi[:, k, P * n:P * n + P], w_lo[:, k, P * n:P * n + P],
                                          hT_hi[:, b, k, :], hT_lo[:, b, k, :], k == 0, k == KT - 1)
                        mm.then_inc(qk_psum[r], 1)
                    for half in range(2):
                        pe.wait_ge(v_read[half], 2 * i + b)
                        for t in range(2):
                            at = P * (2 * half + t)
                            for k in range(KT):
                                mm = product3(pe, pV[:, half, t, :], hT_hi[:, b, k, at:at + P], hT_lo[:, b, k, at:at + P],
                                              w_hi[:, k, 2 * C:3 * C], w_lo[:, k, 2 * C:3 * C], k == 0, k == KT - 1)
                        mm.then_inc(v_psum[half], 1)
                    pe.wait_ge(v_psum[1], 2 * i + b + 1)
                    pe.sem_inc(hT_used[b], 1)


def attention(nc, d, m, second):
    with ExitStack() as ctx:
        name = "a2_" if second else "a1_"
        sb = lambda n, s, t=FP32: ctx.enter_context(nc.sbuf_tensor(name + n, s, t))
        sem = lambda n: nc.alloc_semaphore(name + n)
        KH = 1 if second else HG
        SCALE = HD2 ** -0.5 if second else 1.0
        NS, NR = 3, 3 if second else 4
        STACKS = 2 if second else 1
        q = [sb(f"q{n}", [P, NGRP, HG, GT], F32R) for n in range(STACKS)]
        kmax = sb("kmax", [P, KH, T], F32R)
        kmax_first = sb("kmax_first", [P, KH, GT], F32R)
        key = [sb(f"key{n}", [P, KH, T], F32R) for n in range(STACKS)]
        MAX_ROWS = P if second else 96
        rows_exp = [P] * (STACKS - 1) + [98]
        prob = sb("prob", [P, 4, HG, GT])
        val = sb("val", [P, T // P, KH, 32])
        rowmax = sb("rowmax", [P, 2, HG, NTILE, NGRP])
        fullmax = sb("fullmax", [P, HG * NTILE])
        neg_hi, neg_lo = sb("neg_hi", [HG * NTILE, P], F32R), sb("neg_lo", [HG * NTILE, P], F32R)
        pR = ctx.enter_context(nc.psum_tensor(name + "pR", [P, NR, GT], FP32))
        pS = ctx.enter_context(nc.psum_tensor(name + "pS", [P, NS, GT], FP32))
        pO = ctx.enter_context(nc.psum_tensor(name + "pO", [P, GT], FP32))
        if second:
            ones = sb("ones", [P, 32])
            out, recip = sb("out", [P, 2, GT]), sb("recip", [P, GT])
            zsum = sb("zsum", [P, HG, GT])
            pZ = ctx.enter_context(nc.psum_tensor(name + "pZ", [P, GT], FP32))
        else:
            out, recip = sb("out", [P, 2, NTILE, HG, HD1]), sb("recip", [P, NTILE, HG])
        oT = sb("oT", [P, GT])

        filled = sem("filled")
        dve_passed, sp_passed = sem("dve_passed"), sem("sp_passed")
        q_loaded, kmax_loaded, key_loaded = ([sem(f"{n}{c}") for c in range(NGRP)] for n in ("q_loaded", "kmax_loaded", "key_loaded"))
        first_loaded = [sem("first_loaded")]
        val_ready = sem("val_ready")
        r_psum, r_read = sem("r_psum"), sem("r_read")
        fullmax_ready, neg_hi_ready, neg_ready, neg_stored = sem("fullmax_ready"), sem("neg_hi_ready"), sem("neg_ready"), sem("neg_stored")
        s_psum, exp_ready, pv_done = sem("s_psum"), sem("exp_ready"), sem("pv_done")
        z_added, z_psum, z_copy = sem("z_added"), sem("z_psum"), sem("z_copy")
        o_copied, recip_ready, out_ready = sem("o_copied"), sem("recip_ready"), sem("out_ready")
        out_stored = [sem(f"out_stored{c}") for c in range(2)]
        block = ctx.enter_context(nc.Block())

        s_bank = lambda c, kt, h: (HG * (upto(c) + kt) + h) % NS

        def bank_before(c, kt, h):
            at = HG * (upto(c) + kt) + h
            return at - NS if at >= NS else max(n for n in range(HG * STEPS) if n % NS == at % NS) - HG * STEPS

        upto = lambda c: 2 * c * (c + 1)
        STEPS = upto(NGRP)
        FILLS = 4 if second else 7
        QL = 16 * (6 if second else 4)
        KL = 16 * (3 if second else 4)
        KML = 16 * (2 if second else 4)
        EXP_CREDIT, PV_CREDIT, R_CREDIT = HG, 4, NR
        by_pool = lambda c, kt: c == 0 or kt % 4 != 3
        pool_adds = [by_pool(c, kt) for c in range(NGRP) for kt in range(4 * c + 4)]
        ADDS = sum(pool_adds)

        def adds_before(at):
            return sum(pool_adds[:at]) if at >= 0 else -sum(pool_adds[at:])

        score_step = lambda g, c, kt: STEPS * g + upto(c) + kt
        first_query = lambda c, kt: max(0, P * (kt - 4 * c))

        def rows(c, tiles=range(NTILE)):
            return [("R", c, h, t, kc) for t in tiles for h in range(HG) for kc in range(c + 1)]

        def chain_up(*parts):
            side, late = [], []
            for part in parts:
                side += part[:3] + late + part[3:]
                c, h, t, kc = part[-1][1:]
                late = []
                if t == NTILE - 1:
                    side.append(("F", c))
                    late = [("M", c)]
            return side + late

        def order(side_a, side_b, scores):
            result = []
            for mine, side in (((0, 1, 2), side_a), ((3,), side_b)):
                main = []
                for c in mine if scores else ():
                    for kt in range(4 * c + 4):
                        main += [[("S", c, kt, h)] for h in range(HG)]
                        if c or kt:
                            before = (c, kt - 1) if kt else (c - 1, 4 * c - 1)
                            if before[0] in mine:
                                main[-1].append(("V", *before))
                                if kt == 0:
                                    main[-1].append(("E", c - 1))
                        if c - 1 in mine and second and kt == 1:
                            main[-1].append(("Z", c - 1))
                        if c - 1 in mine and second and kt == 2:
                            for n in range(NTILE):
                                main[n - HG].append(("N", c - 1, n))
                        if c - 1 in mine and kt == 2 and not second:
                            main[-1].append(("O", c - 1))
                weights = [GT - first_query(*x[0][1:3]) for x in main]
                if scores:
                    main.append([("V", mine[-1], 4 * mine[-1] + 3), ("E", mine[-1])])
                spread = max(0, len(side) - 4)
                sent = 0
                for n, items in enumerate(main):
                    result += items
                    goal = spread * sum(weights[:n + 1]) // sum(weights)
                    result += side[sent:goal]
                    sent = max(sent, goal)
                result += side[sent:]
                if scores:
                    result += [("Z", mine[-1])] + [("N", mine[-1], n) for n in range(NTILE)] if second else [("O", mine[-1])]
            return result

        first = order(chain_up(rows(0), rows(1), rows(2, (0, 1, 2))), [], False)
        side_a, side_b = chain_up(rows(2, (3,)), rows(3), rows(0), rows(1, (0, 1))), chain_up(rows(1, (2, 3)), rows(2, (0, 1, 2)))
        body, final = order(side_a, side_b, True), order(chain_up(rows(2, (3,)), rows(3)), [], True)
        bank_uses = lambda items: sum(x[0] in "RMOK" for x in items)
        body = [("K",)] * (-bank_uses(body) % NR) + body
        R_FIRST, R_BODY = bank_uses(first), bank_uses(body)

        def run(eng, work):
            work(first, -1, 0)
            with eng.Fori(0, NG - 1) as g:
                work(body, g, R_FIRST + g * R_BODY)
            work(final, NG - 1, R_FIRST + (NG - 1) * R_BODY)

        r_start = [0, R_FIRST % NR, (R_FIRST + (NG - 1) * R_BODY) % NR]

        def max_count(items, g, c):
            return c if items is first else 4 * g + (c if c >= 2 else 4 + c)

        @block.sync
        def _(sp):
            def load_q(c, g):
                cols = slice(c * GT, (c + 1) * GT)
                if second:
                    for s in range(2):
                        for k in range(2):
                            v = d["q2"][bass.ds(g, 1), s, k, :, cols].rearrange("a (h r) t -> r (a h) t", h=HG)
                            at = 64 * s + 32 * k
                            sp.dma_start(q[0][at:at + 32, c].bitcast(FP32), v).then_inc(q_loaded[c], 16)
                            if s == 0:
                                sp.dma_start(q[1][at:at + 32, c].bitcast(FP32), v).then_inc(q_loaded[c], 16)
                else:
                    for n, s in enumerate((0, 0, 1, 1)):
                        v = d["qk1"][0, s, bass.ds(64 * g, 64), cols].rearrange("(h f) t -> f h t", h=HG)
                        sp.dma_start(q[0][16 * n:16 * n + 16, c].bitcast(FP32), v).then_inc(q_loaded[c], 16)

            def load_kmax(c, g, tile=kmax, signal=kmax_loaded):
                cols = slice(c * GT, (c + 1) * GT)
                if second:
                    sp.sem_inc(sp_passed, 1)
                    for n in range(2):
                        v = d["k2"][bass.ds(g // 4, 1), 0, :, cols].rearrange("a f t -> (a f) t")
                        sp.dma_start(tile[64 * n:64 * n + 64, 0, cols].bitcast(FP32), v).then_inc(signal[c], 16)
                else:
                    for n, s in enumerate((0, 1, 0, 1)):
                        v = d["qk1"][1, s, bass.ds(64 * g, 64), cols].rearrange("(h f) t -> f h t", h=HG)
                        sp.dma_start(tile[16 * n:16 * n + 16, :, cols].bitcast(FP32), v).then_inc(signal[c], 16)

            def load_k(c, g):
                cols = slice(c * GT, (c + 1) * GT)
                if second:
                    sp.sem_inc(sp_passed, 1)
                    for n, at, s in ((0, 0, 0), (0, 64, 0), (1, 0, 1)):
                        v = d["k2"][bass.ds(g // 4, 1), s, :, cols].rearrange("a f t -> (a f) t")
                        sp.dma_start(key[n][at:at + 64, 0, cols].bitcast(FP32), v).then_inc(key_loaded[c], 16)
                else:
                    for n, s in enumerate((0, 1, 0, 1)):
                        v = d["qk1"][1, s, bass.ds(64 * g, 64), cols].rearrange("(h f) t -> f h t", h=HG)
                        sp.dma_start(key[0][16 * n:16 * n + 16, :, cols].bitcast(FP32), v).then_inc(key_loaded[c], 16)

            def store_max(c, count):
                sp.wait_ge(neg_ready, count + 1)
                for row, half in ((96, neg_hi), (97, neg_lo)):
                    sp.dma_start(q[-1][row:row + 1, c].bitcast(FP32), half[:, :].bitcast(FP32)).then_inc(neg_stored, 16)

            def store_out(c, g):
                sp.wait_ge(out_ready, 4 * g + c + 1)
                if second:
                    dst = d["o2"][bass.ds(g, 1), :, c * GT:(c + 1) * GT].rearrange("a p t -> (a p) t")
                    sp.dma_start(dst, out[:, c % 2, :]).then_inc(out_stored[c % 2], 16)
                else:
                    dst = d["o1"][bass.ds(g, 1), c * GT:(c + 1) * GT].rearrange("a (t p) f -> p (a t) f", p=P)
                    sp.dma_start(dst, out[:, c % 2].rearrange("p t h f -> p t (h f)")).then_inc(out_stored[c % 2], 16)

            sp.wait_ge(filled, FILLS)
            load_kmax(0, 0, kmax_first, first_loaded)
            for c in range(3):
                load_q(c, 0)
                load_kmax(c, 0)
            load_kmax(3, 0)
            for c in range(NGRP):
                load_k(c, 0)
            for c in range(2):
                store_max(c, c)
            with sp.Fori(0, NG - 1) as g:
                sp.wait_ge(s_psum, HG * STEPS * g)
                load_q(3, g)
                store_max(2, 4 * g + 2)
                sp.wait_ge(s_psum, HG * (STEPS * g + upto(1)))
                load_q(0, g + 1)
                load_kmax(0, g + 1, kmax_first, first_loaded)
                store_out(0, g)
                sp.wait_ge(s_psum, HG * (STEPS * g + upto(2)))
                load_q(1, g + 1)
                store_out(1, g)
                store_max(3, 4 * g + 3)
                for c in range(NGRP):
                    load_kmax(c, g + 1)
                sp.wait_ge(s_psum, HG * (STEPS * g + upto(3)))
                load_q(2, g + 1)
                store_out(2, g)
                store_max(0, 4 * g + 4)
                for c in range(3):
                    sp.wait_ge(s_psum, HG * (STEPS * g + upto(3) + 4 * c + 4))
                    load_k(c, g + 1)
                    if c == 0:
                        store_max(1, 4 * g + 5)
                sp.wait_ge(s_psum, HG * STEPS * (g + 1))
                load_k(3, g + 1)
                store_out(3, g)
            g = NG - 1
            sp.wait_ge(s_psum, HG * STEPS * g)
            load_q(3, g)
            store_max(2, 4 * g + 2)
            store_out(0, g)
            store_out(1, g)
            store_max(3, 4 * g + 3)
            store_out(2, g)
            store_out(3, g)
            for r in range(2):
                sp.wait_ge(out_stored[r], 16 * 2 * NG)

        @block.gpsimd
        def _(pool):
            fills = [(t[64:P].bitcast(FP32), 0.0) for t in ((q[1], key[1]) if second else (q[0], kmax, kmax_first, key[0]))]
            fills += [(ones[:, :], 1.0)] if second else [(val[:, :, :, 16:32], 0.0), (val[:, :, :, 16:17], 1.0)]
            fills += [(key[-1][96:98].bitcast(FP32), 1.0)]
            for n, (place, value) in enumerate(fills):
                if n:
                    pool.wait_ge(filled, n)
                pool.memset(place, value).then_inc(filled, 1)
            pool.wait_ge(filled, FILLS)

            def values(c, g):
                if second:
                    src = m.lat[:, bass.ds((g // 4) * (T // P) + 4 * c, 4), :]
                    pool.tensor_copy(val[:, 4 * c:4 * c + 4, 0, :], src).then_inc(val_ready, 1)
                else:
                    src = m.v1[:, bass.ds(g, 1), 4 * c:4 * c + 4, :].rearrange("p a t (h f) -> p (a t) h f", h=HG)
                    pool.tensor_copy(val[:, 4 * c:4 * c + 4, :, 0:16], src).then_inc(val_ready, 1)

            if second:
                pool.sem_inc(z_added, EXP_CREDIT)

            def work(items, g, r):
                for item in items:
                    if item[0] == "V" and second and by_pool(*item[1:]):
                        _, c, kt = item
                        n = score_step(g, c, kt)
                        at = first_query(c, kt)
                        pool.wait_ge(exp_ready, EXP_CREDIT + HG * n + HG)
                        before = EXP_CREDIT + ADDS * g + adds_before(upto(c) + kt)
                        if kt == 0:
                            pool.wait_ge(z_psum, 4 * g + c)
                            pool.sem_inc(z_copy, 1)
                            pool.tensor_copy(zsum[:, :, :], prob[:, 0, :, :]).then_inc(z_added, 1)
                        else:
                            pool.wait_ge(z_added, before)
                            pool.tensor_tensor(zsum[:, :, at:GT], zsum[:, :, at:GT], prob[:, kt % 4, :, at:GT], ALU.add).then_inc(z_added, 1)
                    if item[0] == "V" and item[1] == 3 and item[2] % 4 == 3 and items is body:
                        pool.wait_ge(pv_done, PV_CREDIT + score_step(g, 3, item[2]) + 1)
                        values(item[2] // 4, g + 1)

            for c in range(NGRP):
                values(c, 0)
            run(pool, work)

        @block.scalar
        def _(act):
            act.sem_inc(exp_ready, EXP_CREDIT)

            def work(items, g, r):
                for item in items:
                    if item[0] == "S":
                        _, c, kt, h = item
                        n = score_step(g, c, kt)
                        at = first_query(c, kt)
                        if h == 0:
                            act.wait_ge(pv_done, n + 1)
                            if second:
                                act.wait_ge(z_added, EXP_CREDIT + ADDS * g + adds_before(upto(c) + kt - 3))
                        act.wait_ge(s_psum, HG * n + h + 1)
                        act.activation(prob[:, kt % 4, h, at:GT], pS[:, s_bank(c, kt, h), at:GT], ACT.Exp, scale=SCALE).then_inc(exp_ready, 1)
                    if item[0] == "E":
                        c = item[1]
                        act.wait_ge(pv_done, PV_CREDIT + score_step(g, c, 4 * c + 4))
                        act.wait_ge(out_ready, 4 * g + c)
                        act.activation(oT[:, :], pO[:, :], ACT.Copy).then_inc(o_copied, 1)
            run(act, work)

        @block.vector
        def _(dve):
            dve.sem_inc(r_read, R_CREDIT)

            def work(items, g, r0):
                bank0 = r_start[0 if items is first else 1 if items is body else 2]
                used = 0
                for item in items:
                    r, bank = r0 + used, (bank0 + used) % NR
                    if item[0] == "R":
                        _, c, h, t, kc = item
                        used += 1
                        dve.wait_ge(r_psum, r + 1)
                        if kc < c:
                            dve.tensor_reduce(rowmax[:, c % 2, h, t, kc:kc + 1], pR[:, bank, :], axis=AX.X, op=ALU.max).then_inc(r_read, 1)
                        else:
                            n = P * (t + 1)
                            dve.sem_inc(dve_passed, 1)
                            dve.tensor_tensor_reduce(out=pR[:, bank, 0:n], in0=pR[:, bank, 0:n], in1=m.causal[:, GT - n:GT],
                                                     scale=1.0, scalar=-3e38, op0=ALU.add, op1=ALU.max,
                                                     accum_out=rowmax[:, c % 2, h, t, kc:kc + 1]).then_inc(r_read, 1)
                    if item[0] == "K":
                        used += 1
                        dve.wait_ge(r_read, R_CREDIT + r)
                        dve.sem_inc(r_read, 1)
                    if item[0] == "F":
                        c = item[1]
                        dve.wait_ge(r_read, R_CREDIT + r)
                        dve.tensor_reduce(fullmax[:, :], rowmax[:, c % 2, :, :, 0:c + 1].rearrange("p h t k -> p (h t) k"),
                                          axis=AX.X, op=ALU.max).then_inc(fullmax_ready, 1)
                    if item[0] == "M":
                        used += 1
                        count = max_count(items, g, item[1])
                        dve.wait_ge(r_psum, r + 1)
                        dve.wait_ge(neg_stored, 32 * count)
                        dve.tensor_scalar(neg_hi[:, :], pR[0:HG * NTILE, bank, 0:P], -1.0, None, ALU.mult).then_inc(neg_hi_ready, 1)
                        dve.wait_ge(neg_hi_ready, count + 1)
                        dve.scalar_tensor_tensor(out=neg_lo[:, :], in0=pR[0:HG * NTILE, bank, 0:P], scalar=-1.0, in1=neg_hi[:, :],
                                                 op0=ALU.mult, op1=ALU.subtract).then_inc(neg_ready, 1)
                        dve.wait_ge(neg_ready, count + 1)
                        dve.sem_inc(r_read, 1)
                    if item[0] == "O":
                        c = item[1]
                        used += 1
                        n = 4 * g + c
                        dve.wait_ge(r_psum, r + 1)
                        o = pR[:, bank, :].rearrange("p (t h f) -> p t h f", t=NTILE, h=HG)
                        dve.reciprocal(recip[:, :, :], o[:, :, :, HD1]).then_inc(recip_ready, 1)
                        dve.wait_ge(recip_ready, n + 1)
                        dve.wait_ge(out_stored[c % 2], 16 * (2 * g + c // 2))
                        dve.tensor_tensor(out[:, c % 2], o[:, :, :, 0:HD1],
                                          recip[:, :, :].unsqueeze(3).broadcast_to([P, NTILE, HG, HD1]), ALU.mult).then_inc(out_ready, 1)
                        dve.wait_ge(out_ready, n + 1)
                        dve.sem_inc(r_read, 1)
                    if item[0] == "N":
                        _, c, n = item
                        piece = slice(P * n, P * n + P)
                        if n == 0:
                            dve.wait_ge(z_psum, 4 * g + c + 1)
                            dve.wait_ge(o_copied, 4 * g + c + 1)
                            dve.wait_ge(out_stored[c % 2], 16 * (2 * g + c // 2))
                        dve.reciprocal(recip[:, piece], pZ[:, piece]).then_inc(recip_ready, 1)
                        dve.wait_ge(recip_ready, 4 * (4 * g + c) + n + 1)
                        ins = dve.tensor_tensor(out[:, c % 2, piece], oT[:, piece], recip[:, piece], ALU.mult)
                        if n == NTILE - 1:
                            ins.then_inc(out_ready, 1)
            run(dve, work)

        @block.tensor
        def _(pe):
            pe.sem_inc(pv_done, PV_CREDIT)
            pe.wait_ge(filled, FILLS)

            def work(items, g, r0):
                bank0 = r_start[0 if items is first else 1 if items is body else 2]
                used = 0
                for item in items:
                    r, bank = r0 + used, (bank0 + used) % NR
                    if item[0] == "R":
                        _, c, h, t, kc = item
                        used += 1
                        step = g if c == 3 else g + 1
                        if h == 0 and t == 0:
                            if kc == 0:
                                pe.wait_ge(q_loaded[c], QL * (step + 1))
                            pe.wait_ge((kmax_loaded if c else first_loaded)[kc], KML * (step + 1))
                        pe.wait_ge(r_read, r + 1)
                        n = GT if kc < c else P * (t + 1)
                        pe.matmul(pR[:, bank, 0:n], q[0][0:MAX_ROWS, c, h, P * t:P * t + P],
                                  (kmax if c else kmax_first)[0:MAX_ROWS, h % KH, GT * kc:GT * kc + n], start=True, stop=True).then_inc(r_psum, 1)
                    if item[0] == "M":
                        used += 1
                        pe.wait_ge(r_read, r + 1)
                        pe.wait_ge(fullmax_ready, max_count(items, g, item[1]) + 1)
                        pe.transpose(pR[0:HG * NTILE, bank, 0:P], fullmax[:, :], m.eye[:, :]).then_inc(r_psum, 1)
                    if item[0] == "S":
                        _, c, kt, h = item
                        n = score_step(g, c, kt)
                        at = first_query(c, kt)
                        if kt == 0 and h == 0:
                            pe.wait_ge(neg_stored, 32 * (4 * g + 4 if c == 3 else 4 * g + c + 1))
                            pe.wait_ge(q_loaded[c], QL * (g + 1))
                        if kt >= 4 * c and kt % 4 == 0 and h == 0:
                            pe.wait_ge(key_loaded[kt // 4], KL * (g + 1))
                        diagonal = kt >= 4 * c
                        pe.wait_ge(exp_ready, EXP_CREDIT + HG * STEPS * g + bank_before(c, kt, h) + 1)
                        bank_s = s_bank(c, kt, h)
                        for s in range(STACKS):
                            mm = pe.matmul(pS[:, bank_s, at:GT], key[s][0:rows_exp[s], h % KH, P * kt:P * kt + P],
                                           q[s][0:rows_exp[s], c, h, at:GT], start=(s == 0), stop=(s == STACKS - 1 and not diagonal))
                        if diagonal:
                            mm = pe.matmul(pS[:, bank_s, at:at + P], m.after16[:, :], m.eye16[:, :], start=False, stop=True)
                        mm.then_inc(s_psum, 1)
                    if item[0] == "V":
                        _, c, kt = item
                        n = score_step(g, c, kt)
                        at = first_query(c, kt)
                        pe.wait_ge(exp_ready, EXP_CREDIT + HG * n + HG)
                        if kt >= 4 * c:
                            if kt % 4 == 0:
                                pe.wait_ge(val_ready, 4 * g + kt // 4 + 1)
                        if kt == 0:
                            pe.wait_ge(o_copied, 4 * g + c)
                        ends = kt == 4 * c + 3
                        for h in range(HG):
                            mm = pe.matmul(pO[32 * h:32 * h + 32, at:GT], val[:, kt, h % KH, :], prob[:, kt % 4, h, at:GT],
                                           start=(kt == 0), stop=ends)
                        if second and not by_pool(c, kt):
                            if kt == 3:
                                pe.wait_ge(recip_ready, 4 * (4 * g + c))
                            for h in range(HG):
                                mm = pe.matmul(pZ[32 * h:32 * h + 32, at:GT], ones[:, :], prob[:, kt % 4, h, at:GT],
                                               start=(kt == 3), stop=False)
                        mm.then_inc(pv_done, 1)
                    if item[0] == "Z":
                        c = item[1]
                        pe.wait_ge(z_added, EXP_CREDIT + ADDS * g + adds_before(upto(c + 1)))
                        if c == 0:
                            pe.wait_ge(recip_ready, 16 * g)
                        for h in range(HG):
                            mm = pe.matmul(pZ[32 * h:32 * h + 32, :], ones[:, :], zsum[:, h, :], start=(c == 0), stop=True)
                        mm.then_inc(z_psum, 1)
                    if item[0] == "O":
                        used += 1
                        pe.wait_ge(r_read, r + 1)
                        pe.wait_ge(o_copied, 4 * g + item[1] + 1)
                        for t in range(NTILE):
                            mm = pe.transpose(pR[:, bank, P * t:P * t + P], oT[:, P * t:P * t + P], m.eye[:, :])
                        mm.then_inc(r_psum, 1)
                    if item[0] == "K":
                        used += 1
                        pe.wait_ge(r_psum, r)
                        pe.sem_inc(r_psum, 1)
            run(pe, work)


def project2(nc, d, m):
    with ExitStack() as ctx:
        sb = lambda n, s, t=FP32: ctx.enter_context(nc.sbuf_tensor("p2_" + n, s, t))
        sem = lambda n: nc.alloc_semaphore("p2_" + n)
        sems = lambda n: [sem(f"{n}{b}") for b in range(2)]
        G = HEADS // HG
        wq_hi, wq_lo = sb("wq_hi", [P, KT, 3, G, P], F32R), sb("wq_lo", [P, KT, 3, G, P], F32R)
        wk_hi, wk_lo = sb("wk_hi", [P, KT, 2, P], F32R), sb("wk_lo", [P, KT, 2, P], F32R)
        cos, sin = sb("cos", [P, T]), sb("sin", [P, T])
        with ExitStack() as inner:
            st = lambda n, s, t=FP32: inner.enter_context(nc.sbuf_tensor("p2_" + n, s, t))
            wr_st, wk_st = st("wr_st", [P, KT, 2, G, P]), st("wk_st", [P, KT, 2, P])
            wqn, kvb = st("wqn", [P, G, C]), st("kvb", [P, G, P])
            fold_weights(nc, "p2_fold", d, kvb,
                         [(wqn[:, :, :], d["wqnT"].rearrange("(g p) f -> p g f", p=P)), (cos[:, :], d["cos"]), (sin[:, :], d["sin"])],
                         [(wqn[:, g, P * k:P * k + P], kvb[:, g, :], wq_hi[:, k, 0, g, :], wq_lo[:, k, 0, g, :])
                          for g in range(G) for k in range(KT)])
            split_weights(nc, "p2_w", [
                ([(d["wqr"].rearrange("(k p) (s g n) -> p k s g n", p=P, s=2, g=G)[:, k], wr_st[:, k]) for k in range(KT)],
                 wr_st[:, :, :, :, :], wq_hi[:, :, 1:3], wq_lo[:, :, 1:3]),
                ([(d["wk"].rearrange("(k p) (s n) -> p k s n", p=P, s=2), wk_st[:, :, :, :])], wk_st[:, :, :, :], wk_hi[:, :, :, :], wk_lo[:, :, :, :])])
        u, o = sb("u", [P, B, NTILE, C]), sb("o", [P, B, NTILE, C])
        x1, xin = sb("x1", [P, B, NTILE, C]), sb("xin", [P, B, NTILE, C])
        xn = sb("xn", [P, B, NTILE, C])
        stats, mv = sb("stats", [P, B, NTILE, 6]), sb("mv", [P, B, NTILE, 2])
        ssq, sd, rstd = sb("ssq", [P, B, NTILE]), sb("sd", [P, B, NTILE]), sb("rstd", [P, B, NTILE])
        rsd, rrms = sb("rsd", [P, B, NTILE]), sb("rrms", [P, B, NTILE])
        squares = sb("squares", [P, NTILE, C])
        xT_hi, xT_lo = sb("xT_hi", [P, B, KT, GT], F32R), sb("xT_lo", [P, B, KT, GT], F32R)
        n_hi, n_lo = sb("n_hi", [P, 2, GT], F32R), sb("n_lo", [P, 2, GT], F32R)
        r_hi, r_lo = sb("r_hi", [P, 2, GT], F32R), sb("r_lo", [P, 2, GT], F32R)
        by_cos, by_sin, turned = sb("by_cos", [P, GT]), sb("by_sin", [P, GT]), sb("turned", [P, 2, GT])
        pT = ctx.enter_context(nc.psum_tensor("p2_pT", [P, KT, GT], FP32))
        pN = ctx.enter_context(nc.psum_tensor("p2_pN", [P, 2, GT], FP32))
        pR = ctx.enter_context(nc.psum_tensor("p2_pR", [P, 2, GT], FP32))
        pL = ctx.enter_context(nc.psum_tensor("p2_pL", [P, NTILE, LAT], FP32))
        loaded, x1_ready, var_ready, sd_ready, xin_ready = (
            sems(n) for n in ("loaded", "x1_ready", "var_ready", "sd_ready", "xin_ready"))
        stored, ssq_ready, ms_ready, rsd_ready, xn_ready, xT_used = (
            sems(n) for n in ("stored", "ssq_ready", "ms_ready", "rsd_ready", "xn_ready", "xT_used"))
        t_psum, hi_ready, lo_ready = sem("t_psum"), sem("hi_ready"), sem("lo_ready")
        n_psum, n_hi_ready, n_lo_ready, n_stored = (sems(n) for n in ("n_psum", "n_hi_ready", "n_lo_ready", "n_stored"))
        r_psum, r_read, turned_ready = sem("r_psum"), sem("r_read"), sem("turned_ready")
        r_hi_ready, r_lo_ready = sem("r_hi_ready"), sem("r_lo_ready")
        r_stored = sems("r_stored")
        l_psum, l_read = sem("l_psum"), sem("l_read")
        pool_step, stats_ready, passed, sp_passed = sem("pool_step"), sem("stats_ready"), sem("passed"), sem("sp_passed")
        block = ctx.enter_context(nc.Block())
        tok = lambda name: d[name].rearrange("b (i t p) c -> b i p t c", t=NTILE, p=P)
        bc = lambda b, v: m.mod[:, b, v, :].unsqueeze(1).broadcast_to([P, NTILE, C])
        n_use = lambda i, b, g: 4 * i + 2 * b + g // 2
        r_piece = lambda i, b, g: 10 * i + 5 * b + g
        r_ring = lambda b, g: (5 * b + g) % 2
        r_use = lambda i, b, g: 5 * i + (5 * b + g) // 2

        @block.sync
        def _(sp):
            with sp.Fori(0, NGRP) as i:
                for b in range(B):
                    sp.wait_ge(x1_ready[b], i)
                    sp.dma_start(u[:, b], tok("u1")[b, bass.ds(i, 1)].rearrange("a p t c -> (a p) t c")).then_inc(loaded[b], 16)
                    for g in range(G):
                        src = d["o1"][4 * b + g, bass.ds(i * GT, GT)].rearrange("(t p) f -> p t f", p=P)
                        sp.dma_start(o[:, b, :, 64 * g:64 * g + 64], src).then_inc(loaded[b], 16)
                for b in range(B):
                    sp.wait_ge(xin_ready[b], i + 1)
                    sp.dma_start(tok("xin")[b, bass.ds(i, 1)].rearrange("a p t c -> (a p) t c"), xin[:, b]).then_inc(stored[b], 16)
                    for g in range(G + 1):
                        cols = bass.ds(i * GT, GT)
                        if g < G:
                            sp.wait_ge(n_lo_ready[g % 2], n_use(i, b, g) + 1)
                            sp.sem_inc(sp_passed, 1)
                            for s, half in enumerate((n_hi, n_lo)):
                                sp.dma_start(d["q2"][4 * b + g, s, 0, :, cols], half[:, g % 2, :].bitcast(FP32)).then_inc(n_stored[g % 2], 16)
                        sp.wait_ge(r_lo_ready, r_piece(i, b, g) + 1)
                        r = r_ring(b, g)
                        for s, half in enumerate((r_hi, r_lo)):
                            dst, rows = (d["q2"][4 * b + g, s, 1, :, cols], P) if g < G else (d["k2"][b, s, :, cols], 64)
                            sp.dma_start(dst, half[0:rows, r, :].bitcast(FP32)).then_inc(r_stored[r], 16)
                    sp.dma_start(tok("x1")[b, bass.ds(i, 1)].rearrange("a p t c -> (a p) t c"), x1[:, b]).then_inc(stored[b], 16)
            for b in range(B):
                sp.wait_ge(stored[b], 32 * NGRP)
                sp.wait_ge(n_stored[b], 32 * 4 * NGRP)
                sp.wait_ge(r_stored[b], 32 * 5 * NGRP)

        @block.gpsimd
        def _(pool):
            with pool.Fori(0, NGRP) as i:
                for b in range(B):
                    pool.wait_ge(loaded[b], 16 * (G + 1) * (i + 1))
                    pool.wait_ge(stored[b], 32 * i)
                    pool.tensor_tensor(x1[:, b], o[:, b], bc(b, 2), ALU.mult).then_inc(pool_step, 1)
                    pool.wait_ge(pool_step, 2 * i + b + 1)
                    pool.tensor_tensor(x1[:, b], x1[:, b], u[:, b], ALU.add).then_inc(x1_ready[b], 1)

        @block.scalar
        def _(act):
            with act.Fori(0, NGRP) as i:
                for b in range(B):
                    act.wait_ge(var_ready[b], i + 1)
                    act.activation(sd[:, b], mv[:, b, :, 1], ACT.Sqrt).then_inc(sd_ready[b], 1)
                    act.wait_ge(xin_ready[b], i + 1)
                    for t in range(NTILE):
                        last = act.activation(squares[:, t, :], xin[:, b, t, :], ACT.Square, accum_out=ssq[:, b, t:t + 1])
                    last.then_inc(ssq_ready[b], 1)
                    act.wait_ge(ms_ready[b], i + 1)
                    act.activation(rsd[:, b], ssq[:, b], ACT.Sqrt).then_inc(rsd_ready[b], 1)
                for b in range(B):
                    act.wait_ge(xT_used[b], i)
                    for k in range(KT):
                        act.wait_ge(t_psum, 4 * i + 2 * b + k + 1)
                        act.activation(xT_hi[:, b, k, :], pT[:, k, :], ACT.Copy, scale=m.wln[:, 0, k:k + 1]).then_inc(hi_ready, 1)
                    for g in range(G + 1):
                        if g < G:
                            act.wait_ge(n_psum[g % 2], n_use(i, b, g) + 1)
                            act.wait_ge(n_stored[g % 2], 32 * n_use(i, b, g))
                            act.activation(n_hi[:, g % 2, :], pN[:, g % 2, :], ACT.Copy).then_inc(n_hi_ready[g % 2], 1)
                        rows = P if g < G else 64
                        r = r_ring(b, g)
                        act.wait_ge(turned_ready, r_piece(i, b, g) + 1)
                        act.wait_ge(r_stored[r], 32 * r_use(i, b, g))
                        act.activation(r_hi[0:rows, r, :], turned[0:rows, r, :], ACT.Copy).then_inc(r_hi_ready, 1)

        @block.vector
        def _(dve):
            with dve.Fori(0, NGRP) as i:
                for b in range(B):
                    st = lambda n: 7 * (2 * i + b) + n
                    dve.wait_ge(x1_ready[b], i + 1)
                    for t in range(NTILE):
                        last = dve.bn_stats(stats[:, b, t, :], x1[:, b, t, :])
                    last.then_inc(stats_ready, 1)
                    dve.wait_ge(stats_ready, st(1))
                    dve.sem_inc(passed, 1)
                    for t in range(NTILE):
                        last = dve.bn_aggr(mv[:, b, t, :], stats[:, b, t, :])
                    last.then_inc(stats_ready, 1)
                    dve.wait_ge(stats_ready, st(2))
                    dve.tensor_scalar(mv[:, b, :, 1], mv[:, b, :, 1], EPS, None, ALU.add).then_inc(var_ready[b], 1)
                    dve.wait_ge(sd_ready[b], i + 1)
                    dve.reciprocal(rstd[:, b], sd[:, b]).then_inc(stats_ready, 1)
                    dve.wait_ge(stats_ready, st(3))
                    dve.wait_ge(stored[b], 32 * i)
                    for t in range(NTILE):
                        last = dve.tensor_scalar(xin[:, b, t, :], x1[:, b, t, :], mv[:, b, t, 0:1], rstd[:, b, t:t + 1],
                                                 ALU.subtract, ALU.mult)
                    last.then_inc(stats_ready, 1)
                    dve.wait_ge(stats_ready, st(4))
                    dve.tensor_tensor(xin[:, b], xin[:, b], bc(b, 4), ALU.mult).then_inc(stats_ready, 1)
                    dve.wait_ge(stats_ready, st(5))
                    dve.tensor_tensor(xin[:, b], xin[:, b], bc(b, 3), ALU.add).then_inc(xin_ready[b], 1)
                    dve.wait_ge(ssq_ready[b], i + 1)
                    dve.tensor_scalar(ssq[:, b], ssq[:, b], 1.0 / C, EPS, ALU.mult, ALU.add).then_inc(ms_ready[b], 1)
                    dve.wait_ge(rsd_ready[b], i + 1)
                    dve.reciprocal(rrms[:, b], rsd[:, b]).then_inc(stats_ready, 1)
                    dve.wait_ge(stats_ready, st(6))
                    dve.wait_ge(t_psum, 4 * i + 2 * b)
                    for t in range(NTILE):
                        last = dve.tensor_scalar(xn[:, b, t, :], xin[:, b, t, :], rrms[:, b, t:t + 1], None, ALU.mult)
                    last.then_inc(stats_ready, 1)
                    dve.wait_ge(stats_ready, st(7))
                    dve.sem_inc(xn_ready[b], 1)
                for b in range(B):
                    for k in range(KT):
                        dve.wait_ge(hi_ready, 4 * i + 2 * b + k + 1)
                        dve.scalar_tensor_tensor(out=xT_lo[:, b, k, :], in0=pT[:, k, :], scalar=m.wln[:, 0, k:k + 1],
                                                 in1=xT_hi[:, b, k, :], op0=ALU.mult, op1=ALU.subtract).then_inc(lo_ready, 1)
                    for g in range(G + 1):
                        if g < G:
                            dve.wait_ge(n_hi_ready[g % 2], n_use(i, b, g) + 1)
                            dve.tensor_tensor(n_lo[:, g % 2, :], pN[:, g % 2, :], n_hi[:, g % 2, :], ALU.subtract).then_inc(n_lo_ready[g % 2], 1)
                        rows = slice(0, P) if g < G else slice(32, 64)
                        piece = r_piece(i, b, g)
                        dve.wait_ge(r_psum, piece + 1)
                        cols = bass.ds(i * GT, GT)
                        dve.tensor_tensor(by_cos[rows, :], pR[rows, 0, :], cos[rows, cols], ALU.mult)
                        if g == G:
                            dve.tensor_copy(turned[0:32, r_ring(b, g), :], pR[0:32, 0, :])
                        dve.tensor_tensor(by_sin[rows, :], pR[rows, 1, :], sin[rows, cols], ALU.mult).then_inc(r_read, 1)
                        dve.wait_ge(r_read, piece + 1)
                        dve.tensor_tensor(turned[rows, r_ring(b, g), :], by_cos[rows, :], by_sin[rows, :], ALU.add).then_inc(turned_ready, 1)
                        rows = P if g < G else 64
                        dve.wait_ge(r_hi_ready, piece + 1)
                        dve.tensor_tensor(r_lo[0:rows, r_ring(b, g), :], turned[0:rows, r_ring(b, g), :], r_hi[0:rows, r_ring(b, g), :],
                                          ALU.subtract).then_inc(r_lo_ready, 1)
                    dve.wait_ge(l_psum, 2 * i + b + 1)
                    dve.tensor_copy(m.lat[:, bass.ds(i * NTILE + b * (T // P), NTILE), :], pL[:, :, :]).then_inc(l_read, 1)

        @block.tensor
        def _(pe):
            with pe.Fori(0, NGRP) as i:
                for b in range(B):
                    pe.wait_ge(xn_ready[b], i + 1)
                    pe.wait_ge(lo_ready, 4 * i + 2 * b)
                    for k in range(KT):
                        for t in range(NTILE):
                            mm = pe.transpose(pT[:, k, P * t:P * t + P], xn[:, b, t, P * k:P * k + P], m.eye[:, :])
                        mm.then_inc(t_psum, 1)
                    pe.wait_ge(lo_ready, 4 * i + 2 * b + 2)
                    pe.wait_ge(l_read, 2 * i + b)
                    for t in range(NTILE):
                        at = slice(P * t, P * t + P)
                        for k in range(KT):
                            mm = product3(pe, pL[:, t, :], xT_hi[:, b, k, at], xT_lo[:, b, k, at],
                                          wk_hi[:, k, 0, 0:LAT], wk_lo[:, k, 0, 0:LAT], k == 0, k == KT - 1)
                    mm.then_inc(l_psum, 1)
                    for g in range(G + 1):
                        if g < G:
                            pe.wait_ge(n_lo_ready[g % 2], n_use(i, b, g))
                            for k in range(KT):
                                mm = product3(pe, pN[:, g % 2, :], wq_hi[:, k, 0, g, :], wq_lo[:, k, 0, g, :],
                                              xT_hi[:, b, k, :], xT_lo[:, b, k, :], k == 0, k == KT - 1)
                            mm.then_inc(n_psum[g % 2], 1)
                        pe.wait_ge(r_read, r_piece(i, b, g))
                        for s in range(2):
                            for k in range(KT):
                                hi, lo = ((wq_hi[:, k, 1 + s, g, :], wq_lo[:, k, 1 + s, g, :]) if g < G
                                          else (wk_hi[:, k, s, :], wk_lo[:, k, s, :]))
                                mm = product3(pe, pR[:, s, :], hi, lo, xT_hi[:, b, k, :], xT_lo[:, b, k, :], k == 0, k == KT - 1)
                        mm.then_inc(r_psum, 1)
                    pe.wait_ge(r_psum, r_piece(i, b, G) + 1)
                    pe.sem_inc(xT_used[b], 1)


def fold_weights(nc, name, d, kvb, loads, jobs):
    with ExitStack() as ctx:
        sem = lambda n: nc.alloc_semaphore(name + n)
        ps = ctx.enter_context(nc.psum_tensor(name + "_ps", [P, 2, GT], FP32))
        zeroed, loaded, product, high, low = (sem(n) for n in ("_zeroed", "_loaded", "_product", "_high", "_low"))
        block = ctx.enter_context(nc.Block())

        @block.gpsimd
        def _(pool):
            pool.memset(kvb[:, :, :], 0.0).then_inc(zeroed, 1)

        @block.sync
        def _(sp):
            sp.wait_ge(zeroed, 1)
            src = d["wkvbT"].rearrange("(g j n) r -> j n g r", j=HG, n=32)
            for j in range(HG):
                sp.dma_start(kvb[32 * j:32 * j + 32, :, 32 * j:32 * j + 32], src[j]).then_inc(loaded, 16)
            for dst, src in loads:
                sp.dma_start(dst, src).then_inc(loaded, 16)

        @block.tensor
        def _(pe):
            pe.wait_ge(loaded, 16 * (HG + len(loads)))
            for n, (left, right, hi, lo) in enumerate(jobs):
                if n >= 2:
                    pe.wait_ge(low, n - 1)
                pe.matmul(ps[:, n % 2, 0:right.shape[-1]], left, right, start=True, stop=True).then_inc(product, 1)

        @block.scalar
        def _(act):
            for n, (left, right, hi, lo) in enumerate(jobs):
                act.wait_ge(product, n + 1)
                act.activation(hi, ps[:, n % 2, 0:right.shape[-1]], ACT.Copy).then_inc(high, 1)

        @block.vector
        def _(dve):
            for n, (left, right, hi, lo) in enumerate(jobs):
                dve.wait_ge(high, n + 1)
                dve.tensor_tensor(lo, ps[:, n % 2, 0:right.shape[-1]], hi, ALU.subtract).then_inc(low, 1)


def experts(nc, d, m):
    with ExitStack() as ctx:
        sb = lambda n, s, t=FP32: ctx.enter_context(nc.sbuf_tensor("e_" + n, s, t))
        sem = lambda n: nc.alloc_semaphore("e_" + n)
        sems = lambda n: [sem(f"{n}{b}") for b in range(2)]
        G, EX = HEADS // HG, E + 1
        wo_hi, wo_lo = sb("wo_hi", [P, G, C], F32R), sb("wo_lo", [P, G, C], F32R)
        wg_hi, wg_lo = sb("wg_hi", [P, KT, EX, I], F32R), sb("wg_lo", [P, KT, EX, I], F32R)
        wu_hi, wu_lo = sb("wu_hi", [P, KT, EX, I], F32R), sb("wu_lo", [P, KT, EX, I], F32R)
        wd_hi, wd_lo = sb("wd_hi", [P, EX, C], F32R), sb("wd_lo", [P, EX, C], F32R)
        gate_hi, gate_lo = sb("gate_hi", [P, KT, E], F32R), sb("gate_lo", [P, KT, E], F32R)
        sel_st = sb("sel_st", [64, E, P])
        sel = sb("sel", [64, E, P], F32R)
        rank = sb("rank", [P, E])
        with ExitStack() as inner:
            st = lambda n, s, t=FP32: inner.enter_context(nc.sbuf_tensor("e_" + n, s, t))
            wo, kvb = st("wo", [P, G, C]), st("kvb", [P, G, P])
            fold_weights(nc, "e_fold", d, kvb,
                         [(wo[32 * j:32 * j + 32, :, :], d["Wo"].rearrange("(g j n) c -> j n g c", j=HG, n=HD2)[j, 0:32])
                          for j in range(HG)] + [(sel_st[:, :, :], d["sel"].rearrange("k (e p) -> k e p", e=E)),
                                                 (rank[:, :], d["rank"].rearrange("(a n) -> a n", a=1).broadcast_to([P, E]))],
                         [(kvb[:, g, :], wo[:, g, :], wo_hi[:, g, :], wo_lo[:, g, :]) for g in range(G)])
        with ExitStack() as inner:
            st = lambda n, s, t=FP32: inner.enter_context(nc.sbuf_tensor("e_" + n, s, t))
            g_st, u_st, d_st, gate_st = (st("g_st", [P, KT, EX, I]), st("u_st", [P, KT, EX, I]), st("d_st", [P, EX, C]),
                                         st("gate_st", [P, KT, E]))
            up = lambda name: d[name].rearrange("e (k p) n -> p k e n", p=P)
            split_weights(nc, "e_w", [
                ([(up("Wg")[:, k], g_st[:, k, 0:E]) for k in range(KT)] + [(up("sWg")[:, k], g_st[:, k, E:EX]) for k in range(KT)],
                 g_st[:, :, :, :], wg_hi[:, :, :, :], wg_lo[:, :, :, :]),
                ([(up("Wu")[:, k], u_st[:, k, 0:E]) for k in range(KT)] + [(up("sWu")[:, k], u_st[:, k, E:EX]) for k in range(KT)],
                 u_st[:, :, :, :], wu_hi[:, :, :, :], wu_lo[:, :, :, :]),
                ([(d["Wd"].rearrange("e p n -> p e n"), d_st[:, 0:E, :]), (d["sWd"].rearrange("e p n -> p e n"), d_st[:, E:EX, :])],
                 d_st[:, :, :], wd_hi[:, :, :], wd_lo[:, :, :]),
                ([(d["Wgate"].rearrange("(k p) n -> p k n", p=P), gate_st[:, :, :])],
                 gate_st[:, :, :], gate_hi[:, :, :], gate_lo[:, :, :])])
        o_st = sb("o_st", [P, G, GT])
        o_hi, o_lo = sb("o_hi", [P, G, GT], F32R), sb("o_lo", [P, G, GT], F32R)
        xin, x1, x2 = sb("xin", [P, B, NTILE, C]), sb("x1", [P, B, NTILE, C]), sb("x2", [P, B, NTILE, C])
        y = sb("y", [P, B, NTILE, C])
        xn, squares = sb("xn", [P, NTILE, C]), sb("squares", [P, NTILE, C])
        ssq, rms, rrms = sb("ssq", [P, NTILE]), sb("rms", [P, NTILE]), sb("rrms", [P, NTILE])
        xT_hi, xT_lo = sb("xT_hi", [P, B, KT, GT], F32R), sb("xT_lo", [P, B, KT, GT], F32R)
        logit, pick1, pick2 = sb("logit", [P, NTILE, E]), sb("pick1", [P, NTILE, E]), sb("pick2", [P, NTILE, E])
        top, best = sb("top", [P, 2, NTILE]), sb("best", [P, NTILE])
        gap, weight = sb("gap", [P, 2, NTILE]), sb("weight", [P, 2, NTILE])
        comb = sb("comb", [P, NTILE, E])
        combT = sb("combT", [64, B, GT], F32R)
        silu, prod = sb("silu", [P, 2, GT]), sb("prod", [P, 2, GT])
        p_hi, p_lo = sb("p_hi", [P, 2, GT], F32R), sb("p_lo", [P, 2, GT], F32R)
        pPair = ctx.enter_context(nc.psum_tensor("e_pPair", [P, 2, 2, GT], FP32))
        pD = ctx.enter_context(nc.psum_tensor("e_pD", [P, NTILE, C], FP32))
        pB = ctx.enter_context(nc.psum_tensor("e_pB", [P, GT], FP32))
        pG = ctx.enter_context(nc.psum_tensor("e_pG", [P, GT], FP32))

        filled, sel_ready, sp_passed = sem("filled"), sem("sel_ready"), sem("sp_passed")
        o_loaded, x_loaded, out_stored = sem("o_loaded"), sems("x_loaded"), sems("out_stored")
        o_hi_ready, o_lo_ready = sem("o_hi_ready"), sem("o_lo_ready")
        pair_psum, pair_read = sem("pair_psum"), sem("pair_read")
        x2_ready, ssq_ready, ms_ready, rms_ready, xn_ready = sem("x2_ready"), sem("ssq_ready"), sem("ms_ready"), sem("rms_ready"), sem("xn_ready")
        xT_hi_ready, xT_ready = sem("xT_hi_ready"), sem("xT_ready")
        g_psum, g_read, chain = sem("g_psum"), sem("g_read"), sem("chain")
        gap_ready, weight_ready, comb_ready, combT_hi_ready, combT_ready = (
            sem("gap_ready"), sem("weight_ready"), sem("comb_ready"), sem("combT_hi_ready"), sem("combT_ready"))
        b_psum, b_read = sem("b_psum"), sem("b_read")
        silu_ready, gated, prod_ready, p_hi_ready, p_lo_ready = (
            sem("silu_ready"), sem("gated"), sem("prod_ready"), sem("p_hi_ready"), sem("p_lo_ready"))
        down_done, y_sum, y_scaled, y_ready = sem("down_done"), sem("y_sum"), sem("y_scaled"), sem("y_ready")
        block = ctx.enter_context(nc.Block())
        RING = 2

        FRONT = ("P", "A", "N", "R", "X", "L", "W", "C")

        def order(experts_too, front):
            after = {1: "P", 2: "A", 3: "NR", 4: "X", 5: "L", 6: "W", 7: "C"}
            if not experts_too:
                return [(s, 0) for s in FRONT]
            items = []
            for j in range(EX):
                items.append(("G", j))
                if j < E:
                    items.append(("B", j))
                if j:
                    items.append(("D", j - 1))
                if front:
                    items += [(s, 0) for s in after.get(j, "")]
            return items + [("D", E), ("Y", 0)]

        PAIRS = EX + 2

        def run(eng, work):
            work(order(False, True), -1, 1, 0, 0, 0, 0)
            with eng.Fori(0, NGRP - 1) as i:
                for b in range(B):
                    work(order(True, True), i, b, i + b, 1 - b, 2 + PAIRS * (2 * i + b), b)
            i = NGRP - 1
            work(order(True, True), i, 0, i, 1, 2 + PAIRS * 2 * i, 0)
            work(order(True, False), i, 1, 0, 0, 2 + PAIRS * (2 * i + 1), 1)

        tok = lambda name, b, i: d[name].rearrange("b (i t p) c -> b i p t c", t=NTILE, p=P)[b, bass.ds(i, 1)].rearrange("a p t c -> (a p) t c")

        @block.sync
        def _(sp):
            def work(items, i, b, fi, fb, pair, parity):
                if ("P", 0) in items:
                    fn = 2 * fi + fb
                    sp.wait_ge(o_lo_ready, fn)
                    sp.dma_start(o_st[:, :, :], d["o2"][4 * fb:4 * fb + 4, :, bass.ds(fi * GT, GT)].rearrange("g p t -> p g t")).then_inc(o_loaded, 16)
                    if ("Y", 0) in items:
                        sp.wait_ge(y_ready, 2 * i + b)
                        sp.sem_inc(sp_passed, 1)
                    sp.dma_start(xin[:, fb], tok("xin", fb, fi)).then_inc(x_loaded[fb], 16)
                    sp.dma_start(x1[:, fb], tok("x1", fb, fi)).then_inc(x_loaded[fb], 16)
                if ("Y", 0) in items:
                    sp.wait_ge(y_ready, 2 * i + b + 1)
                    sp.sem_inc(sp_passed, 1)
                    sp.dma_start(tok("out", b, i), y[:, b]).then_inc(out_stored[b], 16)
            run(sp, work)
            for b in range(B):
                sp.wait_ge(out_stored[b], 16 * NGRP)

        @block.gpsimd
        def _(pool):
            pool.memset(combT[:, :, :].bitcast(FP32), 0.0).then_inc(filled, 1)
            pool.sem_inc(p_lo_ready, RING)

            def work(items, i, b, fi, fb, pair, parity):
                n, fn = 2 * i + b, 2 * fi + fb
                for step, j in items:
                    use, s = EX * n + j, (b + j) % 2
                    if step == "P":
                        pool.wait_ge(o_hi_ready, fn + 1)
                        pool.tensor_tensor(o_lo[:, :, :], o_st[:, :, :], o_hi[:, :, :], ALU.subtract).then_inc(o_lo_ready, 1)
                    if step == "B" or step == "G" and j == E:
                        pool.wait_ge(p_hi_ready, use + 1)
                        pool.wait_ge(down_done, use + 1)
                        pool.tensor_tensor(p_lo[:, s, :], prod[:, s, :], p_hi[:, s, :], ALU.subtract).then_inc(p_lo_ready, 1)
                    if step == "Y":
                        pool.wait_ge(y_sum, n + 1)
                        pool.tensor_tensor(y[:, b], y[:, b], m.mod[:, b, 5, :].unsqueeze(1).broadcast_to([P, NTILE, C]),
                                           ALU.mult).then_inc(y_scaled, 1)
                        pool.wait_ge(y_scaled, n + 1)
                        pool.tensor_tensor(y[:, b], y[:, b], x1[:, b], ALU.add).then_inc(y_ready, 1)
            run(pool, work)

        @block.scalar
        def _(act):
            act.activation(sel[:, :, :], sel_st[:, :, :], ACT.Copy).then_inc(sel_ready, 1)

            def work(items, i, b, fi, fb, pair, parity):
                n, fn = 2 * i + b, 2 * fi + fb
                used = 0
                for step, j in items:
                    use, s = EX * n + j, (b + j) % 2
                    if step == "P":
                        act.wait_ge(o_loaded, 16 * (fn + 1))
                        act.wait_ge(x2_ready, fn)
                        act.activation(o_hi[:, :, :], o_st[:, :, :], ACT.Copy).then_inc(o_hi_ready, 1)
                    if step == "N":
                        act.wait_ge(x2_ready, fn + 1)
                        for t in range(NTILE):
                            last = act.activation(squares[:, t, :], x2[:, fb, t, :], ACT.Square, accum_out=ssq[:, t:t + 1])
                        last.then_inc(ssq_ready, 1)
                    if step == "R":
                        act.wait_ge(ms_ready, fn + 1)
                        act.activation(rms[:, :], ssq[:, :], ACT.Sqrt).then_inc(rms_ready, 1)
                    if step == "X":
                        act.wait_ge(pair_psum, pair + used + 1)
                        for k in range(KT):
                            last = act.activation(xT_hi[:, fb, k, :], pPair[:, (parity + used) % 2, k, :], ACT.Copy, scale=m.wln[:, 1, k:k + 1])
                        last.then_inc(xT_hi_ready, 1)
                    if step == "W":
                        act.wait_ge(gap_ready, fn + 1)
                        act.activation(weight[:, :, :], gap[:, :, :], ACT.Sigmoid).then_inc(weight_ready, 1)
                    if step == "C":
                        act.wait_ge(g_psum, 2 * fn + 2)
                        act.activation(combT[0:E, fb, :], pG[0:E, :], ACT.Copy).then_inc(combT_hi_ready, 1)
                    if step == "G":
                        act.wait_ge(pair_psum, pair + used + 1)
                        act.wait_ge(prod_ready, use + 1)
                        act.activation(silu[:, s, :], pPair[:, (parity + used) % 2, 0, :], ACT.Silu).then_inc(silu_ready, 1)
                    if step == "B" or step == "G" and j == E:
                        act.wait_ge(prod_ready, RING + use + 1)
                        act.wait_ge(down_done, use + 1)
                        act.activation(p_hi[:, s, :], prod[:, s, :], ACT.Copy).then_inc(p_hi_ready, 1)
                    used += step in "GAX"
            run(act, work)

        @block.vector
        def _(dve):
            dve.sem_inc(prod_ready, RING)
            dve.sem_inc(pair_read, RING)
            dve.sem_inc(g_read, 1)
            dve.sem_inc(b_read, 1)
            LINKS = 11

            def work(items, i, b, fi, fb, pair, parity):
                n, fn = 2 * i + b, 2 * fi + fb
                used, links = 0, 0
                per_token = lambda t: t.unsqueeze(2).broadcast_to([P, NTILE, E])

                for step, j in items:
                    use, s = EX * n + j, (b + j) % 2
                    q = (parity + used) % 2
                    if step == "A":
                        dve.wait_ge(pair_psum, pair + used + 1)
                        dve.wait_ge(x_loaded[fb], 32 * (fi + 1))
                        dve.tensor_tensor(x2[:, fb], xin[:, fb], pPair[:, q, :, :].rearrange("p k (t c) -> p (k t) c", c=C),
                                          ALU.add).then_inc(x2_ready, 1)
                        dve.wait_ge(x2_ready, fn + 1)
                        dve.sem_inc(pair_read, 1)
                    if step == "R":
                        dve.wait_ge(ssq_ready, fn + 1)
                        dve.tensor_scalar(ssq[:, :], ssq[:, :], 1.0 / C, EPS, ALU.mult, ALU.add).then_inc(ms_ready, 1)
                        dve.wait_ge(rms_ready, fn + 1)
                        dve.reciprocal(rrms[:, :], rms[:, :]).then_inc(chain, 1)
                        dve.wait_ge(chain, LINKS * fn + 1)
                        for t in range(NTILE):
                            last = dve.tensor_scalar(xn[:, t, :], x2[:, fb, t, :], rrms[:, t:t + 1], None, ALU.mult)
                        last.then_inc(xn_ready, 1)
                    if step == "X":
                        dve.wait_ge(xT_hi_ready, fn + 1)
                        for k in range(KT):
                            last = dve.scalar_tensor_tensor(out=xT_lo[:, fb, k, :], in0=pPair[:, q, k, :], scalar=m.wln[:, 1, k:k + 1],
                                                            in1=xT_hi[:, fb, k, :], op0=ALU.mult, op1=ALU.subtract)
                        last.then_inc(xT_ready, 1)
                        dve.wait_ge(xT_ready, fn + 1)
                        dve.sem_inc(pair_read, 1)
                    if step == "L":
                        links = 1

                        def link(ins):
                            nonlocal links
                            links += 1
                            ins.then_inc(chain, 1)
                            dve.wait_ge(chain, LINKS * fn + links)

                        dve.wait_ge(g_psum, 2 * fn + 1)
                        dve.tensor_tensor(logit[:, :, :], pG[:, 0:NTILE * E].rearrange("p (t e) -> p t e", e=E),
                                          m.ebias[:, :].unsqueeze(1).broadcast_to([P, NTILE, E]), ALU.add).then_inc(g_read, 1)
                        dve.wait_ge(g_read, 1 + 2 * fn + 1)
                        for c, pick in enumerate((pick1, pick2)):
                            link(dve.tensor_reduce(top[:, c, :], logit[:, :, :], axis=AX.X, op=ALU.max))
                            link(dve.tensor_tensor(pick[:, :, :], logit[:, :, :], per_token(top[:, c, :]), ALU.is_equal))
                            link(dve.tensor_tensor(pick[:, :, :], pick[:, :, :], rank[:, :].unsqueeze(1).broadcast_to([P, NTILE, E]), ALU.mult))
                            link(dve.tensor_reduce(best[:, :], pick[:, :, :], axis=AX.X, op=ALU.max))
                            if c == 0:
                                link(dve.tensor_tensor(pick[:, :, :], pick[:, :, :], per_token(best[:, :]), ALU.is_equal))
                                link(dve.scalar_tensor_tensor(out=logit[:, :, :], in0=pick[:, :, :], scalar=NEG, in1=logit[:, :, :],
                                                              op0=ALU.mult, op1=ALU.add))
                            else:
                                dve.tensor_tensor(pick[:, :, :], pick[:, :, :], per_token(best[:, :]), ALU.is_equal)
                        dve.tensor_tensor(gap[:, 0, :], top[:, 0, :], top[:, 1, :], ALU.subtract)
                        dve.tensor_tensor(gap[:, 1, :], top[:, 1, :], top[:, 0, :], ALU.subtract).then_inc(gap_ready, 1)
                        assert links == LINKS
                    if step == "W":
                        dve.wait_ge(weight_ready, fn + 1)
                        dve.tensor_tensor(pick1[:, :, :], pick1[:, :, :], per_token(weight[:, 0, :]), ALU.mult)
                        dve.tensor_tensor(pick2[:, :, :], pick2[:, :, :], per_token(weight[:, 1, :]), ALU.mult).then_inc(comb_ready, 1)
                        dve.wait_ge(comb_ready, 2 * fn + 1)
                        dve.tensor_tensor(comb[:, :, :], pick1[:, :, :], pick2[:, :, :], ALU.add).then_inc(comb_ready, 1)
                    if step == "C":
                        dve.wait_ge(combT_hi_ready, fn + 1)
                        dve.tensor_tensor(combT[32:32 + E, fb, :], pG[0:E, :], combT[0:E, fb, :], ALU.subtract).then_inc(combT_ready, 1)
                        dve.wait_ge(combT_ready, fn + 1)
                        dve.sem_inc(g_read, 1)
                    if step == "G":
                        dve.wait_ge(silu_ready, use + 1)
                        dve.wait_ge(p_lo_ready, use + 1)
                        dve.tensor_tensor(prod[:, s, :], pPair[:, q, 1, :], silu[:, s, :], ALU.mult).then_inc(pair_read, 1)
                        if j == E:
                            dve.wait_ge(pair_read, RING + pair + used + 1)
                            dve.sem_inc(prod_ready, 1)
                    if step == "B":
                        before = used - 1
                        dve.wait_ge(pair_read, RING + pair + before + 1)
                        dve.wait_ge(b_psum, E * n + j + 1)
                        dve.tensor_tensor(prod[:, s, :], prod[:, s, :], pB[:, :], ALU.mult).then_inc(prod_ready, 1)
                        dve.wait_ge(prod_ready, RING + use + 1)
                        dve.sem_inc(b_read, 1)
                    if step == "Y":
                        dve.wait_ge(down_done, RING + EX * (n + 1))
                        dve.wait_ge(out_stored[b], 16 * i)
                        dve.tensor_tensor(y[:, b], x2[:, b], pD[:, :, :], ALU.add).then_inc(y_sum, 1)
                    used += step in "GAX"
            run(dve, work)

        @block.tensor
        def _(pe):
            pe.sem_inc(down_done, RING)
            pe.wait_ge(filled, 1)
            pe.wait_ge(sel_ready, 1)

            def work(items, i, b, fi, fb, pair, parity):
                n, fn = 2 * i + b, 2 * fi + fb
                used = 0
                for step, j in items:
                    use, s = EX * n + j, (b + j) % 2
                    q = (parity + used) % 2
                    if step in "GAX":
                        pe.wait_ge(pair_read, pair + used + 1)
                        used += 1
                    if step == "A":
                        pe.wait_ge(o_lo_ready, fn + 1)
                        for t in range(NTILE):
                            at = slice(P * t, P * t + P)
                            for g in range(G):
                                mm = product3(pe, pPair[:, q, t // 2, C * (t % 2):C * (t % 2) + C], o_hi[:, g, at], o_lo[:, g, at],
                                              wo_hi[:, g, :], wo_lo[:, g, :], g == 0, g == G - 1)
                        mm.then_inc(pair_psum, 1)
                    if step == "X":
                        pe.wait_ge(xn_ready, fn + 1)
                        for k in range(KT):
                            for t in range(NTILE):
                                mm = pe.transpose(pPair[:, q, k, P * t:P * t + P], xn[:, t, P * k:P * k + P], m.eye[:, :])
                        mm.then_inc(pair_psum, 1)
                    if step == "L":
                        pe.wait_ge(xT_ready, fn + 1)
                        pe.wait_ge(g_read, 2 * fn + 1)
                        for t in range(NTILE):
                            at = slice(P * t, P * t + P)
                            for k in range(KT):
                                mm = product3(pe, pG[:, E * t:E * t + E], xT_hi[:, fb, k, at], xT_lo[:, fb, k, at],
                                              gate_hi[:, k, :], gate_lo[:, k, :], k == 0, k == KT - 1)
                        mm.then_inc(g_psum, 1)
                    if step == "C":
                        pe.wait_ge(comb_ready, 2 * fn + 2)
                        for t in range(NTILE):
                            mm = pe.transpose(pG[0:E, P * t:P * t + P], comb[:, t, :], m.eye[:, :])
                        mm.then_inc(g_psum, 1)
                    if step == "G":
                        if j == 0:
                            pe.wait_ge(combT_ready, n + 1)
                        for s_, (hi, lo) in enumerate(((wg_hi, wg_lo), (wu_hi, wu_lo))):
                            for k in range(KT):
                                mm = product3(pe, pPair[:, q, s_, :], hi[:, k, j, :], lo[:, k, j, :],
                                              xT_hi[:, b, k, :], xT_lo[:, b, k, :], k == 0, k == KT - 1)
                        mm.then_inc(pair_psum, 1)
                    if step == "B":
                        pe.wait_ge(b_read, E * n + j + 1)
                        pe.matmul(pB[:, :], sel[:, j, :], combT[:, b, :], start=True, stop=True).then_inc(b_psum, 1)
                    if step == "D":
                        if j == 0:
                            pe.wait_ge(y_sum, n)
                        pe.wait_ge(p_lo_ready, RING + use + 1)
                        for t in range(NTILE):
                            at = slice(P * t, P * t + P)
                            mm = product3(pe, pD[:, t, :], p_hi[:, s, at], p_lo[:, s, at], wd_hi[:, j, :], wd_lo[:, j, :],
                                          j == 0 and t % 2 == 0, j == E, skip_group_check=True)
                        mm.then_inc(down_done, 1)
            run(pe, work)


class Resident:
    pass


def adaln_moe_kernel(nc, d):
    for name, shape in (("u1", (B, T, C)), ("qk1", (2, 2, B * C, T)), ("o1", (NG, T, HG * HD1)), ("x1", (B, T, C)),
                        ("xin", (B, T, C)), ("q2", (NG, 2, 2, P, T)), ("k2", (B, 2, LAT + ROPE, T)), ("o2", (NG, P, T))):
        d[name] = nc.dram_tensor("mid_" + name, shape, FP32, kind="Internal").ap()
    m = Resident()
    with ExitStack() as ctx:
        sb = lambda n, s, t=FP32: ctx.enter_context(nc.sbuf_tensor(n, s, t))
        m.eye, m.causal = sb("eye", [P, P]), sb("causal", [P, GT])
        m.bqk, m.bv = sb("bqk", [P, 2 * KT]), sb("bv", [P, C])
        m.wln, m.ebias = sb("wln", [P, 2, KT]), sb("ebias", [P, E])
        m.eye16, m.after16 = sb("eye16", [P, P], BF16), sb("after16", [P, P], BF16)
        m.mod = sb("mod", [P, B, 6, C])
        with nc.cleanup_on_exit():
            modulation(nc, d, m)
        with ExitStack() as inner:
            m.v1 = inner.enter_context(nc.sbuf_tensor("v1", [P, NG, T // P, HG * HD1], FP32))
            with nc.cleanup_on_exit():
                project1(nc, d, m)
            with nc.cleanup_on_exit():
                attention(nc, d, m, False)
        with ExitStack() as inner:
            m.lat = inner.enter_context(nc.sbuf_tensor("lat", [P, B * T // P, LAT], FP32))
            with nc.cleanup_on_exit():
                project2(nc, d, m)
            with nc.cleanup_on_exit():
                attention(nc, d, m, True)
        with nc.cleanup_on_exit():
            experts(nc, d, m)


def kernel(**inputs):
    import numpy as _np
    import concourse.bacc as _bacc
    from concourse import mybir as _mybir
    from concourse.bass_utils import run_bass_kernel_spmd as _run

    f = {name: _np.asarray(value) for name, value in inputs.items()}
    wq = f["L0_ffn_Wq"].reshape(C, HEADS, HD2)
    turn = _np.concatenate([_np.arange(0, ROPE, 2), _np.arange(1, ROPE, 2)])
    swap = _np.concatenate([turn[ROPE // 2:], turn[:ROPE // 2]])
    wkva = f["L0_ffn_Wkva"]
    latent = wkva[:, :LAT]
    cos, sin = rope_tables()
    causal = _np.zeros((P, GT), _np.float32)
    causal[:, GT - P:] = _np.where(_np.arange(P)[None, :] > _np.arange(P)[:, None], _np.float32(NEG), _np.float32(0))
    sel = _np.zeros((64, E, P), _np.float32)
    for e in range(E):
        sel[e, e] = sel[32 + e, e] = 1
    data = {
        "x": f["L0_attn_x"], "wT": f["L0_attn_W"].T, "bqk": f["L0_attn_b"][:2 * C].reshape(-1, P).T,
        "bv": f["L0_attn_b"][2 * C:], "cT": f["L0_c"].T, "wmod": f["L0_wmod"],
        "wln": _np.stack([f["L0_ffn_w_ln1"].reshape(KT, P).T, f["L0_ffn_w_ln2"].reshape(KT, P).T], axis=1), "ebias": f["L0_ffn_expert_bias"],
        "wqnT": wq[:, :, :HD2 - ROPE].transpose(1, 2, 0).reshape(-1, C), "wkvbT": f["L0_ffn_Wkvb"].T,
        "wqr": _np.stack([wq[:, :, ROPE:][:, :, turn], wq[:, :, ROPE:][:, :, swap]], axis=1).reshape(C, -1),
        "wk": _np.concatenate([latent, wkva[:, LAT:][:, turn], latent, wkva[:, LAT:][:, turn]] + [wkva[:, LAT:][:, swap]] * 4, axis=1),
        "Wo": f["L0_ffn_Wo"], "Wgate": f["L0_ffn_Wgate"], "Wg": f["L0_ffn_Wg"], "Wu": f["L0_ffn_Wu"], "Wd": f["L0_ffn_Wd"],
        "sWg": f["L0_ffn_sWg"], "sWu": f["L0_ffn_sWu"], "sWd": f["L0_ffn_sWd"],
        "eye": _np.eye(P, dtype=_np.float32), "causal": causal, "cos": _np.tile(cos, (4, 1)), "sin": _np.tile(sin, (4, 1)),
        "sel": sel.reshape(64, -1), "rank": _np.arange(E, 0, -1).astype(_np.float32),
    }
    nc = _bacc.Bacc("TRN2", target_bir_lowering=False, num_devices=1)
    arrays, d = {}, {}
    for name, a in data.items():
        a = _np.ascontiguousarray(a)
        arrays[f"in_{name}_dram"] = a
        d[name] = nc.dram_tensor(f"in_{name}_dram", a.shape, _mybir.dt.from_np(a.dtype), kind="ExternalInput").ap()
    d["out"] = nc.dram_tensor("out_0_dram", (B, T, C), _mybir.dt.from_np(_np.dtype("float32")), kind="ExternalOutput").ap()
    adaln_moe_kernel(nc, d)
    r = _run(nc, [arrays], core_ids=[0])
    return r.results[0]["out_0_dram"]
```

```python
import numpy as np
import concourse.bass as bass
from concourse import mybir
from concourse.alu_op_type import AluOpType as ALU
from contextlib import ExitStack

FP32 = mybir.dt.float32
F32R = mybir.dt.float32r
BF16 = mybir.dt.bfloat16
ACT = mybir.ActivationFunctionType
AX = mybir.AxisListType

B, T, C = 2, 2048, 256
P = 128
KT = C // P
GT = 512
NTILE = GT // P
NGRP = T // GT
HEADS = 16
HG = 4
NG = B * HEADS // HG
HD1 = C // HEADS
HD2, ROPE, LAT = 64, 32, 32
E, I = 8, 128
EPS = 1e-5
NEG = -1e30


def rope_tables():
    freqs = (np.float32(1.0) / np.float32(100000.0) ** (np.arange(0, ROPE, 2, dtype=np.float32) / np.float32(ROPE))).astype(np.float32)
    ang = np.outer(freqs, np.arange(T, dtype=np.float32)).astype(np.float32)
    cos, sin = np.cos(ang).astype(np.float32), np.sin(ang).astype(np.float32)
    return np.concatenate([cos, cos]), np.concatenate([-sin, sin])



def modulation(nc, d, m):
    with ExitStack() as ctx:
        sb = lambda n, s, t=FP32: ctx.enter_context(nc.sbuf_tensor(n, s, t))
        sem = lambda n: nc.alloc_semaphore(n)
        cT, cE = sb("cT", [P, KT, B]), sb("cE", [P, KT, B])
        cB = sb("cB", [P, KT, B, P])
        wmod = sb("wmod", [P, KT, 6 * C])
        size, sign = sb("ga_size", [P, B, C]), sb("ga_sign", [P, B, C])
        ps = ctx.enter_context(nc.psum_tensor("ps_mod", [P, 6, 512], FP32))
        loaded, c_exp, c_ready, mod_psum, mod_read, chain = (
            sem(n) for n in ("mod_loaded", "mod_c_exp", "mod_c_ready", "mod_psum", "mod_read", "mod_chain"))
        block = ctx.enter_context(nc.Block())
        LOADS = 8

        @block.sync
        def _(sp):
            sp.dma_start(cT[:, :, :], d["cT"].rearrange("(k p) b -> p k b", p=P)).then_inc(loaded, 16)
            sp.dma_start(wmod[:, :, :], d["wmod"].rearrange("(k p) n -> p k n", p=P)).then_inc(loaded, 16)
            sp.dma_start(m.eye[:, :], d["eye"]).then_inc(loaded, 16)
            sp.dma_start(m.causal[:, :], d["causal"]).then_inc(loaded, 16)
            sp.dma_start(m.bqk[:, :], d["bqk"]).then_inc(loaded, 16)
            sp.dma_start(m.bv[:, :], d["bv"].rearrange("(a n) -> a n", a=1).broadcast_to([P, C])).then_inc(loaded, 16)
            sp.dma_start(m.wln[:, :, :], d["wln"]).then_inc(loaded, 16)
            sp.dma_start(m.ebias[:, :], d["ebias"].rearrange("(a n) -> a n", a=1).broadcast_to([P, E])).then_inc(loaded, 16)

        @block.scalar
        def _(act):
            act.wait_ge(loaded, 16 * LOADS)
            act.activation(cE[:, :, :], cT[:, :, :], ACT.Exp, scale=-1.0).then_inc(c_exp, 1)

        @block.tensor
        def _(pe):
            pe.wait_ge(c_ready, 1)
            for b in range(B):
                for n in range(3):
                    for k in range(KT):
                        mm = pe.matmul(ps[:, 3 * b + n, :], cB[:, k, b, :], wmod[:, k, 512 * n:512 * n + 512],
                                       start=(k == 0), stop=(k == KT - 1))
                    mm.then_inc(mod_psum, 1)

        @block.vector
        def _(dve):
            done = [0]

            def link(ins):
                done[0] += 1
                ins.then_inc(chain, 1)
                dve.wait_ge(chain, done[0])

            dve.wait_ge(c_exp, 1)
            dve.tensor_copy(m.eye16[:, :], m.eye[:, :])
            dve.tensor_copy(m.after16[:, :], m.causal[:, GT - P:GT])
            link(dve.tensor_scalar(cE[:, :, :], cE[:, :, :], 1.0, None, ALU.add))
            link(dve.reciprocal(cE[:, :, :], cE[:, :, :]))
            link(dve.tensor_tensor(cT[:, :, :], cT[:, :, :], cE[:, :, :], ALU.mult))
            dve.tensor_copy(cB[:, :, :, :], cT[:, :, :].unsqueeze(3).broadcast_to([P, KT, B, P])).then_inc(c_ready, 1)
            for b in range(B):
                for n in range(3):
                    dve.wait_ge(mod_psum, 3 * b + n + 1)
                    dve.tensor_copy(m.mod[:, b, 2 * n:2 * n + 2, :],
                                    ps[:, 3 * b + n, :].rearrange("p (a c) -> p a c", a=2)).then_inc(mod_read, 1)
            dve.wait_ge(mod_read, 6)
            for v in (1, 4):
                link(dve.tensor_scalar(m.mod[:, :, v, :], m.mod[:, :, v, :], 1.0, None, ALU.add))
            for v in (2, 5):
                link(dve.tensor_scalar(sign[:, :, :], m.mod[:, :, v, :], 0.0, 2.0, ALU.is_ge, ALU.mult))
                link(dve.tensor_scalar(size[:, :, :], m.mod[:, :, v, :], -1.0, None, ALU.mult))
                link(dve.tensor_tensor(size[:, :, :], size[:, :, :], m.mod[:, :, v, :], ALU.max))
                link(dve.tensor_scalar(size[:, :, :], size[:, :, :], 0.25, None, ALU.max))
                link(dve.scalar_tensor_tensor(out=m.mod[:, :, v, :], in0=sign[:, :, :], scalar=-1.0, in1=size[:, :, :],
                                              op0=ALU.add, op1=ALU.mult))


def product3(pe, out, hi, lo, x_hi, x_lo, first, last, **kw):
    pe.matmul(out, lo, x_hi, start=first, stop=False, **kw)
    pe.matmul(out, hi, x_lo, start=False, stop=False, **kw)
    return pe.matmul(out, hi, x_hi, start=False, stop=last, **kw)


def split_weights(nc, name, jobs):
    with ExitStack() as ctx:
        sem = lambda n: nc.alloc_semaphore(name + n)
        loaded = [sem(f"_loaded{n}") for n in range(len(jobs))]
        high = sem("_high")
        block = ctx.enter_context(nc.Block())

        @block.sync
        def _(sp):
            for n, (loads, stage, hi, lo) in enumerate(jobs):
                for src, place in loads:
                    sp.dma_start(place, src).then_inc(loaded[n], 16)

        @block.scalar
        def _(act):
            for n, (loads, stage, hi, lo) in enumerate(jobs):
                act.wait_ge(loaded[n], 16 * len(loads))
                act.activation(hi, stage, ACT.Copy).then_inc(high, 1)

        @block.vector
        def _(dve):
            for n, (loads, stage, hi, lo) in enumerate(jobs):
                dve.wait_ge(high, n + 1)
                dve.tensor_tensor(lo, stage, hi, ALU.subtract)


def project1(nc, d, m):
    with ExitStack() as ctx:
        sb = lambda n, s, t=FP32: ctx.enter_context(nc.sbuf_tensor("p1_" + n, s, t))
        sem = lambda n: nc.alloc_semaphore("p1_" + n)
        sems = lambda n: [sem(f"{n}{b}") for b in range(2)]
        w_st = sb("w_st", [P, KT, 3 * C])
        w_hi, w_lo = sb("w_hi", [P, KT, 3 * C], F32R), sb("w_lo", [P, KT, 3 * C], F32R)
        split_weights(nc, "p1_w", [([(d["wT"].rearrange("(k p) n -> p k n", p=P), w_st[:, :, :])], w_st[:, :, :], w_hi[:, :, :], w_lo[:, :, :])])
        x = sb("x", [P, B, NTILE, C])
        h = sb("h", [P, B, NTILE, C])
        u = sb("u", [P, B, NTILE, C])
        stats, mv = sb("stats", [P, B, NTILE, 6]), sb("mv", [P, B, NTILE, 2])
        sd, rstd = sb("sd", [P, B, NTILE]), sb("rstd", [P, B, NTILE])
        hT_hi, hT_lo = sb("hT_hi", [P, B, KT, GT], F32R), sb("hT_lo", [P, B, KT, GT], F32R)
        qk_hi, qk_lo = sb("qk_hi", [P, 2, GT], F32R), sb("qk_lo", [P, 2, GT], F32R)
        pT = ctx.enter_context(nc.psum_tensor("p1_pT", [P, KT, GT], FP32))
        pQK = ctx.enter_context(nc.psum_tensor("p1_pQK", [P, 2, GT], FP32))
        pV = ctx.enter_context(nc.psum_tensor("p1_pV", [P, 2, 2, C], FP32))
        x_loaded, var_ready, sd_ready, h_ready, u_ready, u_stored = (
            sems(n) for n in ("x_loaded", "var_ready", "sd_ready", "h_ready", "u_ready", "u_stored"))
        hT_used = sems("hT_used")
        t_psum, hi_ready, lo_ready = sem("t_psum"), sem("hi_ready"), sem("lo_ready")
        qk_psum, qk_hi_ready, qk_lo_ready, qk_stored = (sems(n) for n in ("qk_psum", "qk_hi_ready", "qk_lo_ready", "qk_stored"))
        v_psum, v_read = sems("v_psum"), sems("v_read")
        stats_ready, norm_ready, ga_h, passed = sem("stats_ready"), sem("norm_ready"), sem("ga_h"), sem("passed")
        block = ctx.enter_context(nc.Block())
        x_v = d["x"].rearrange("b (i t p) c -> b i p t c", t=NTILE, p=P)
        u_v = d["u1"].rearrange("b (i t p) c -> b i p t c", t=NTILE, p=P)
        use = lambda i, b, n: 4 * i + 2 * b + n // 2

        @block.sync
        def _(sp):
            with sp.Fori(0, NGRP) as i:
                for b in range(B):
                    sp.wait_ge(u_ready[b], i)
                    sp.dma_start(x[:, b], x_v[b, bass.ds(i, 1)].rearrange("a p t c -> (a p) t c")).then_inc(x_loaded[b], 16)
                for b in range(B):
                    for n in range(4):
                        r = n % 2
                        sp.wait_ge(qk_lo_ready[r], use(i, b, n) + 1)
                        row = b * C + P * r
                        for s, half in enumerate((qk_hi, qk_lo)):
                            sp.dma_start(d["qk1"][n // 2, s, row:row + P, bass.ds(i * GT, GT)],
                                         half[:, r, :].bitcast(FP32)).then_inc(qk_stored[r], 16)
                    sp.wait_ge(u_ready[b], i + 1)
                    sp.dma_start(u_v[b, bass.ds(i, 1)].rearrange("a p t c -> (a p) t c"), u[:, b]).then_inc(u_stored[b], 16)
            for b in range(B):
                sp.wait_ge(u_stored[b], 16 * NGRP)
                sp.wait_ge(qk_stored[b], 16 * 2 * 4 * NGRP)

        @block.gpsimd
        def _(pool):
            with pool.Fori(0, NGRP) as i:
                for b in range(B):
                    ga = m.mod[:, b, 2, :].unsqueeze(1).broadcast_to([P, NTILE, C])
                    pool.wait_ge(h_ready[b], i + 1)
                    pool.wait_ge(u_stored[b], 16 * i)
                    pool.tensor_tensor(u[:, b], h[:, b], ga, ALU.mult).then_inc(ga_h, 1)
                    pool.wait_ge(ga_h, 2 * i + b + 1)
                    pool.tensor_tensor(u[:, b], u[:, b], x[:, b], ALU.add).then_inc(u_ready[b], 1)

        @block.scalar
        def _(act):
            with act.Fori(0, NGRP) as i:
                for b in range(B):
                    act.wait_ge(var_ready[b], i + 1)
                    act.activation(sd[:, b], mv[:, b, :, 1], ACT.Sqrt).then_inc(sd_ready[b], 1)
                for b in range(B):
                    act.wait_ge(hT_used[b], i)
                    for k in range(KT):
                        act.wait_ge(t_psum, 4 * i + 2 * b + k + 1)
                        act.activation(hT_hi[:, b, k, :], pT[:, k, :], ACT.Copy).then_inc(hi_ready, 1)
                    for n in range(4):
                        r = n % 2
                        act.wait_ge(qk_psum[r], use(i, b, n) + 1)
                        act.wait_ge(qk_stored[r], 32 * use(i, b, n))
                        act.activation(qk_hi[:, r, :], pQK[:, r, :], ACT.Identity, bias=m.bqk[:, n:n + 1]).then_inc(qk_hi_ready[r], 1)

        @block.vector
        def _(dve):
            with dve.Fori(0, NGRP) as i:
                for b in range(B):
                    dve.wait_ge(x_loaded[b], 16 * (i + 1))
                    for t in range(NTILE):
                        last = dve.bn_stats(stats[:, b, t, :], x[:, b, t, :])
                    last.then_inc(stats_ready, 1)
                    dve.wait_ge(stats_ready, 6 * i + 3 * b + 1)
                    dve.sem_inc(passed, 1)
                    for t in range(NTILE):
                        last = dve.bn_aggr(mv[:, b, t, :], stats[:, b, t, :])
                    last.then_inc(stats_ready, 1)
                    dve.wait_ge(stats_ready, 6 * i + 3 * b + 2)
                    dve.tensor_scalar(mv[:, b, :, 1], mv[:, b, :, 1], EPS, None, ALU.add).then_inc(var_ready[b], 1)
                    dve.wait_ge(sd_ready[b], i + 1)
                    dve.reciprocal(rstd[:, b], sd[:, b]).then_inc(stats_ready, 1)
                    dve.wait_ge(stats_ready, 6 * i + 3 * b + 3)
                    dve.wait_ge(u_ready[b], i)
                    for t in range(NTILE):
                        last = dve.tensor_scalar(h[:, b, t, :], x[:, b, t, :], mv[:, b, t, 0:1], rstd[:, b, t:t + 1],
                                                 ALU.subtract, ALU.mult)
                    last.then_inc(norm_ready, 1)
                    dve.wait_ge(norm_ready, 4 * i + 2 * b + 1)
                    dve.tensor_tensor(h[:, b], h[:, b], m.mod[:, b, 1, :].unsqueeze(1).broadcast_to([P, NTILE, C]),
                                      ALU.mult).then_inc(norm_ready, 1)
                    dve.wait_ge(norm_ready, 4 * i + 2 * b + 2)
                    dve.tensor_tensor(h[:, b], h[:, b], m.mod[:, b, 0, :].unsqueeze(1).broadcast_to([P, NTILE, C]),
                                      ALU.add).then_inc(h_ready[b], 1)
                for b in range(B):
                    for k in range(KT):
                        dve.wait_ge(hi_ready, 4 * i + 2 * b + k + 1)
                        dve.tensor_tensor(hT_lo[:, b, k, :], pT[:, k, :], hT_hi[:, b, k, :], ALU.subtract).then_inc(lo_ready, 1)
                    for n in range(4):
                        r = n % 2
                        dve.wait_ge(qk_hi_ready[r], use(i, b, n) + 1)
                        dve.scalar_tensor_tensor(out=qk_lo[:, r, :], in0=pQK[:, r, :], scalar=m.bqk[:, n:n + 1],
                                                 in1=qk_hi[:, r, :], op0=ALU.add, op1=ALU.subtract).then_inc(qk_lo_ready[r], 1)
                    for half in range(2):
                        dve.wait_ge(v_psum[half], 2 * i + b + 1)
                        dst = m.v1[:, 4 * b:4 * b + 4, bass.ds(i * NTILE + 2 * half, 2), :].rearrange("p g t f -> p t g f")
                        dve.tensor_tensor(dst, pV[:, half].rearrange("p t (g f) -> p t g f", g=4),
                                          m.bv[:, :].rearrange("p (g f) -> p g f", g=4).unsqueeze(1).broadcast_to([P, 2, 4, C // 4]),
                                          ALU.add).then_inc(v_read[half], 1)

        @block.tensor
        def _(pe):
            with pe.Fori(0, NGRP) as i:
                for b in range(B):
                    pe.wait_ge(h_ready[b], i + 1)
                    pe.wait_ge(lo_ready, 4 * i + 2 * b)
                    for k in range(KT):
                        for t in range(NTILE):
                            mm = pe.transpose(pT[:, k, P * t:P * t + P], h[:, b, t, P * k:P * k + P], m.eye[:, :])
                        mm.then_inc(t_psum, 1)
                    pe.wait_ge(lo_ready, 4 * i + 2 * b + 2)
                    for n in range(4):
                        r = n % 2
                        pe.wait_ge(qk_lo_ready[r], use(i, b, n))
                        for k in range(KT):
                            mm = product3(pe, pQK[:, r, :], w_hi[:, k, P * n:P * n + P], w_lo[:, k, P * n:P * n + P],
                                          hT_hi[:, b, k, :], hT_lo[:, b, k, :], k == 0, k == KT - 1)
                        mm.then_inc(qk_psum[r], 1)
                    for half in range(2):
                        pe.wait_ge(v_read[half], 2 * i + b)
                        for t in range(2):
                            at = P * (2 * half + t)
                            for k in range(KT):
                                mm = product3(pe, pV[:, half, t, :], hT_hi[:, b, k, at:at + P], hT_lo[:, b, k, at:at + P],
                                              w_hi[:, k, 2 * C:3 * C], w_lo[:, k, 2 * C:3 * C], k == 0, k == KT - 1)
                        mm.then_inc(v_psum[half], 1)
                    pe.wait_ge(v_psum[1], 2 * i + b + 1)
                    pe.sem_inc(hT_used[b], 1)


def attention(nc, d, m, second):
    with ExitStack() as ctx:
        name = "a2_" if second else "a1_"
        sb = lambda n, s, t=FP32: ctx.enter_context(nc.sbuf_tensor(name + n, s, t))
        sem = lambda n: nc.alloc_semaphore(name + n)
        KH = 1 if second else HG
        SCALE = HD2 ** -0.5 if second else 1.0
        NS, NR = 3, 3 if second else 4
        STACKS = 2 if second else 1
        q = [sb(f"q{n}", [P, NGRP, HG, GT], F32R) for n in range(STACKS)]
        kmax = sb("kmax", [P, KH, T], F32R)
        kmax_first = sb("kmax_first", [P, KH, GT], F32R)
        key = [sb(f"key{n}", [P, KH, T], F32R) for n in range(STACKS)]
        MAX_ROWS = P if second else 96
        rows_exp = [P] * (STACKS - 1) + [98]
        prob = sb("prob", [P, 4, HG, GT])
        val = sb("val", [P, T // P, KH, 32])
        rowmax = sb("rowmax", [P, 2, HG, NTILE, NGRP])
        fullmax = sb("fullmax", [P, HG * NTILE])
        neg_hi, neg_lo = sb("neg_hi", [HG * NTILE, P], F32R), sb("neg_lo", [HG * NTILE, P], F32R)
        pR = ctx.enter_context(nc.psum_tensor(name + "pR", [P, NR, GT], FP32))
        pS = ctx.enter_context(nc.psum_tensor(name + "pS", [P, NS, GT], FP32))
        pO = ctx.enter_context(nc.psum_tensor(name + "pO", [P, GT], FP32))
        if second:
            ones = sb("ones", [P, 32])
            out, recip = sb("out", [P, 2, GT]), sb("recip", [P, GT])
            zsum = sb("zsum", [P, HG, GT])
            pZ = ctx.enter_context(nc.psum_tensor(name + "pZ", [P, GT], FP32))
        else:
            out, recip = sb("out", [P, 2, NTILE, HG, HD1]), sb("recip", [P, NTILE, HG])
        oT = sb("oT", [P, GT])

        filled = sem("filled")
        dve_passed, sp_passed = sem("dve_passed"), sem("sp_passed")
        q_loaded, kmax_loaded, key_loaded = ([sem(f"{n}{c}") for c in range(NGRP)] for n in ("q_loaded", "kmax_loaded", "key_loaded"))
        first_loaded = [sem("first_loaded")]
        val_ready = sem("val_ready")
        r_psum, r_read = sem("r_psum"), sem("r_read")
        fullmax_ready, neg_hi_ready, neg_ready, neg_stored = sem("fullmax_ready"), sem("neg_hi_ready"), sem("neg_ready"), sem("neg_stored")
        s_psum, exp_ready, pv_done = sem("s_psum"), sem("exp_ready"), sem("pv_done")
        z_added, z_psum = sem("z_added"), sem("z_psum")
        o_copied, recip_ready, out_ready = sem("o_copied"), sem("recip_ready"), sem("out_ready")
        out_stored = [sem(f"out_stored{c}") for c in range(2)]
        block = ctx.enter_context(nc.Block())

        s_bank = lambda c, kt, h: (HG * (upto(c) + kt) + h) % NS

        def bank_before(c, kt, h):
            at = HG * (upto(c) + kt) + h
            return at - NS if at >= NS else max(n for n in range(HG * STEPS) if n % NS == at % NS) - HG * STEPS

        upto = lambda c: 2 * c * (c + 1)
        STEPS = upto(NGRP)
        FILLS = 4 if second else 7
        QL = 16 * (6 if second else 4)
        KL = 16 * (3 if second else 4)
        KML = 16 * (2 if second else 4)
        EXP_CREDIT, PV_CREDIT, R_CREDIT = HG, 4, NR
        by_pool = lambda c, kt: c > 0 and kt % 4 != 3
        pool_adds = [by_pool(c, kt) and kt > 0 for c in range(NGRP) for kt in range(4 * c + 4)]
        ADDS = sum(pool_adds)

        def adds_before(at):
            return sum(pool_adds[:at]) if at >= 0 else -sum(pool_adds[at:])

        score_step = lambda g, c, kt: STEPS * g + upto(c) + kt
        first_query = lambda c, kt: max(0, P * (kt - 4 * c))

        def rows(c, tiles=range(NTILE)):
            return [("R", c, h, t, kc) for t in tiles for h in range(HG) for kc in range(c + 1)]

        def chain_up(*parts):
            side, late = [], []
            for part in parts:
                side += part[:3] + late + part[3:]
                c, h, t, kc = part[-1][1:]
                late = []
                if t == NTILE - 1:
                    side.append(("F", c))
                    late = [("M", c)]
            return side + late

        def order(side, scores, deferred=False):
            main = []
            for c in range(NGRP) if scores else ():
                for kt in range(4 * c + 4):
                    main += [[("S", c, kt, h)] for h in range(HG)]
                    if c or kt:
                        main[-1].append(("V", c, kt - 1) if kt else ("V", c - 1, 4 * c - 1))
                    if c and kt == 0:
                        main[-1].append(("E", c - 1))
            if scores:
                main.append([("V", NGRP - 1, 4 * NGRP - 1), ("E", NGRP - 1)])
                for c in range(0 if deferred else 1, NGRP):
                    at = HG * upto(c)
                    if not second:
                        main[at + 2 * HG].append(("O", c - 1))
                        continue
                    main[at + (HG + 3 if c else 0)].append(("Z", c - 1))
                    for n in range(NTILE):
                        main[at + (2 * HG + 2 * n if c else 1 + n)].append(("N", c - 1, n))
            cost = {"R": 612, "N": 1090, "O": 600, "M": 400, "F": 200}
            price = lambda x: 100 + P * (x[3] + 1) if x[0] == "R" and x[4] == x[1] else cost.get(x[0], 0)
            weights = [sum(GT - first_query(*x[1:3]) for x in items if x[0] == "S") for items in main]
            whole = sum(map(price, side)) + sum(price(x) for items in main for x in items)
            result, side, paid = [], list(side), 0
            for n, items in enumerate(main):
                result += items
                paid += sum(map(price, items))
                while side and paid + price(side[0]) <= whole * sum(weights[:n + 1]) / max(1, sum(weights)) + 1:
                    paid += price(side[0])
                    result.append(side.pop(0))
            return result + side

        first = order(chain_up(rows(0), rows(1), rows(2, (0, 1, 2))), False)
        side = chain_up(rows(2, (3,)), rows(3), rows(0), rows(1), rows(2, (0, 1, 2)))
        body0, body = order(side, True), order(side, True, True)
        of_next = lambda x: x[0] in "RFM" and (x[1] < 2 or x[0] == "R" and x[1] == 2 and x[3] < 3)
        final = [x for x in body if not of_next(x)]
        final += [("Z", NGRP - 1)] + [("N", NGRP - 1, n) for n in range(NTILE)] if second else [("O", NGRP - 1)]
        bank_uses = lambda items: sum(x[0] in "RMOK" for x in items)
        body = [("K",)] * (-bank_uses(body) % NR) + body
        R_FIRST, R_BODY = bank_uses(first), bank_uses(body)
        R_LOOP = R_FIRST + bank_uses(body0)
        bank_at_start = {id(first): 0, id(body0): R_FIRST % NR, id(body): R_LOOP % NR, id(final): R_LOOP % NR}

        def run(eng, work):
            work(first, -1, 0)
            work(body0, 0, R_FIRST)
            with eng.Fori(0, NG - 2) as k:
                work(body, k + 1, R_LOOP + k * R_BODY)
            work(final, NG - 1, R_LOOP + (NG - 2) * R_BODY)

        def max_count(items, g, c):
            return c if items is first else 4 * g + (c if c >= 2 else 4 + c)

        @block.sync
        def _(sp):
            def load_q(c, g):
                cols = slice(c * GT, (c + 1) * GT)
                if second:
                    for s in range(2):
                        for k in range(2):
                            v = d["q2"][bass.ds(g, 1), s, k, :, cols].rearrange("a (h r) t -> r (a h) t", h=HG)
                            at = 64 * s + 32 * k
                            sp.dma_start(q[0][at:at + 32, c].bitcast(FP32), v).then_inc(q_loaded[c], 16)
                            if s == 0:
                                sp.dma_start(q[1][at:at + 32, c].bitcast(FP32), v).then_inc(q_loaded[c], 16)
                else:
                    for n, s in enumerate((0, 0, 1, 1)):
                        v = d["qk1"][0, s, bass.ds(64 * g, 64), cols].rearrange("(h f) t -> f h t", h=HG)
                        sp.dma_start(q[0][16 * n:16 * n + 16, c].bitcast(FP32), v).then_inc(q_loaded[c], 16)

            def load_kmax(c, g, tile=kmax, signal=kmax_loaded):
                cols = slice(c * GT, (c + 1) * GT)
                if second:
                    sp.sem_inc(sp_passed, 1)
                    for n in range(2):
                        v = d["k2"][bass.ds(g // 4, 1), 0, :, cols].rearrange("a f t -> (a f) t")
                        sp.dma_start(tile[64 * n:64 * n + 64, 0, cols].bitcast(FP32), v).then_inc(signal[c], 16)
                else:
                    for n, s in enumerate((0, 1, 0, 1)):
                        v = d["qk1"][1, s, bass.ds(64 * g, 64), cols].rearrange("(h f) t -> f h t", h=HG)
                        sp.dma_start(tile[16 * n:16 * n + 16, :, cols].bitcast(FP32), v).then_inc(signal[c], 16)

            def load_k(c, g):
                cols = slice(c * GT, (c + 1) * GT)
                if second:
                    sp.sem_inc(sp_passed, 1)
                    for n, at, s in ((0, 0, 0), (0, 64, 0), (1, 0, 1)):
                        v = d["k2"][bass.ds(g // 4, 1), s, :, cols].rearrange("a f t -> (a f) t")
                        sp.dma_start(key[n][at:at + 64, 0, cols].bitcast(FP32), v).then_inc(key_loaded[c], 16)
                else:
                    for n, s in enumerate((0, 1, 0, 1)):
                        v = d["qk1"][1, s, bass.ds(64 * g, 64), cols].rearrange("(h f) t -> f h t", h=HG)
                        sp.dma_start(key[0][16 * n:16 * n + 16, :, cols].bitcast(FP32), v).then_inc(key_loaded[c], 16)

            def store_max(c, count):
                sp.wait_ge(neg_ready, count + 1)
                for row, half in ((96, neg_hi), (97, neg_lo)):
                    sp.dma_start(q[-1][row:row + 1, c].bitcast(FP32), half[:, :].bitcast(FP32)).then_inc(neg_stored, 16)

            def store_out(c, g):
                sp.wait_ge(out_ready, 4 * g + c + 1)
                cols = slice(c % NGRP * GT, (c % NGRP + 1) * GT)
                if second:
                    dst = d["o2"][bass.ds(g + min(c, 0), 1), :, cols].rearrange("a p t -> (a p) t")
                    sp.dma_start(dst, out[:, c % 2, :]).then_inc(out_stored[c % 2], 16)
                else:
                    dst = d["o1"][bass.ds(g + min(c, 0), 1), cols].rearrange("a (t p) f -> p (a t) f", p=P)
                    sp.dma_start(dst, out[:, c % 2].rearrange("p t h f -> p t (h f)")).then_inc(out_stored[c % 2], 16)

            sp.wait_ge(filled, FILLS)
            load_kmax(0, 0, kmax_first, first_loaded)
            for c in range(3):
                load_q(c, 0)
                load_kmax(c, 0)
            load_kmax(3, 0)
            for c in range(NGRP):
                load_k(c, 0)
            for c in range(2):
                store_max(c, c)

            def step(g, has_before, has_next):
                sp.wait_ge(s_psum, HG * STEPS * g)
                load_q(3, g)
                store_max(2, 4 * g + 2)
                if has_before:
                    load_k(3, g)
                    store_out(-1, g)
                if has_next:
                    sp.wait_ge(s_psum, HG * (STEPS * g + upto(1)))
                    load_q(0, g + 1)
                    load_kmax(0, g + 1, kmax_first, first_loaded)
                store_out(0, g)
                if has_next:
                    sp.wait_ge(s_psum, HG * (STEPS * g + upto(2)))
                    load_q(1, g + 1)
                store_out(1, g)
                store_max(3, 4 * g + 3)
                if has_next:
                    for c in range(NGRP):
                        load_kmax(c, g + 1)
                    sp.wait_ge(s_psum, HG * (STEPS * g + upto(3)))
                    load_q(2, g + 1)
                store_out(2, g)
                if has_next:
                    for c in range(3):
                        sp.wait_ge(s_psum, HG * (STEPS * g + upto(3) + 4 * c + 4))
                        load_k(c, g + 1)
                        if c < 2:
                            store_max(c, 4 * g + 4 + c)

            step(0, False, True)
            with sp.Fori(0, NG - 2) as k:
                step(k + 1, True, True)
            step(NG - 1, True, False)
            store_out(NGRP - 1, NG - 1)
            for r in range(2):
                sp.wait_ge(out_stored[r], 16 * 2 * NG)

        @block.gpsimd
        def _(pool):
            fills = [(t[64:P].bitcast(FP32), 0.0) for t in ((q[1], key[1]) if second else (q[0], kmax, kmax_first, key[0]))]
            fills += [(ones[:, :], 1.0)] if second else [(val[:, :, :, 16:32], 0.0), (val[:, :, :, 16:17], 1.0)]
            fills += [(key[-1][96:98].bitcast(FP32), 1.0)]
            for n, (place, value) in enumerate(fills):
                if n:
                    pool.wait_ge(filled, n)
                pool.memset(place, value).then_inc(filled, 1)
            pool.wait_ge(filled, FILLS)

            def values(c, g):
                if second:
                    src = m.lat[:, bass.ds((g // 4) * (T // P) + 4 * c, 4), :]
                    pool.tensor_copy(val[:, 4 * c:4 * c + 4, 0, :], src).then_inc(val_ready, 1)
                else:
                    src = m.v1[:, bass.ds(g, 1), 4 * c:4 * c + 4, :].rearrange("p a t (h f) -> p (a t) h f", h=HG)
                    pool.tensor_copy(val[:, 4 * c:4 * c + 4, :, 0:16], src).then_inc(val_ready, 1)

            if second:
                pool.sem_inc(z_added, EXP_CREDIT)

            def work(items, g, r):
                for item in items:
                    if item[0] == "V" and second and by_pool(*item[1:]) and item[2] > 0:
                        _, c, kt = item
                        n = score_step(g, c, kt)
                        at = first_query(c, kt)
                        pool.wait_ge(exp_ready, EXP_CREDIT + HG * n + HG)
                        before = EXP_CREDIT + ADDS * g + adds_before(upto(c) + kt)
                        if kt == 1:
                            pool.wait_ge(z_psum, 4 * g + c)
                            pool.tensor_tensor(zsum[:, :, :], prob[:, 0, :, :], prob[:, 1, :, :], ALU.add).then_inc(z_added, 1)
                        else:
                            pool.wait_ge(z_added, before)
                            pool.tensor_tensor(zsum[:, :, at:GT], zsum[:, :, at:GT], prob[:, kt % 4, :, at:GT], ALU.add).then_inc(z_added, 1)
                    if item[0] == "V" and item[1] == 3 and item[2] % 4 == 3 and items is not final:
                        pool.wait_ge(pv_done, PV_CREDIT + score_step(g, 3, item[2]) + 1)
                        values(item[2] // 4, g + 1)

            for c in range(NGRP):
                values(c, 0)
            run(pool, work)

        @block.scalar
        def _(act):
            act.sem_inc(exp_ready, EXP_CREDIT)

            def work(items, g, r):
                for item in items:
                    if item[0] == "S":
                        _, c, kt, h = item
                        n = score_step(g, c, kt)
                        at = first_query(c, kt)
                        if h == 0:
                            act.wait_ge(pv_done, n + 1)
                            if second:
                                done = upto(c) + kt - (2 if c and kt == 4 else 3)
                                act.wait_ge(z_added, EXP_CREDIT + ADDS * g + adds_before(done))
                        act.wait_ge(s_psum, HG * n + h + 1)
                        act.activation(prob[:, kt % 4, h, at:GT], pS[:, s_bank(c, kt, h), at:GT], ACT.Exp, scale=SCALE).then_inc(exp_ready, 1)
                    if item[0] == "E":
                        c = item[1]
                        act.wait_ge(pv_done, PV_CREDIT + score_step(g, c, 4 * c + 4))
                        act.wait_ge(out_ready, 4 * g + c)
                        act.activation(oT[:, :], pO[:, :], ACT.Copy).then_inc(o_copied, 1)
            run(act, work)

        @block.vector
        def _(dve):
            dve.sem_inc(r_read, R_CREDIT)

            def work(items, g, r0):
                bank0 = bank_at_start[id(items)]
                used = 0
                for item in items:
                    r, bank = r0 + used, (bank0 + used) % NR
                    if item[0] == "R":
                        _, c, h, t, kc = item
                        used += 1
                        dve.wait_ge(r_psum, r + 1)
                        if kc < c:
                            dve.tensor_reduce(rowmax[:, c % 2, h, t, kc:kc + 1], pR[:, bank, :], axis=AX.X, op=ALU.max).then_inc(r_read, 1)
                        else:
                            n = P * (t + 1)
                            dve.sem_inc(dve_passed, 1)
                            dve.tensor_tensor_reduce(out=pR[:, bank, 0:n], in0=pR[:, bank, 0:n], in1=m.causal[:, GT - n:GT],
                                                     scale=1.0, scalar=-3e38, op0=ALU.add, op1=ALU.max,
                                                     accum_out=rowmax[:, c % 2, h, t, kc:kc + 1]).then_inc(r_read, 1)
                    if item[0] == "K":
                        used += 1
                        dve.wait_ge(r_read, R_CREDIT + r)
                        dve.sem_inc(r_read, 1)
                    if item[0] == "F":
                        c = item[1]
                        dve.wait_ge(r_read, R_CREDIT + r)
                        dve.tensor_reduce(fullmax[:, :], rowmax[:, c % 2, :, :, 0:c + 1].rearrange("p h t k -> p (h t) k"),
                                          axis=AX.X, op=ALU.max).then_inc(fullmax_ready, 1)
                    if item[0] == "M":
                        used += 1
                        count = max_count(items, g, item[1])
                        dve.wait_ge(r_psum, r + 1)
                        dve.wait_ge(neg_stored, 32 * count)
                        dve.tensor_scalar(neg_hi[:, :], pR[0:HG * NTILE, bank, 0:P], -1.0, None, ALU.mult).then_inc(neg_hi_ready, 1)
                        dve.wait_ge(neg_hi_ready, count + 1)
                        dve.scalar_tensor_tensor(out=neg_lo[:, :], in0=pR[0:HG * NTILE, bank, 0:P], scalar=-1.0, in1=neg_hi[:, :],
                                                 op0=ALU.mult, op1=ALU.subtract).then_inc(neg_ready, 1)
                        dve.wait_ge(neg_ready, count + 1)
                        dve.sem_inc(r_read, 1)
                    if item[0] == "O":
                        c = item[1]
                        used += 1
                        n = 4 * g + c
                        dve.wait_ge(r_psum, r + 1)
                        o = pR[:, bank, :].rearrange("p (t h f) -> p t h f", t=NTILE, h=HG)
                        dve.reciprocal(recip[:, :, :], o[:, :, :, HD1]).then_inc(recip_ready, 1)
                        dve.wait_ge(recip_ready, n + 1)
                        dve.wait_ge(out_stored[c % 2], 16 * (2 * g + c // 2))
                        dve.tensor_tensor(out[:, c % 2], o[:, :, :, 0:HD1],
                                          recip[:, :, :].unsqueeze(3).broadcast_to([P, NTILE, HG, HD1]), ALU.mult).then_inc(out_ready, 1)
                        dve.wait_ge(out_ready, n + 1)
                        dve.sem_inc(r_read, 1)
                    if item[0] == "N":
                        _, c, n = item
                        piece = slice(P * n, P * n + P)
                        if n == 0:
                            dve.wait_ge(z_psum, 4 * g + c + 1)
                            dve.wait_ge(o_copied, 4 * g + c + 1)
                            dve.wait_ge(out_stored[c % 2], 16 * (2 * g + c // 2))
                        dve.reciprocal(recip[:, piece], pZ[:, piece]).then_inc(recip_ready, 1)
                        dve.wait_ge(recip_ready, 4 * (4 * g + c) + n + 1)
                        ins = dve.tensor_tensor(out[:, c % 2, piece], oT[:, piece], recip[:, piece], ALU.mult)
                        if n == NTILE - 1:
                            ins.then_inc(out_ready, 1)
            run(dve, work)

        @block.tensor
        def _(pe):
            pe.sem_inc(pv_done, PV_CREDIT)
            pe.wait_ge(filled, FILLS)

            def work(items, g, r0):
                bank0 = bank_at_start[id(items)]
                used = 0
                for item in items:
                    r, bank = r0 + used, (bank0 + used) % NR
                    if item[0] == "R":
                        _, c, h, t, kc = item
                        used += 1
                        step = g if c == 3 else g + 1
                        if h == 0 and t == 0:
                            if kc == 0:
                                pe.wait_ge(q_loaded[c], QL * (step + 1))
                            pe.wait_ge((kmax_loaded if c else first_loaded)[kc], KML * (step + 1))
                        pe.wait_ge(r_read, r + 1)
                        n = GT if kc < c else P * (t + 1)
                        pe.matmul(pR[:, bank, 0:n], q[0][0:MAX_ROWS, c, h, P * t:P * t + P],
                                  (kmax if c else kmax_first)[0:MAX_ROWS, h % KH, GT * kc:GT * kc + n], start=True, stop=True).then_inc(r_psum, 1)
                    if item[0] == "M":
                        used += 1
                        pe.wait_ge(r_read, r + 1)
                        pe.wait_ge(fullmax_ready, max_count(items, g, item[1]) + 1)
                        pe.transpose(pR[0:HG * NTILE, bank, 0:P], fullmax[:, :], m.eye[:, :]).then_inc(r_psum, 1)
                    if item[0] == "S":
                        _, c, kt, h = item
                        n = score_step(g, c, kt)
                        at = first_query(c, kt)
                        if kt == 0 and h == 0:
                            pe.wait_ge(neg_stored, 32 * (4 * g + 4 if c == 3 else 4 * g + c + 1))
                            pe.wait_ge(q_loaded[c], QL * (g + 1))
                        if kt >= 4 * c and kt % 4 == 0 and h == 0:
                            pe.wait_ge(key_loaded[kt // 4], KL * (g + 1))
                        diagonal = kt >= 4 * c
                        pe.wait_ge(exp_ready, EXP_CREDIT + HG * STEPS * g + bank_before(c, kt, h) + 1)
                        bank_s = s_bank(c, kt, h)
                        for s in range(STACKS):
                            mm = pe.matmul(pS[:, bank_s, at:GT], key[s][0:rows_exp[s], h % KH, P * kt:P * kt + P],
                                           q[s][0:rows_exp[s], c, h, at:GT], start=(s == 0), stop=(s == STACKS - 1 and not diagonal))
                        if diagonal:
                            mm = pe.matmul(pS[:, bank_s, at:at + P], m.after16[:, :], m.eye16[:, :], start=False, stop=True)
                        mm.then_inc(s_psum, 1)
                    if item[0] == "V":
                        _, c, kt = item
                        n = score_step(g, c, kt)
                        at = first_query(c, kt)
                        pe.wait_ge(exp_ready, EXP_CREDIT + HG * n + HG)
                        if kt >= 4 * c:
                            if kt % 4 == 0:
                                pe.wait_ge(val_ready, 4 * g + kt // 4 + 1)
                        if kt == 0:
                            pe.wait_ge(o_copied, 4 * g + c)
                        ends = kt == 4 * c + 3
                        for h in range(HG):
                            mm = pe.matmul(pO[32 * h:32 * h + 32, at:GT], val[:, kt, h % KH, :], prob[:, kt % 4, h, at:GT],
                                           start=(kt == 0), stop=ends)
                        if second and not by_pool(c, kt):
                            begins = kt == (3 if c else 0)
                            if begins:
                                pe.wait_ge(recip_ready, 4 * (4 * g + c))
                            for h in range(HG):
                                mm = pe.matmul(pZ[32 * h:32 * h + 32, at:GT], ones[:, :], prob[:, kt % 4, h, at:GT],
                                               start=begins, stop=(c == 0 and kt == 3))
                        mm.then_inc(pv_done, 1)
                    if item[0] == "Z":
                        c = item[1]
                        pe.wait_ge(z_added, EXP_CREDIT + ADDS * g + adds_before(upto(c + 1)))
                        if c == 0:
                            pe.wait_ge(pv_done, PV_CREDIT + score_step(g, 0, 4))
                            pe.sem_inc(z_psum, 1)
                            continue
                        for h in range(HG):
                            mm = pe.matmul(pZ[32 * h:32 * h + 32, :], ones[:, :], zsum[:, h, :], start=False, stop=True)
                        mm.then_inc(z_psum, 1)
                    if item[0] == "O":
                        used += 1
                        pe.wait_ge(r_read, r + 1)
                        pe.wait_ge(o_copied, 4 * g + item[1] + 1)
                        for t in range(NTILE):
                            mm = pe.transpose(pR[:, bank, P * t:P * t + P], oT[:, P * t:P * t + P], m.eye[:, :])
                        mm.then_inc(r_psum, 1)
                    if item[0] == "K":
                        used += 1
                        pe.wait_ge(r_psum, r)
                        pe.sem_inc(r_psum, 1)
            run(pe, work)


def project2(nc, d, m):
    with ExitStack() as ctx:
        sb = lambda n, s, t=FP32: ctx.enter_context(nc.sbuf_tensor("p2_" + n, s, t))
        sem = lambda n: nc.alloc_semaphore("p2_" + n)
        sems = lambda n: [sem(f"{n}{b}") for b in range(2)]
        G = HEADS // HG
        wq_hi, wq_lo = sb("wq_hi", [P, KT, 3, G, P], F32R), sb("wq_lo", [P, KT, 3, G, P], F32R)
        wk_hi, wk_lo = sb("wk_hi", [P, KT, 2, P], F32R), sb("wk_lo", [P, KT, 2, P], F32R)
        cos, sin = sb("cos", [P, 2, T]), sb("sin", [P, 2, T])
        with ExitStack() as inner:
            st = lambda n, s, t=FP32: inner.enter_context(nc.sbuf_tensor("p2_" + n, s, t))
            wr_st, wk_st = st("wr_st", [P, KT, 2, G, P]), st("wk_st", [P, KT, 2, P])
            wqn, kvb = st("wqn", [P, G, C]), st("kvb", [P, G, P])
            fold_weights(nc, "p2_fold", d, kvb,
                         [(wqn[:, :, :], d["wqnT"].rearrange("(g p) f -> p g f", p=P)), (cos[:, :, :], d["cos"]), (sin[:, :, :], d["sin"])],
                         [(wqn[:, g, P * k:P * k + P], kvb[:, g, :], wq_hi[:, k, 0, g, :], wq_lo[:, k, 0, g, :])
                          for g in range(G) for k in range(KT)])
            split_weights(nc, "p2_w", [
                ([(d["wqr"].rearrange("(k p) (s g n) -> p k s g n", p=P, s=2, g=G)[:, k], wr_st[:, k]) for k in range(KT)],
                 wr_st[:, :, :, :, :], wq_hi[:, :, 1:3], wq_lo[:, :, 1:3]),
                ([(d["wk"].rearrange("(k p) (s n) -> p k s n", p=P, s=2), wk_st[:, :, :, :])], wk_st[:, :, :, :], wk_hi[:, :, :, :], wk_lo[:, :, :, :])])
        u, o = sb("u", [P, B, NTILE, C]), sb("o", [P, B, NTILE, C])
        x1, xin = sb("x1", [P, B, NTILE, C]), sb("xin", [P, B, NTILE, C])
        xn = sb("xn", [P, B, NTILE, C])
        stats, mv = sb("stats", [P, B, NTILE, 6]), sb("mv", [P, B, NTILE, 2])
        ssq, sd, rstd = sb("ssq", [P, B, NTILE]), sb("sd", [P, B, NTILE]), sb("rstd", [P, B, NTILE])
        rsd, rrms = sb("rsd", [P, B, NTILE]), sb("rrms", [P, B, NTILE])
        squares = sb("squares", [P, NTILE, C])
        xT_hi, xT_lo = sb("xT_hi", [P, B, KT, GT], F32R), sb("xT_lo", [P, B, KT, GT], F32R)
        n_hi, n_lo = sb("n_hi", [P, 2, GT], F32R), sb("n_lo", [P, 2, GT], F32R)
        r_hi, r_lo = sb("r_hi", [P, 2, GT], F32R), sb("r_lo", [P, 2, GT], F32R)
        by_cos, by_sin, turned = sb("by_cos", [P, 2, GT]), sb("by_sin", [P, 2, GT]), sb("turned", [P, 2, GT])
        pT = ctx.enter_context(nc.psum_tensor("p2_pT", [P, KT, GT], FP32))
        pN = ctx.enter_context(nc.psum_tensor("p2_pN", [P, GT], FP32))
        pR = ctx.enter_context(nc.psum_tensor("p2_pR", [P, 2, 2, GT], FP32))
        pL = ctx.enter_context(nc.psum_tensor("p2_pL", [P, NTILE, LAT], FP32))
        loaded, stored = sems("loaded"), sems("stored")
        gated, x1_ready, var_ready, sd_ready, rstd_ready, unit_ready, scaled, xin_ready = (
            sem(n) for n in ("gated", "x1_ready", "var_ready", "sd_ready", "rstd_ready", "unit_ready", "scaled", "xin_ready"))
        ssq_ready, ms_ready, rms_ready, rrms_ready, xn_ready = (
            sem(n) for n in ("ssq_ready", "ms_ready", "rms_ready", "rrms_ready", "xn_ready"))
        t_psum, hi_ready, lo_ready = sem("t_psum"), sem("hi_ready"), sem("lo_ready")
        n_psum, n_hi_ready, n_lo_ready, n_stored = sem("n_psum"), sem("n_hi_ready"), sem("n_lo_ready"), sems("n_stored")
        r_psum, r_read, turned_ready = sem("r_psum"), sem("r_read"), sem("turned_ready")
        r_hi_ready, r_lo_ready, r_stored = sem("r_hi_ready"), sem("r_lo_ready"), sems("r_stored")
        l_psum, l_read = sem("l_psum"), sem("l_read")
        stats_ready, passed, sp_passed = sem("stats_ready"), sem("passed"), sem("sp_passed")
        block = ctx.enter_context(nc.Block())
        RING = 2
        tok = lambda name: d[name].rearrange("b (i t p) c -> b i p t c", t=NTILE, p=P)
        spread = lambda b, v: m.mod[:, b, v, :].unsqueeze(1).broadcast_to([P, NTILE, C])
        PIECES = G + 1

        def order(products, front):
            after = {0: "AB", 1: "CD", 2: "SM", 3: "T", 4: "L"}
            items = []
            for g in range(PIECES) if products else ():
                items += [("N", g)] * (g < G) + [("Q", g)] + [(x, 0) for x in (after[g] if front else "")]
            return items if products else [(x, 0) for x in "ABCDSMTL"]

        def run(eng, work):
            work(order(False, True), -1, 1, 0, 0)
            with eng.Fori(0, NGRP - 1) as i:
                for b in range(B):
                    work(order(True, True), i, b, i + b, 1 - b)
            work(order(True, True), NGRP - 1, 0, NGRP - 1, 1)
            work(order(True, False), NGRP - 1, 1, 0, 0)

        @block.sync
        def _(sp):
            def load(i, b):
                sp.dma_start(u[:, b], tok("u1")[b, bass.ds(i, 1)].rearrange("a p t c -> (a p) t c")).then_inc(loaded[b], 16)
                for g in range(G):
                    src = d["o1"][4 * b + g, bass.ds(i * GT, GT)].rearrange("(t p) f -> p t f", p=P)
                    sp.dma_start(o[:, b, :, 64 * g:64 * g + 64], src).then_inc(loaded[b], 16)

            def work(items, i, b, fi, fb):
                n, fn = 2 * i + b, 2 * fi + fb
                for step, g in items:
                    if step == "A":
                        if ("Q", 0) not in items:
                            load(0, 0)
                            load(0, 1)
                    if step == "D":
                        sp.wait_ge(xin_ready, fn + 1)
                        sp.dma_start(tok("xin")[fb, bass.ds(fi, 1)].rearrange("a p t c -> (a p) t c"), xin[:, fb]).then_inc(stored[fb], 16)
                        sp.dma_start(tok("x1")[fb, bass.ds(fi, 1)].rearrange("a p t c -> (a p) t c"), x1[:, fb]).then_inc(stored[fb], 16)
                    cols = bass.ds(i * GT, GT)
                    if step == "N":
                        sp.wait_ge(n_lo_ready, G * n + g + 1)
                        sp.sem_inc(sp_passed, 1)
                        for s, half in enumerate((n_hi, n_lo)):
                            sp.dma_start(d["q2"][4 * b + g, s, 0, :, cols], half[:, g % 2, :].bitcast(FP32)).then_inc(n_stored[g % 2], 16)
                    if step == "Q":
                        ring = (b + g) % 2
                        sp.wait_ge(r_lo_ready, PIECES * n + g + 1)
                        sp.sem_inc(sp_passed, 1)
                        for s, half in enumerate((r_hi, r_lo)):
                            dst, rows = (d["q2"][4 * b + g, s, 1, :, cols], P) if g < G else (d["k2"][b, s, :, cols], LAT + ROPE)
                            sp.dma_start(dst, half[0:rows, ring, :].bitcast(FP32)).then_inc(r_stored[ring], 16)

            work(order(False, True), -1, 1, 0, 0)
            with sp.Fori(0, NGRP - 1) as i:
                for b in range(B):
                    sp.wait_ge(x1_ready, 2 * i + b + 1)
                    sp.sem_inc(sp_passed, 1)
                    load(i + 1, b)
                    work(order(True, True), i, b, i + b, 1 - b)
            work(order(True, True), NGRP - 1, 0, NGRP - 1, 1)
            work(order(True, False), NGRP - 1, 1, 0, 0)
            for b in range(B):
                sp.wait_ge(stored[b], 32 * NGRP)
                sp.wait_ge(n_stored[b], 16 * G * B * NGRP)
                sp.wait_ge(r_stored[b], 16 * PIECES * B * NGRP)

        @block.gpsimd
        def _(pool):
            pool.sem_inc(turned_ready, RING)

            def work(items, i, b, fi, fb):
                n, fn = 2 * i + b, 2 * fi + fb
                for step, g in items:
                    if step == "A":
                        pool.wait_ge(loaded[fb], 16 * (G + 1) * (fi + 1))
                        pool.wait_ge(stored[fb], 32 * fi)
                        pool.tensor_tensor(x1[:, fb], o[:, fb], spread(fb, 2), ALU.mult).then_inc(gated, 1)
                        pool.wait_ge(gated, fn + 1)
                        pool.tensor_tensor(x1[:, fb], x1[:, fb], u[:, fb], ALU.add).then_inc(x1_ready, 1)
                    if step == "D":
                        pool.wait_ge(unit_ready, fn + 1)
                        pool.tensor_tensor(xin[:, fb], xin[:, fb], spread(fb, 4), ALU.mult).then_inc(scaled, 1)
                        pool.wait_ge(scaled, fn + 1)
                        pool.tensor_tensor(xin[:, fb], xin[:, fb], spread(fb, 3), ALU.add).then_inc(xin_ready, 1)
                    if step == "Q":
                        ring = (b + g) % 2
                        piece = PIECES * n + g
                        pool.wait_ge(r_read, RING + piece + 1)
                        pool.tensor_tensor(turned[:, ring, :], by_cos[:, ring, :], by_sin[:, ring, :], ALU.add).then_inc(turned_ready, 1)
            run(pool, work)

        @block.scalar
        def _(act):
            def work(items, i, b, fi, fb):
                n, fn = 2 * i + b, 2 * fi + fb
                for step, g in items:
                    if step == "B":
                        act.wait_ge(var_ready, fn + 1)
                        act.activation(sd[:, fb], mv[:, fb, :, 1], ACT.Sqrt).then_inc(sd_ready, 1)
                    if step == "S":
                        act.wait_ge(xin_ready, fn + 1)
                        for t in range(NTILE):
                            last = act.activation(squares[:, t, :], xin[:, fb, t, :], ACT.Square, accum_out=ssq[:, fb, t:t + 1])
                        last.then_inc(ssq_ready, 1)
                    if step == "M":
                        act.wait_ge(ms_ready, fn + 1)
                        act.activation(rsd[:, fb], ssq[:, fb], ACT.Sqrt).then_inc(rms_ready, 1)
                    if step == "T":
                        for k in range(KT):
                            act.wait_ge(t_psum, KT * fn + k + 1)
                            act.activation(xT_hi[:, fb, k, :], pT[:, k, :], ACT.Copy, scale=m.wln[:, 0, k:k + 1]).then_inc(hi_ready, 1)
                    if step == "N":
                        act.wait_ge(n_psum, G * n + g + 1)
                        act.wait_ge(n_stored[g % 2], 32 * (2 * n + g // 2))
                        act.activation(n_hi[:, g % 2, :], pN[:, :], ACT.Copy).then_inc(n_hi_ready, 1)
                    if step == "Q":
                        ring = (b + g) % 2
                        act.wait_ge(turned_ready, RING + PIECES * n + g + 1)
                        act.wait_ge(r_stored[ring], 32 * (PIECES * i + (PIECES * b + g) // 2))
                        act.activation(r_hi[:, ring, :], turned[:, ring, :], ACT.Copy).then_inc(r_hi_ready, 1)
            run(act, work)

        @block.vector
        def _(dve):
            dve.sem_inc(r_read, RING)

            def split_turned(n, b, g):
                ring = (b + g) % 2
                dve.wait_ge(r_hi_ready, PIECES * n + g + 1)
                dve.tensor_tensor(r_lo[:, ring, :], turned[:, ring, :], r_hi[:, ring, :], ALU.subtract).then_inc(r_lo_ready, 1)

            def work(items, i, b, fi, fb):
                n, fn = 2 * i + b, 2 * fi + fb
                for step, g in items:
                    if step == "B":
                        dve.wait_ge(x1_ready, fn + 1)
                        for t in range(NTILE):
                            last = dve.bn_stats(stats[:, fb, t, :], x1[:, fb, t, :])
                        last.then_inc(stats_ready, 1)
                        dve.wait_ge(stats_ready, 2 * fn + 1)
                        dve.sem_inc(passed, 1)
                        for t in range(NTILE):
                            last = dve.bn_aggr(mv[:, fb, t, :], stats[:, fb, t, :])
                        last.then_inc(stats_ready, 1)
                        dve.wait_ge(stats_ready, 2 * fn + 2)
                        dve.tensor_scalar(mv[:, fb, :, 1], mv[:, fb, :, 1], EPS, None, ALU.add).then_inc(var_ready, 1)
                    if step == "C":
                        dve.wait_ge(sd_ready, fn + 1)
                        dve.reciprocal(rstd[:, fb], sd[:, fb]).then_inc(rstd_ready, 1)
                        dve.wait_ge(rstd_ready, fn + 1)
                        dve.wait_ge(stored[fb], 32 * fi)
                        for t in range(NTILE):
                            last = dve.tensor_scalar(xin[:, fb, t, :], x1[:, fb, t, :], mv[:, fb, t, 0:1], rstd[:, fb, t:t + 1],
                                                     ALU.subtract, ALU.mult)
                        last.then_inc(unit_ready, 1)
                    if step == "M":
                        dve.wait_ge(ssq_ready, fn + 1)
                        dve.tensor_scalar(ssq[:, fb], ssq[:, fb], 1.0 / C, EPS, ALU.mult, ALU.add).then_inc(ms_ready, 1)
                        dve.wait_ge(rms_ready, fn + 1)
                        dve.reciprocal(rrms[:, fb], rsd[:, fb]).then_inc(rrms_ready, 1)
                        dve.wait_ge(rrms_ready, fn + 1)
                        for t in range(NTILE):
                            last = dve.tensor_scalar(xn[:, fb, t, :], xin[:, fb, t, :], rrms[:, fb, t:t + 1], None, ALU.mult)
                        last.then_inc(xn_ready, 1)
                    if step == "T":
                        for k in range(KT):
                            dve.wait_ge(hi_ready, KT * fn + k + 1)
                            dve.scalar_tensor_tensor(out=xT_lo[:, fb, k, :], in0=pT[:, k, :], scalar=m.wln[:, 0, k:k + 1],
                                                     in1=xT_hi[:, fb, k, :], op0=ALU.mult, op1=ALU.subtract).then_inc(lo_ready, 1)
                    if step == "L":
                        dve.wait_ge(l_psum, fn + 1)
                        dve.tensor_copy(m.lat[:, bass.ds(fi * NTILE + fb * (T // P), NTILE), :], pL[:, :, :]).then_inc(l_read, 1)
                    if step == "N":
                        dve.wait_ge(n_hi_ready, G * n + g + 1)
                        dve.tensor_tensor(n_lo[:, g % 2, :], pN[:, :], n_hi[:, g % 2, :], ALU.subtract).then_inc(n_lo_ready, 1)
                    if step == "Q":
                        ring, table = (b + g) % 2, g // G
                        piece = PIECES * n + g
                        cols = bass.ds(i * GT, GT)
                        dve.wait_ge(r_psum, piece + 1)
                        dve.wait_ge(turned_ready, piece + 1)
                        dve.tensor_tensor(by_cos[:, ring, :], pR[:, ring, 0, :], cos[:, table, cols], ALU.mult)
                        dve.tensor_tensor(by_sin[:, ring, :], pR[:, ring, 1, :], sin[:, table, cols], ALU.mult).then_inc(r_read, 1)
                        if g:
                            split_turned(n, b, g - 1)
                        if g == G:
                            split_turned(n, b, g)
            run(dve, work)

        @block.tensor
        def _(pe):
            def work(items, i, b, fi, fb):
                n, fn = 2 * i + b, 2 * fi + fb
                for step, g in items:
                    if step == "T":
                        pe.wait_ge(xn_ready, fn + 1)
                        pe.wait_ge(lo_ready, KT * fn)
                        for k in range(KT):
                            for t in range(NTILE):
                                mm = pe.transpose(pT[:, k, P * t:P * t + P], xn[:, fb, t, P * k:P * k + P], m.eye[:, :])
                            mm.then_inc(t_psum, 1)
                    if step == "L":
                        pe.wait_ge(lo_ready, KT * fn + KT)
                        pe.wait_ge(l_read, fn)
                        for t in range(NTILE):
                            at = slice(P * t, P * t + P)
                            for k in range(KT):
                                mm = product3(pe, pL[:, t, :], xT_hi[:, fb, k, at], xT_lo[:, fb, k, at],
                                              wk_hi[:, k, 0, 0:LAT], wk_lo[:, k, 0, 0:LAT], k == 0, k == KT - 1)
                        mm.then_inc(l_psum, 1)
                    if step == "N":
                        pe.wait_ge(n_lo_ready, G * n + g)
                        for k in range(KT):
                            mm = product3(pe, pN[:, :], wq_hi[:, k, 0, g, :], wq_lo[:, k, 0, g, :],
                                          xT_hi[:, b, k, :], xT_lo[:, b, k, :], k == 0, k == KT - 1)
                        mm.then_inc(n_psum, 1)
                    if step == "Q":
                        ring = (b + g) % 2
                        pe.wait_ge(r_read, PIECES * n + g + 1)
                        for s in range(2):
                            for k in range(KT):
                                hi, lo = ((wq_hi[:, k, 1 + s, g, :], wq_lo[:, k, 1 + s, g, :]) if g < G
                                          else (wk_hi[:, k, s, :], wk_lo[:, k, s, :]))
                                mm = product3(pe, pR[:, ring, s, :], hi, lo, xT_hi[:, b, k, :], xT_lo[:, b, k, :], k == 0, k == KT - 1)
                        mm.then_inc(r_psum, 1)
            run(pe, work)


def fold_weights(nc, name, d, kvb, loads, jobs):
    with ExitStack() as ctx:
        sem = lambda n: nc.alloc_semaphore(name + n)
        ps = ctx.enter_context(nc.psum_tensor(name + "_ps", [P, 2, GT], FP32))
        zeroed, loaded, product, high, low = (sem(n) for n in ("_zeroed", "_loaded", "_product", "_high", "_low"))
        block = ctx.enter_context(nc.Block())

        @block.gpsimd
        def _(pool):
            pool.memset(kvb[:, :, :], 0.0).then_inc(zeroed, 1)

        @block.sync
        def _(sp):
            sp.wait_ge(zeroed, 1)
            src = d["wkvbT"].rearrange("(g j n) r -> j n g r", j=HG, n=32)
            for j in range(HG):
                sp.dma_start(kvb[32 * j:32 * j + 32, :, 32 * j:32 * j + 32], src[j]).then_inc(loaded, 16)
            for dst, src in loads:
                sp.dma_start(dst, src).then_inc(loaded, 16)

        @block.tensor
        def _(pe):
            pe.wait_ge(loaded, 16 * (HG + len(loads)))
            for n, (left, right, hi, lo) in enumerate(jobs):
                if n >= 2:
                    pe.wait_ge(low, n - 1)
                pe.matmul(ps[:, n % 2, 0:right.shape[-1]], left, right, start=True, stop=True).then_inc(product, 1)

        @block.scalar
        def _(act):
            for n, (left, right, hi, lo) in enumerate(jobs):
                act.wait_ge(product, n + 1)
                act.activation(hi, ps[:, n % 2, 0:right.shape[-1]], ACT.Copy).then_inc(high, 1)

        @block.vector
        def _(dve):
            for n, (left, right, hi, lo) in enumerate(jobs):
                dve.wait_ge(high, n + 1)
                dve.tensor_tensor(lo, ps[:, n % 2, 0:right.shape[-1]], hi, ALU.subtract).then_inc(low, 1)


def experts(nc, d, m):
    with ExitStack() as ctx:
        sb = lambda n, s, t=FP32: ctx.enter_context(nc.sbuf_tensor("e_" + n, s, t))
        sem = lambda n: nc.alloc_semaphore("e_" + n)
        sems = lambda n: [sem(f"{n}{b}") for b in range(2)]
        G, EX = HEADS // HG, E + 1
        wo_hi, wo_lo = sb("wo_hi", [P, G, C], F32R), sb("wo_lo", [P, G, C], F32R)
        wg_hi, wg_lo = sb("wg_hi", [P, KT, EX, I], F32R), sb("wg_lo", [P, KT, EX, I], F32R)
        wu_hi, wu_lo = sb("wu_hi", [P, KT, EX, I], F32R), sb("wu_lo", [P, KT, EX, I], F32R)
        wd_hi, wd_lo = sb("wd_hi", [P, EX, C], F32R), sb("wd_lo", [P, EX, C], F32R)
        gate_hi, gate_lo = sb("gate_hi", [P, KT, E], F32R), sb("gate_lo", [P, KT, E], F32R)
        sel_st = sb("sel_st", [64, E, P])
        sel = sb("sel", [64, E, P], F32R)
        rank = sb("rank", [P, E])
        with ExitStack() as inner:
            st = lambda n, s, t=FP32: inner.enter_context(nc.sbuf_tensor("e_" + n, s, t))
            wo, kvb = st("wo", [P, G, C]), st("kvb", [P, G, P])
            fold_weights(nc, "e_fold", d, kvb,
                         [(wo[32 * j:32 * j + 32, :, :], d["Wo"].rearrange("(g j n) c -> j n g c", j=HG, n=HD2)[j, 0:32])
                          for j in range(HG)] + [(sel_st[:, :, :], d["sel"].rearrange("k (e p) -> k e p", e=E)),
                                                 (rank[:, :], d["rank"].rearrange("(a n) -> a n", a=1).broadcast_to([P, E]))],
                         [(kvb[:, g, :], wo[:, g, :], wo_hi[:, g, :], wo_lo[:, g, :]) for g in range(G)])
        with ExitStack() as inner:
            st = lambda n, s, t=FP32: inner.enter_context(nc.sbuf_tensor("e_" + n, s, t))
            g_st, u_st, d_st, gate_st = (st("g_st", [P, KT, EX, I]), st("u_st", [P, KT, EX, I]), st("d_st", [P, EX, C]),
                                         st("gate_st", [P, KT, E]))
            up = lambda name: d[name].rearrange("e (k p) n -> p k e n", p=P)
            split_weights(nc, "e_w", [
                ([(up("Wg")[:, k], g_st[:, k, 0:E]) for k in range(KT)] + [(up("sWg")[:, k], g_st[:, k, E:EX]) for k in range(KT)],
                 g_st[:, :, :, :], wg_hi[:, :, :, :], wg_lo[:, :, :, :]),
                ([(up("Wu")[:, k], u_st[:, k, 0:E]) for k in range(KT)] + [(up("sWu")[:, k], u_st[:, k, E:EX]) for k in range(KT)],
                 u_st[:, :, :, :], wu_hi[:, :, :, :], wu_lo[:, :, :, :]),
                ([(d["Wd"].rearrange("e p n -> p e n"), d_st[:, 0:E, :]), (d["sWd"].rearrange("e p n -> p e n"), d_st[:, E:EX, :])],
                 d_st[:, :, :], wd_hi[:, :, :], wd_lo[:, :, :]),
                ([(d["Wgate"].rearrange("(k p) n -> p k n", p=P), gate_st[:, :, :])],
                 gate_st[:, :, :], gate_hi[:, :, :], gate_lo[:, :, :])])
        o_st = sb("o_st", [P, G, GT])
        o_hi, o_lo = sb("o_hi", [P, G, GT], F32R), sb("o_lo", [P, G, GT], F32R)
        xin, x1, x2 = sb("xin", [P, B, NTILE, C]), sb("x1", [P, B, NTILE, C]), sb("x2", [P, B, NTILE, C])
        y = sb("y", [P, B, NTILE, C])
        xn, squares = sb("xn", [P, NTILE, C]), sb("squares", [P, NTILE, C])
        ssq, rms, rrms = sb("ssq", [P, NTILE]), sb("rms", [P, NTILE]), sb("rrms", [P, NTILE])
        xT_hi, xT_lo = sb("xT_hi", [P, B, KT, GT], F32R), sb("xT_lo", [P, B, KT, GT], F32R)
        logit, pick1, pick2 = sb("logit", [P, NTILE, E]), sb("pick1", [P, NTILE, E]), sb("pick2", [P, NTILE, E])
        top, best = sb("top", [P, 2, NTILE]), sb("best", [P, NTILE])
        gap, weight = sb("gap", [P, 2, NTILE]), sb("weight", [P, 2, NTILE])
        comb = sb("comb", [P, NTILE, E])
        combT = sb("combT", [64, B, GT], F32R)
        silu, prod = sb("silu", [P, 2, GT]), sb("prod", [P, 2, GT])
        p_hi, p_lo = sb("p_hi", [P, 2, GT], F32R), sb("p_lo", [P, 2, GT], F32R)
        pPair = ctx.enter_context(nc.psum_tensor("e_pPair", [P, 2, 2, GT], FP32))
        pD = ctx.enter_context(nc.psum_tensor("e_pD", [P, NTILE, C], FP32))
        pB = ctx.enter_context(nc.psum_tensor("e_pB", [P, GT], FP32))
        pG = ctx.enter_context(nc.psum_tensor("e_pG", [P, GT], FP32))

        filled, sel_ready, sp_passed = sem("filled"), sem("sel_ready"), sem("sp_passed")
        o_loaded, x_loaded, out_stored = sem("o_loaded"), sems("x_loaded"), sems("out_stored")
        o_hi_ready, o_lo_ready = sem("o_hi_ready"), sem("o_lo_ready")
        pair_psum, pair_read = sem("pair_psum"), sem("pair_read")
        x2_ready, ssq_ready, ms_ready, rms_ready, xn_ready = sem("x2_ready"), sem("ssq_ready"), sem("ms_ready"), sem("rms_ready"), sem("xn_ready")
        xT_hi_ready, xT_ready = sem("xT_hi_ready"), sem("xT_ready")
        g_psum, g_read, chain = sem("g_psum"), sem("g_read"), sem("chain")
        gap_ready, weight_ready, comb_ready, combT_hi_ready, combT_ready = (
            sem("gap_ready"), sem("weight_ready"), sem("comb_ready"), sem("combT_hi_ready"), sem("combT_ready"))
        b_psum, b_read = sem("b_psum"), sem("b_read")
        silu_ready, gated, prod_ready, p_hi_ready, p_lo_ready = (
            sem("silu_ready"), sem("gated"), sem("prod_ready"), sem("p_hi_ready"), sem("p_lo_ready"))
        down_done, y_sum, y_scaled, y_ready = sem("down_done"), sem("y_sum"), sem("y_scaled"), sem("y_ready")
        block = ctx.enter_context(nc.Block())
        RING = 2

        FRONT = ("P", "A", "N", "R", "X", "L", "W", "C")

        def order(experts_too, front):
            after = {1: "P", 2: "A", 3: "NR", 4: "X", 5: "L", 6: "W", 7: "C"}
            if not experts_too:
                return [(s, 0) for s in FRONT]
            items = []
            for j in range(EX):
                items.append(("G", j))
                if j < E:
                    items.append(("B", j))
                if j:
                    items.append(("D", j - 1))
                if front:
                    items += [(s, 0) for s in after.get(j, "")]
            return items + [("D", E), ("Y", 0)]

        PAIRS = EX + 2

        def run(eng, work):
            work(order(False, True), -1, 1, 0, 0, 0, 0)
            with eng.Fori(0, NGRP - 1) as i:
                for b in range(B):
                    work(order(True, True), i, b, i + b, 1 - b, 2 + PAIRS * (2 * i + b), b)
            i = NGRP - 1
            work(order(True, True), i, 0, i, 1, 2 + PAIRS * 2 * i, 0)
            work(order(True, False), i, 1, 0, 0, 2 + PAIRS * (2 * i + 1), 1)

        tok = lambda name, b, i: d[name].rearrange("b (i t p) c -> b i p t c", t=NTILE, p=P)[b, bass.ds(i, 1)].rearrange("a p t c -> (a p) t c")

        @block.sync
        def _(sp):
            def work(items, i, b, fi, fb, pair, parity):
                if ("P", 0) in items:
                    fn = 2 * fi + fb
                    sp.wait_ge(o_lo_ready, fn)
                    sp.dma_start(o_st[:, :, :], d["o2"][4 * fb:4 * fb + 4, :, bass.ds(fi * GT, GT)].rearrange("g p t -> p g t")).then_inc(o_loaded, 16)
                    if ("Y", 0) in items:
                        sp.wait_ge(y_ready, 2 * i + b)
                        sp.sem_inc(sp_passed, 1)
                    sp.dma_start(xin[:, fb], tok("xin", fb, fi)).then_inc(x_loaded[fb], 16)
                    sp.dma_start(x1[:, fb], tok("x1", fb, fi)).then_inc(x_loaded[fb], 16)
                if ("Y", 0) in items:
                    sp.wait_ge(y_ready, 2 * i + b + 1)
                    sp.sem_inc(sp_passed, 1)
                    sp.dma_start(tok("out", b, i), y[:, b]).then_inc(out_stored[b], 16)
            run(sp, work)
            for b in range(B):
                sp.wait_ge(out_stored[b], 16 * NGRP)

        @block.gpsimd
        def _(pool):
            pool.memset(combT[:, :, :].bitcast(FP32), 0.0).then_inc(filled, 1)
            pool.sem_inc(p_lo_ready, RING)

            def work(items, i, b, fi, fb, pair, parity):
                n, fn = 2 * i + b, 2 * fi + fb
                for step, j in items:
                    use, s = EX * n + j, (b + j) % 2
                    if step == "P":
                        pool.wait_ge(o_hi_ready, fn + 1)
                        pool.tensor_tensor(o_lo[:, :, :], o_st[:, :, :], o_hi[:, :, :], ALU.subtract).then_inc(o_lo_ready, 1)
                    if step == "B" or step == "G" and j == E:
                        pool.wait_ge(p_hi_ready, use + 1)
                        pool.wait_ge(down_done, use + 1)
                        pool.tensor_tensor(p_lo[:, s, :], prod[:, s, :], p_hi[:, s, :], ALU.subtract).then_inc(p_lo_ready, 1)
                    if step == "Y":
                        pool.wait_ge(y_sum, n + 1)
                        pool.tensor_tensor(y[:, b], y[:, b], m.mod[:, b, 5, :].unsqueeze(1).broadcast_to([P, NTILE, C]),
                                           ALU.mult).then_inc(y_scaled, 1)
                        pool.wait_ge(y_scaled, n + 1)
                        pool.tensor_tensor(y[:, b], y[:, b], x1[:, b], ALU.add).then_inc(y_ready, 1)
            run(pool, work)

        @block.scalar
        def _(act):
            act.activation(sel[:, :, :], sel_st[:, :, :], ACT.Copy).then_inc(sel_ready, 1)

            def work(items, i, b, fi, fb, pair, parity):
                n, fn = 2 * i + b, 2 * fi + fb
                used = 0
                for step, j in items:
                    use, s = EX * n + j, (b + j) % 2
                    if step == "P":
                        act.wait_ge(o_loaded, 16 * (fn + 1))
                        act.wait_ge(x2_ready, fn)
                        act.activation(o_hi[:, :, :], o_st[:, :, :], ACT.Copy).then_inc(o_hi_ready, 1)
                    if step == "N":
                        act.wait_ge(x2_ready, fn + 1)
                        for t in range(NTILE):
                            last = act.activation(squares[:, t, :], x2[:, fb, t, :], ACT.Square, accum_out=ssq[:, t:t + 1])
                        last.then_inc(ssq_ready, 1)
                    if step == "R":
                        act.wait_ge(ms_ready, fn + 1)
                        act.activation(rms[:, :], ssq[:, :], ACT.Sqrt).then_inc(rms_ready, 1)
                    if step == "X":
                        act.wait_ge(pair_psum, pair + used + 1)
                        for k in range(KT):
                            last = act.activation(xT_hi[:, fb, k, :], pPair[:, (parity + used) % 2, k, :], ACT.Copy, scale=m.wln[:, 1, k:k + 1])
                        last.then_inc(xT_hi_ready, 1)
                    if step == "W":
                        act.wait_ge(gap_ready, fn + 1)
                        act.activation(weight[:, :, :], gap[:, :, :], ACT.Sigmoid).then_inc(weight_ready, 1)
                    if step == "C":
                        act.wait_ge(g_psum, 2 * fn + 2)
                        act.activation(combT[0:E, fb, :], pG[0:E, :], ACT.Copy).then_inc(combT_hi_ready, 1)
                    if step == "G":
                        act.wait_ge(pair_psum, pair + used + 1)
                        act.wait_ge(prod_ready, use + 1)
                        act.activation(silu[:, s, :], pPair[:, (parity + used) % 2, 0, :], ACT.Silu).then_inc(silu_ready, 1)
                    if step == "B" or step == "G" and j == E:
                        act.wait_ge(prod_ready, RING + use + 1)
                        act.wait_ge(down_done, use + 1)
                        act.activation(p_hi[:, s, :], prod[:, s, :], ACT.Copy).then_inc(p_hi_ready, 1)
                    used += step in "GAX"
            run(act, work)

        @block.vector
        def _(dve):
            dve.sem_inc(prod_ready, RING)
            dve.sem_inc(pair_read, RING)
            dve.sem_inc(g_read, 1)
            dve.sem_inc(b_read, 1)
            LINKS = 11

            def work(items, i, b, fi, fb, pair, parity):
                n, fn = 2 * i + b, 2 * fi + fb
                used, links = 0, 0
                per_token = lambda t: t.unsqueeze(2).broadcast_to([P, NTILE, E])

                for step, j in items:
                    use, s = EX * n + j, (b + j) % 2
                    q = (parity + used) % 2
                    if step == "A":
                        dve.wait_ge(pair_psum, pair + used + 1)
                        dve.wait_ge(x_loaded[fb], 32 * (fi + 1))
                        dve.tensor_tensor(x2[:, fb], xin[:, fb], pPair[:, q, :, :].rearrange("p k (t c) -> p (k t) c", c=C),
                                          ALU.add).then_inc(x2_ready, 1)
                        dve.wait_ge(x2_ready, fn + 1)
                        dve.sem_inc(pair_read, 1)
                    if step == "R":
                        dve.wait_ge(ssq_ready, fn + 1)
                        dve.tensor_scalar(ssq[:, :], ssq[:, :], 1.0 / C, EPS, ALU.mult, ALU.add).then_inc(ms_ready, 1)
                        dve.wait_ge(rms_ready, fn + 1)
                        dve.reciprocal(rrms[:, :], rms[:, :]).then_inc(chain, 1)
                        dve.wait_ge(chain, LINKS * fn + 1)
                        for t in range(NTILE):
                            last = dve.tensor_scalar(xn[:, t, :], x2[:, fb, t, :], rrms[:, t:t + 1], None, ALU.mult)
                        last.then_inc(xn_ready, 1)
                    if step == "X":
                        dve.wait_ge(xT_hi_ready, fn + 1)
                        for k in range(KT):
                            last = dve.scalar_tensor_tensor(out=xT_lo[:, fb, k, :], in0=pPair[:, q, k, :], scalar=m.wln[:, 1, k:k + 1],
                                                            in1=xT_hi[:, fb, k, :], op0=ALU.mult, op1=ALU.subtract)
                        last.then_inc(xT_ready, 1)
                        dve.wait_ge(xT_ready, fn + 1)
                        dve.sem_inc(pair_read, 1)
                    if step == "L":
                        links = 1

                        def link(ins):
                            nonlocal links
                            links += 1
                            ins.then_inc(chain, 1)
                            dve.wait_ge(chain, LINKS * fn + links)

                        dve.wait_ge(g_psum, 2 * fn + 1)
                        dve.tensor_tensor(logit[:, :, :], pG[:, 0:NTILE * E].rearrange("p (t e) -> p t e", e=E),
                                          m.ebias[:, :].unsqueeze(1).broadcast_to([P, NTILE, E]), ALU.add).then_inc(g_read, 1)
                        dve.wait_ge(g_read, 1 + 2 * fn + 1)
                        for c, pick in enumerate((pick1, pick2)):
                            link(dve.tensor_reduce(top[:, c, :], logit[:, :, :], axis=AX.X, op=ALU.max))
                            link(dve.tensor_tensor(pick[:, :, :], logit[:, :, :], per_token(top[:, c, :]), ALU.is_equal))
                            link(dve.tensor_tensor(pick[:, :, :], pick[:, :, :], rank[:, :].unsqueeze(1).broadcast_to([P, NTILE, E]), ALU.mult))
                            link(dve.tensor_reduce(best[:, :], pick[:, :, :], axis=AX.X, op=ALU.max))
                            if c == 0:
                                link(dve.tensor_tensor(pick[:, :, :], pick[:, :, :], per_token(best[:, :]), ALU.is_equal))
                                link(dve.scalar_tensor_tensor(out=logit[:, :, :], in0=pick[:, :, :], scalar=NEG, in1=logit[:, :, :],
                                                              op0=ALU.mult, op1=ALU.add))
                            else:
                                dve.tensor_tensor(pick[:, :, :], pick[:, :, :], per_token(best[:, :]), ALU.is_equal)
                        dve.tensor_tensor(gap[:, 0, :], top[:, 0, :], top[:, 1, :], ALU.subtract)
                        dve.tensor_tensor(gap[:, 1, :], top[:, 1, :], top[:, 0, :], ALU.subtract).then_inc(gap_ready, 1)
                        assert links == LINKS
                    if step == "W":
                        dve.wait_ge(weight_ready, fn + 1)
                        dve.tensor_tensor(pick1[:, :, :], pick1[:, :, :], per_token(weight[:, 0, :]), ALU.mult)
                        dve.tensor_tensor(pick2[:, :, :], pick2[:, :, :], per_token(weight[:, 1, :]), ALU.mult).then_inc(comb_ready, 1)
                        dve.wait_ge(comb_ready, 2 * fn + 1)
                        dve.tensor_tensor(comb[:, :, :], pick1[:, :, :], pick2[:, :, :], ALU.add).then_inc(comb_ready, 1)
                    if step == "C":
                        dve.wait_ge(combT_hi_ready, fn + 1)
                        dve.tensor_tensor(combT[32:32 + E, fb, :], pG[0:E, :], combT[0:E, fb, :], ALU.subtract).then_inc(combT_ready, 1)
                        dve.wait_ge(combT_ready, fn + 1)
                        dve.sem_inc(g_read, 1)
                    if step == "G":
                        dve.wait_ge(silu_ready, use + 1)
                        dve.wait_ge(p_lo_ready, use + 1)
                        dve.tensor_tensor(prod[:, s, :], pPair[:, q, 1, :], silu[:, s, :], ALU.mult).then_inc(pair_read, 1)
                        if j == E:
                            dve.wait_ge(pair_read, RING + pair + used + 1)
                            dve.sem_inc(prod_ready, 1)
                    if step == "B":
                        before = used - 1
                        dve.wait_ge(pair_read, RING + pair + before + 1)
                        dve.wait_ge(b_psum, E * n + j + 1)
                        dve.tensor_tensor(prod[:, s, :], prod[:, s, :], pB[:, :], ALU.mult).then_inc(prod_ready, 1)
                        dve.wait_ge(prod_ready, RING + use + 1)
                        dve.sem_inc(b_read, 1)
                    if step == "Y":
                        dve.wait_ge(down_done, RING + EX * (n + 1))
                        dve.wait_ge(out_stored[b], 16 * i)
                        dve.tensor_tensor(y[:, b], x2[:, b], pD[:, :, :], ALU.add).then_inc(y_sum, 1)
                    used += step in "GAX"
            run(dve, work)

        @block.tensor
        def _(pe):
            pe.sem_inc(down_done, RING)
            pe.wait_ge(filled, 1)
            pe.wait_ge(sel_ready, 1)

            def work(items, i, b, fi, fb, pair, parity):
                n, fn = 2 * i + b, 2 * fi + fb
                used = 0
                for step, j in items:
                    use, s = EX * n + j, (b + j) % 2
                    q = (parity + used) % 2
                    if step in "GAX":
                        pe.wait_ge(pair_read, pair + used + 1)
                        used += 1
                    if step == "A":
                        pe.wait_ge(o_lo_ready, fn + 1)
                        for t in range(NTILE):
                            at = slice(P * t, P * t + P)
                            for g in range(G):
                                mm = product3(pe, pPair[:, q, t // 2, C * (t % 2):C * (t % 2) + C], o_hi[:, g, at], o_lo[:, g, at],
                                              wo_hi[:, g, :], wo_lo[:, g, :], g == 0, g == G - 1)
                        mm.then_inc(pair_psum, 1)
                    if step == "X":
                        pe.wait_ge(xn_ready, fn + 1)
                        for k in range(KT):
                            for t in range(NTILE):
                                mm = pe.transpose(pPair[:, q, k, P * t:P * t + P], xn[:, t, P * k:P * k + P], m.eye[:, :])
                        mm.then_inc(pair_psum, 1)
                    if step == "L":
                        pe.wait_ge(xT_ready, fn + 1)
                        pe.wait_ge(g_read, 2 * fn + 1)
                        for t in range(NTILE):
                            at = slice(P * t, P * t + P)
                            for k in range(KT):
                                mm = product3(pe, pG[:, E * t:E * t + E], xT_hi[:, fb, k, at], xT_lo[:, fb, k, at],
                                              gate_hi[:, k, :], gate_lo[:, k, :], k == 0, k == KT - 1)
                        mm.then_inc(g_psum, 1)
                    if step == "C":
                        pe.wait_ge(comb_ready, 2 * fn + 2)
                        for t in range(NTILE):
                            mm = pe.transpose(pG[0:E, P * t:P * t + P], comb[:, t, :], m.eye[:, :])
                        mm.then_inc(g_psum, 1)
                    if step == "G":
                        if j == 0:
                            pe.wait_ge(combT_ready, n + 1)
                        for s_, (hi, lo) in enumerate(((wg_hi, wg_lo), (wu_hi, wu_lo))):
                            for k in range(KT):
                                mm = product3(pe, pPair[:, q, s_, :], hi[:, k, j, :], lo[:, k, j, :],
                                              xT_hi[:, b, k, :], xT_lo[:, b, k, :], k == 0, k == KT - 1)
                        mm.then_inc(pair_psum, 1)
                    if step == "B":
                        pe.wait_ge(b_read, E * n + j + 1)
                        pe.matmul(pB[:, :], sel[:, j, :], combT[:, b, :], start=True, stop=True).then_inc(b_psum, 1)
                    if step == "D":
                        if j == 0:
                            pe.wait_ge(y_sum, n)
                        pe.wait_ge(p_lo_ready, RING + use + 1)
                        for t in range(NTILE):
                            at = slice(P * t, P * t + P)
                            mm = product3(pe, pD[:, t, :], p_hi[:, s, at], p_lo[:, s, at], wd_hi[:, j, :], wd_lo[:, j, :],
                                          j == 0 and t % 2 == 0, j == E, skip_group_check=True)
                        mm.then_inc(down_done, 1)
            run(pe, work)


class Resident:
    pass


def adaln_moe_kernel(nc, d):
    for name, shape in (("u1", (B, T, C)), ("qk1", (2, 2, B * C, T)), ("o1", (NG, T, HG * HD1)), ("x1", (B, T, C)),
                        ("xin", (B, T, C)), ("q2", (NG, 2, 2, P, T)), ("k2", (B, 2, LAT + ROPE, T)), ("o2", (NG, P, T))):
        d[name] = nc.dram_tensor("mid_" + name, shape, FP32, kind="Internal").ap()
    m = Resident()
    with ExitStack() as ctx:
        sb = lambda n, s, t=FP32: ctx.enter_context(nc.sbuf_tensor(n, s, t))
        m.eye, m.causal = sb("eye", [P, P]), sb("causal", [P, GT])
        m.bqk, m.bv = sb("bqk", [P, 2 * KT]), sb("bv", [P, C])
        m.wln, m.ebias = sb("wln", [P, 2, KT]), sb("ebias", [P, E])
        m.eye16, m.after16 = sb("eye16", [P, P], BF16), sb("after16", [P, P], BF16)
        m.mod = sb("mod", [P, B, 6, C])
        with nc.cleanup_on_exit():
            modulation(nc, d, m)
        with ExitStack() as inner:
            m.v1 = inner.enter_context(nc.sbuf_tensor("v1", [P, NG, T // P, HG * HD1], FP32))
            with nc.cleanup_on_exit():
                project1(nc, d, m)
            with nc.cleanup_on_exit():
                attention(nc, d, m, False)
        with ExitStack() as inner:
            m.lat = inner.enter_context(nc.sbuf_tensor("lat", [P, B * T // P, LAT], FP32))
            with nc.cleanup_on_exit():
                project2(nc, d, m)
            with nc.cleanup_on_exit():
                attention(nc, d, m, True)
        with nc.cleanup_on_exit():
            experts(nc, d, m)


def kernel(**inputs):
    import numpy as _np
    import concourse.bacc as _bacc
    from concourse import mybir as _mybir
    from concourse.bass_utils import run_bass_kernel_spmd as _run

    f = {name: _np.asarray(value) for name, value in inputs.items()}
    wq = f["L0_ffn_Wq"].reshape(C, HEADS, HD2)
    turn = _np.concatenate([_np.arange(0, ROPE, 2), _np.arange(1, ROPE, 2)])
    swap = _np.concatenate([turn[ROPE // 2:], turn[:ROPE // 2]])
    wkva = f["L0_ffn_Wkva"]
    latent = wkva[:, :LAT]
    cos, sin = rope_tables()
    causal = _np.zeros((P, GT), _np.float32)
    causal[:, GT - P:] = _np.where(_np.arange(P)[None, :] > _np.arange(P)[:, None], _np.float32(NEG), _np.float32(0))
    sel = _np.zeros((64, E, P), _np.float32)
    for e in range(E):
        sel[e, e] = sel[32 + e, e] = 1
    data = {
        "x": f["L0_attn_x"], "wT": f["L0_attn_W"].T, "bqk": f["L0_attn_b"][:2 * C].reshape(-1, P).T,
        "bv": f["L0_attn_b"][2 * C:], "cT": f["L0_c"].T, "wmod": f["L0_wmod"],
        "wln": _np.stack([f["L0_ffn_w_ln1"].reshape(KT, P).T, f["L0_ffn_w_ln2"].reshape(KT, P).T], axis=1), "ebias": f["L0_ffn_expert_bias"],
        "wqnT": wq[:, :, :HD2 - ROPE].transpose(1, 2, 0).reshape(-1, C), "wkvbT": f["L0_ffn_Wkvb"].T,
        "wqr": _np.stack([wq[:, :, ROPE:][:, :, turn], wq[:, :, ROPE:][:, :, swap]], axis=1).reshape(C, -1),
        "wk": _np.concatenate([latent, wkva[:, LAT:][:, turn], latent, wkva[:, LAT:][:, turn]] + [wkva[:, LAT:][:, swap]] * 4, axis=1),
        "Wo": f["L0_ffn_Wo"], "Wgate": f["L0_ffn_Wgate"], "Wg": f["L0_ffn_Wg"], "Wu": f["L0_ffn_Wu"], "Wd": f["L0_ffn_Wd"],
        "sWg": f["L0_ffn_sWg"], "sWu": f["L0_ffn_sWu"], "sWd": f["L0_ffn_sWd"],
        "eye": _np.eye(P, dtype=_np.float32), "causal": causal, 
        "cos": _np.stack([_np.tile(cos, (4, 1)), _np.tile(_np.concatenate([_np.ones_like(cos), cos]), (2, 1))], axis=1),
        "sin": _np.stack([_np.tile(sin, (4, 1)), _np.tile(_np.concatenate([_np.zeros_like(sin), sin]), (2, 1))], axis=1),
        "sel": sel.reshape(64, -1), "rank": _np.arange(E, 0, -1).astype(_np.float32),
    }
    nc = _bacc.Bacc("TRN2", target_bir_lowering=False, num_devices=1)
    arrays, d = {}, {}
    for name, a in data.items():
        a = _np.ascontiguousarray(a)
        arrays[f"in_{name}_dram"] = a
        d[name] = nc.dram_tensor(f"in_{name}_dram", a.shape, _mybir.dt.from_np(a.dtype), kind="ExternalInput").ap()
    d["out"] = nc.dram_tensor("out_0_dram", (B, T, C), _mybir.dt.from_np(_np.dtype("float32")), kind="ExternalOutput").ap()
    adaln_moe_kernel(nc, d)
    r = _run(nc, [arrays], core_ids=[0])
    return r.results[0]["out_0_dram"]
```

```python
import numpy as np
import concourse.bass as bass
from concourse import mybir
from concourse.alu_op_type import AluOpType as ALU
from contextlib import ExitStack

FP32 = mybir.dt.float32
F32R = mybir.dt.float32r
BF16 = mybir.dt.bfloat16
ACT = mybir.ActivationFunctionType
AX = mybir.AxisListType

B, T, C = 2, 2048, 256
P = 128
KT = C // P
GT = 512
NTILE = GT // P
NGRP = T // GT
HEADS = 16
HG = 4
NG = B * HEADS // HG
HD1 = C // HEADS
HD2, ROPE, LAT = 64, 32, 32
E, I = 8, 128
EPS = 1e-5
NEG = -1e30


def rope_tables():
    freqs = (np.float32(1.0) / np.float32(100000.0) ** (np.arange(0, ROPE, 2, dtype=np.float32) / np.float32(ROPE))).astype(np.float32)
    ang = np.outer(freqs, np.arange(T, dtype=np.float32)).astype(np.float32)
    cos, sin = np.cos(ang).astype(np.float32), np.sin(ang).astype(np.float32)
    return np.concatenate([cos, cos]), np.concatenate([-sin, sin])



def modulation(nc, d, m):
    with ExitStack() as ctx:
        sb = lambda n, s, t=FP32: ctx.enter_context(nc.sbuf_tensor(n, s, t))
        sem = lambda n: nc.alloc_semaphore(n)
        cT, cE = sb("cT", [P, KT, B]), sb("cE", [P, KT, B])
        cB = sb("cB", [P, KT, B, P])
        wmod = sb("wmod", [P, KT, 6 * C])
        size, sign = sb("ga_size", [P, B, C]), sb("ga_sign", [P, B, C])
        ps = ctx.enter_context(nc.psum_tensor("ps_mod", [P, 6, 512], FP32))
        loaded, c_exp, c_ready, mod_psum, mod_read, chain = (
            sem(n) for n in ("mod_loaded", "mod_c_exp", "mod_c_ready", "mod_psum", "mod_read", "mod_chain"))
        block = ctx.enter_context(nc.Block())
        LOADS = 8

        @block.sync
        def _(sp):
            sp.dma_start(cT[:, :, :], d["cT"].rearrange("(k p) b -> p k b", p=P)).then_inc(loaded, 16)
            sp.dma_start(wmod[:, :, :], d["wmod"].rearrange("(k p) n -> p k n", p=P)).then_inc(loaded, 16)
            sp.dma_start(m.eye[:, :], d["eye"]).then_inc(loaded, 16)
            sp.dma_start(m.causal[:, :], d["causal"]).then_inc(loaded, 16)
            sp.dma_start(m.bqk[:, :], d["bqk"]).then_inc(loaded, 16)
            sp.dma_start(m.bv[:, :], d["bv"].rearrange("(a n) -> a n", a=1).broadcast_to([P, C])).then_inc(loaded, 16)
            sp.dma_start(m.wln[:, :, :], d["wln"]).then_inc(loaded, 16)
            sp.dma_start(m.ebias[:, :], d["ebias"].rearrange("(a n) -> a n", a=1).broadcast_to([P, E])).then_inc(loaded, 16)

        @block.scalar
        def _(act):
            act.wait_ge(loaded, 16 * LOADS)
            act.activation(cE[:, :, :], cT[:, :, :], ACT.Exp, scale=-1.0).then_inc(c_exp, 1)

        @block.tensor
        def _(pe):
            pe.wait_ge(c_ready, 1)
            for b in range(B):
                for n in range(3):
                    for k in range(KT):
                        mm = pe.matmul(ps[:, 3 * b + n, :], cB[:, k, b, :], wmod[:, k, 512 * n:512 * n + 512],
                                       start=(k == 0), stop=(k == KT - 1))
                    mm.then_inc(mod_psum, 1)

        @block.vector
        def _(dve):
            done = [0]

            def link(ins):
                done[0] += 1
                ins.then_inc(chain, 1)
                dve.wait_ge(chain, done[0])

            dve.wait_ge(c_exp, 1)
            dve.tensor_copy(m.eye16[:, :], m.eye[:, :])
            dve.tensor_copy(m.after16[:, :], m.causal[:, GT - P:GT])
            link(dve.tensor_scalar(cE[:, :, :], cE[:, :, :], 1.0, None, ALU.add))
            link(dve.reciprocal(cE[:, :, :], cE[:, :, :]))
            link(dve.tensor_tensor(cT[:, :, :], cT[:, :, :], cE[:, :, :], ALU.mult))
            dve.tensor_copy(cB[:, :, :, :], cT[:, :, :].unsqueeze(3).broadcast_to([P, KT, B, P])).then_inc(c_ready, 1)
            for b in range(B):
                for n in range(3):
                    dve.wait_ge(mod_psum, 3 * b + n + 1)
                    dve.tensor_copy(m.mod[:, b, 2 * n:2 * n + 2, :],
                                    ps[:, 3 * b + n, :].rearrange("p (a c) -> p a c", a=2)).then_inc(mod_read, 1)
            dve.wait_ge(mod_read, 6)
            for v in (1, 4):
                link(dve.tensor_scalar(m.mod[:, :, v, :], m.mod[:, :, v, :], 1.0, None, ALU.add))
            for v in (2, 5):
                link(dve.tensor_scalar(sign[:, :, :], m.mod[:, :, v, :], 0.0, 2.0, ALU.is_ge, ALU.mult))
                link(dve.tensor_scalar(size[:, :, :], m.mod[:, :, v, :], -1.0, None, ALU.mult))
                link(dve.tensor_tensor(size[:, :, :], size[:, :, :], m.mod[:, :, v, :], ALU.max))
                link(dve.tensor_scalar(size[:, :, :], size[:, :, :], 0.25, None, ALU.max))
                link(dve.scalar_tensor_tensor(out=m.mod[:, :, v, :], in0=sign[:, :, :], scalar=-1.0, in1=size[:, :, :],
                                              op0=ALU.add, op1=ALU.mult))


def product3(pe, out, hi, lo, x_hi, x_lo, first, last, **kw):
    pe.matmul(out, lo, x_hi, start=first, stop=False, **kw)
    pe.matmul(out, hi, x_lo, start=False, stop=False, **kw)
    return pe.matmul(out, hi, x_hi, start=False, stop=last, **kw)


def split_weights(nc, name, jobs):
    with ExitStack() as ctx:
        sem = lambda n: nc.alloc_semaphore(name + n)
        loaded = [sem(f"_loaded{n}") for n in range(len(jobs))]
        high = sem("_high")
        block = ctx.enter_context(nc.Block())

        @block.sync
        def _(sp):
            for n, (loads, stage, hi, lo) in enumerate(jobs):
                for src, place in loads:
                    sp.dma_start(place, src).then_inc(loaded[n], 16)

        @block.scalar
        def _(act):
            for n, (loads, stage, hi, lo) in enumerate(jobs):
                if loads:
                    act.wait_ge(loaded[n], 16 * len(loads))
                act.activation(hi, stage, ACT.Copy).then_inc(high, 1)

        @block.vector
        def _(dve):
            for n, (loads, stage, hi, lo) in enumerate(jobs):
                dve.wait_ge(high, n + 1)
                dve.tensor_tensor(lo, stage, hi, ALU.subtract)


def project1(nc, d, m):
    with ExitStack() as ctx:
        sb = lambda n, s, t=FP32: ctx.enter_context(nc.sbuf_tensor("p1_" + n, s, t))
        sem = lambda n: nc.alloc_semaphore("p1_" + n)
        sems = lambda n: [sem(f"{n}{b}") for b in range(2)]
        w_st = sb("w_st", [P, KT, 3 * C])
        w_hi, w_lo = sb("w_hi", [P, KT, 3 * C], F32R), sb("w_lo", [P, KT, 3 * C], F32R)
        split_weights(nc, "p1_w", [([(d["wT"].rearrange("(k p) n -> p k n", p=P), w_st[:, :, :])], w_st[:, :, :], w_hi[:, :, :], w_lo[:, :, :])])
        x = sb("x", [P, B, NTILE, C])
        h = sb("h", [P, B, NTILE, C])
        u = sb("u", [P, B, NTILE, C])
        stats, mv = sb("stats", [P, B, NTILE, 6]), sb("mv", [P, B, NTILE, 2])
        sd, rstd = sb("sd", [P, B, NTILE]), sb("rstd", [P, B, NTILE])
        hT_hi, hT_lo = sb("hT_hi", [P, B, KT, GT], F32R), sb("hT_lo", [P, B, KT, GT], F32R)
        qk_hi, qk_lo = sb("qk_hi", [P, 2, GT], F32R), sb("qk_lo", [P, 2, GT], F32R)
        pT = ctx.enter_context(nc.psum_tensor("p1_pT", [P, KT, GT], FP32))
        pQK = ctx.enter_context(nc.psum_tensor("p1_pQK", [P, 2, GT], FP32))
        pV = ctx.enter_context(nc.psum_tensor("p1_pV", [P, 2, 2, C], FP32))
        x_loaded, u_stored, qk_stored = sems("x_loaded"), sems("u_stored"), sems("qk_stored")
        stats_ready, var_ready, sd_ready, rstd_ready, unit_ready, scaled, h_ready = (
            sem(n) for n in ("stats_ready", "var_ready", "sd_ready", "rstd_ready", "unit_ready", "scaled", "h_ready"))
        gated, u_ready, t_psum, hi_ready, lo_ready = (sem(n) for n in ("gated", "u_ready", "t_psum", "hi_ready", "lo_ready"))
        qk_psum, qk_hi_ready, qk_lo_ready, v_psum, v_read = (
            sem(n) for n in ("qk_psum", "qk_hi_ready", "qk_lo_ready", "v_psum", "v_read"))
        passed, sp_passed = sem("passed"), sem("sp_passed")
        block = ctx.enter_context(nc.Block())
        RING, QK = 2, 4
        spread = lambda b, v: m.mod[:, b, v, :].unsqueeze(1).broadcast_to([P, NTILE, C])
        token = lambda name, b, i: d[name].rearrange("b (i t p) c -> b i p t c", t=NTILE, p=P)[b, bass.ds(i, 1)].rearrange("a p t c -> (a p) t c")

        def order(products, front):
            if not products:
                return [(x, 0) for x in "BCDUT"]
            after = {0: "B", 1: "CD", 3: "U"} if front else {}
            items = []
            for g in range(QK):
                items += [("Q", g)] + [(x, 0) for x in after.get(g, "")]
            return items + [("V", 0), ("V", 1)] + [("T", 0)] * front

        def run(eng, work):
            work(order(False, True), -1, 1, 0, 0)
            with eng.Fori(0, NGRP - 1) as i:
                for b in range(B):
                    work(order(True, True), i, b, i + b, 1 - b)
            work(order(True, True), NGRP - 1, 0, NGRP - 1, 1)
            work(order(True, False), NGRP - 1, 1, 0, 0)

        @block.sync
        def _(sp):
            def work(items, i, b, fi, fb):
                n, fn = 2 * i + b, 2 * fi + fb
                for step, g in items:
                    if step == "Q":
                        sp.wait_ge(qk_lo_ready, RING + QK * n + g + 1)
                        sp.sem_inc(sp_passed, 1)
                        for s, half in enumerate((qk_hi, qk_lo)):
                            row = b * C + P * (g % 2)
                            sp.dma_start(d["qk1"][g // 2, s, row:row + P, bass.ds(i * GT, GT)],
                                         half[:, g % 2, :].bitcast(FP32)).then_inc(qk_stored[g % 2], 16)
                    if step == "T":
                        sp.wait_ge(u_ready, fn + 1)
                        sp.sem_inc(sp_passed, 1)
                        sp.dma_start(token("u1", fb, fi), u[:, fb]).then_inc(u_stored[fb], 16)

            for b in range(B):
                sp.dma_start(x[:, b], token("x", b, 0)).then_inc(x_loaded[b], 16)
            work(order(False, True), -1, 1, 0, 0)
            with sp.Fori(0, NGRP - 1) as i:
                for b in range(B):
                    sp.wait_ge(u_ready, 2 * i + b + 1)
                    sp.sem_inc(sp_passed, 1)
                    sp.dma_start(x[:, b], token("x", b, i + 1)).then_inc(x_loaded[b], 16)
                    work(order(True, True), i, b, i + b, 1 - b)
            work(order(True, True), NGRP - 1, 0, NGRP - 1, 1)
            work(order(True, False), NGRP - 1, 1, 0, 0)
            for b in range(B):
                sp.wait_ge(u_stored[b], 16 * NGRP)
                sp.wait_ge(qk_stored[b], 16 * 2 * QK * NGRP)

        @block.gpsimd
        def _(pool):
            def work(items, i, b, fi, fb):
                fn = 2 * fi + fb
                for step, g in items:
                    if step == "D":
                        pool.wait_ge(scaled, fn + 1)
                        pool.tensor_tensor(h[:, fb], h[:, fb], spread(fb, 0), ALU.add).then_inc(h_ready, 1)
                    if step == "U":
                        pool.wait_ge(h_ready, fn + 1)
                        pool.wait_ge(u_stored[fb], 16 * fi)
                        pool.tensor_tensor(u[:, fb], h[:, fb], spread(fb, 2), ALU.mult).then_inc(gated, 1)
                        pool.wait_ge(gated, fn + 1)
                        pool.tensor_tensor(u[:, fb], u[:, fb], x[:, fb], ALU.add).then_inc(u_ready, 1)
            run(pool, work)

        @block.scalar
        def _(act):
            def work(items, i, b, fi, fb):
                n, fn = 2 * i + b, 2 * fi + fb
                for step, g in items:
                    if step == "B":
                        act.wait_ge(var_ready, fn + 1)
                        act.activation(sd[:, fb], mv[:, fb, :, 1], ACT.Sqrt).then_inc(sd_ready, 1)
                    if step == "T":
                        for k in range(KT):
                            act.wait_ge(t_psum, KT * fn + k + 1)
                            act.activation(hT_hi[:, fb, k, :], pT[:, k, :], ACT.Copy).then_inc(hi_ready, 1)
                    if step == "Q":
                        act.wait_ge(qk_psum, QK * n + g + 1)
                        act.wait_ge(qk_stored[g % 2], 32 * (2 * n + g // 2))
                        act.activation(qk_hi[:, g % 2, :], pQK[:, g % 2, :], ACT.Identity, bias=m.bqk[:, g:g + 1]).then_inc(qk_hi_ready, 1)
            run(act, work)

        @block.vector
        def _(dve):
            dve.sem_inc(qk_lo_ready, RING)
            dve.sem_inc(v_read, RING)

            def work(items, i, b, fi, fb):
                n, fn = 2 * i + b, 2 * fi + fb
                for step, g in items:
                    if step == "B":
                        dve.wait_ge(x_loaded[fb], 16 * (fi + 1))
                        for t in range(NTILE):
                            last = dve.bn_stats(stats[:, fb, t, :], x[:, fb, t, :])
                        last.then_inc(stats_ready, 1)
                        dve.wait_ge(stats_ready, 2 * fn + 1)
                        dve.sem_inc(passed, 1)
                        for t in range(NTILE):
                            last = dve.bn_aggr(mv[:, fb, t, :], stats[:, fb, t, :])
                        last.then_inc(stats_ready, 1)
                        dve.wait_ge(stats_ready, 2 * fn + 2)
                        dve.tensor_scalar(mv[:, fb, :, 1], mv[:, fb, :, 1], EPS, None, ALU.add).then_inc(var_ready, 1)
                    if step == "C":
                        dve.wait_ge(sd_ready, fn + 1)
                        dve.reciprocal(rstd[:, fb], sd[:, fb]).then_inc(rstd_ready, 1)
                        dve.wait_ge(rstd_ready, fn + 1)
                        for t in range(NTILE):
                            last = dve.tensor_scalar(h[:, fb, t, :], x[:, fb, t, :], mv[:, fb, t, 0:1], rstd[:, fb, t:t + 1],
                                                     ALU.subtract, ALU.mult)
                        last.then_inc(unit_ready, 1)
                    if step == "D":
                        dve.wait_ge(unit_ready, fn + 1)
                        dve.tensor_tensor(h[:, fb], h[:, fb], spread(fb, 1), ALU.mult).then_inc(scaled, 1)
                    if step == "T":
                        for k in range(KT):
                            dve.wait_ge(hi_ready, KT * fn + k + 1)
                            dve.tensor_tensor(hT_lo[:, fb, k, :], pT[:, k, :], hT_hi[:, fb, k, :], ALU.subtract).then_inc(lo_ready, 1)
                    if step == "Q":
                        dve.wait_ge(qk_hi_ready, QK * n + g + 1)
                        dve.scalar_tensor_tensor(out=qk_lo[:, g % 2, :], in0=pQK[:, g % 2, :], scalar=m.bqk[:, g:g + 1],
                                                 in1=qk_hi[:, g % 2, :], op0=ALU.add, op1=ALU.subtract).then_inc(qk_lo_ready, 1)
                    if step == "V":
                        dve.wait_ge(v_psum, 2 * n + g + 1)
                        dst = m.v1[:, 4 * b:4 * b + 4, bass.ds(i * NTILE + 2 * g, 2), :].rearrange("p g t f -> p t g f")
                        dve.tensor_tensor(dst, pV[:, g].rearrange("p t (g f) -> p t g f", g=4),
                                          m.bv[:, :].rearrange("p (g f) -> p g f", g=4).unsqueeze(1).broadcast_to([P, 2, 4, C // 4]),
                                          ALU.add).then_inc(v_read, 1)
            run(dve, work)

        @block.tensor
        def _(pe):
            def work(items, i, b, fi, fb):
                n, fn = 2 * i + b, 2 * fi + fb
                for step, g in items:
                    if step == "T":
                        pe.wait_ge(h_ready, fn + 1)
                        pe.wait_ge(lo_ready, KT * fn)
                        for k in range(KT):
                            for t in range(NTILE):
                                mm = pe.transpose(pT[:, k, P * t:P * t + P], h[:, fb, t, P * k:P * k + P], m.eye[:, :])
                            mm.then_inc(t_psum, 1)
                    if step == "Q":
                        if g == 0:
                            pe.wait_ge(lo_ready, KT * n + KT)
                        pe.wait_ge(qk_lo_ready, QK * n + g + 1)
                        for k in range(KT):
                            mm = product3(pe, pQK[:, g % 2, :], w_hi[:, k, P * g:P * g + P], w_lo[:, k, P * g:P * g + P],
                                          hT_hi[:, b, k, :], hT_lo[:, b, k, :], k == 0, k == KT - 1)
                        mm.then_inc(qk_psum, 1)
                    if step == "V":
                        pe.wait_ge(v_read, 2 * n + g + 1)
                        for t in range(2):
                            at = P * (2 * g + t)
                            for k in range(KT):
                                mm = product3(pe, pV[:, g, t, :], hT_hi[:, b, k, at:at + P], hT_lo[:, b, k, at:at + P],
                                              w_hi[:, k, 2 * C:3 * C], w_lo[:, k, 2 * C:3 * C], k == 0, k == KT - 1)
                        mm.then_inc(v_psum, 1)
            run(pe, work)


def attention(nc, d, m, second):
    with ExitStack() as ctx:
        name = "a2_" if second else "a1_"
        sb = lambda n, s, t=FP32: ctx.enter_context(nc.sbuf_tensor(name + n, s, t))
        sem = lambda n: nc.alloc_semaphore(name + n)
        KH = 1 if second else HG
        SCALE = HD2 ** -0.5 if second else 1.0
        NS, NR = 3, 3 if second else 4
        STACKS = 2 if second else 1
        q = [sb(f"q{n}", [P, NGRP, HG, GT], F32R) for n in range(STACKS)]
        kmax = sb("kmax", [P, KH, T], F32R)
        kmax_first = sb("kmax_first", [P, KH, GT], F32R)
        key = [sb(f"key{n}", [P, KH, T], F32R) for n in range(STACKS)]
        MAX_ROWS = P if second else 96
        rows_exp = [P] * (STACKS - 1) + [98]
        prob = sb("prob", [P, 4, HG, GT])
        val = sb("val", [P, T // P, KH, 32])
        rowmax = sb("rowmax", [P, 2, HG, NTILE, NGRP])
        fullmax = sb("fullmax", [P, HG * NTILE])
        neg_hi, neg_lo = sb("neg_hi", [HG * NTILE, P], F32R), sb("neg_lo", [HG * NTILE, P], F32R)
        pR = ctx.enter_context(nc.psum_tensor(name + "pR", [P, NR, GT], FP32))
        pS = ctx.enter_context(nc.psum_tensor(name + "pS", [P, NS, GT], FP32))
        pO = ctx.enter_context(nc.psum_tensor(name + "pO", [P, GT], FP32))
        if second:
            ones = sb("ones", [P, 32])
            out, recip = sb("out", [P, 2, GT]), sb("recip", [P, GT])
            zsum = sb("zsum", [P, HG, GT])
            pZ = ctx.enter_context(nc.psum_tensor(name + "pZ", [P, GT], FP32))
        else:
            out, recip = sb("out", [P, 2, NTILE, HG, HD1]), sb("recip", [P, NTILE, HG])
        oT = sb("oT", [P, GT])

        filled, q_filled = sem("filled"), sem("q_filled")
        dve_passed, sp_passed = sem("dve_passed"), sem("sp_passed")
        q_loaded, kmax_loaded, key_loaded = ([sem(f"{n}{c}") for c in range(NGRP)] for n in ("q_loaded", "kmax_loaded", "key_loaded"))
        first_loaded = [sem("first_loaded")]
        val_ready = sem("val_ready")
        r_psum, r_read = sem("r_psum"), sem("r_read")
        fullmax_ready, neg_hi_ready, neg_ready, neg_stored = sem("fullmax_ready"), sem("neg_hi_ready"), sem("neg_ready"), sem("neg_stored")
        s_psum, exp_ready, pv_done = sem("s_psum"), sem("exp_ready"), sem("pv_done")
        z_added, z_psum = sem("z_added"), sem("z_psum")
        experts_loaded = sem("experts_loaded")
        o_copied, recip_ready, out_ready = sem("o_copied"), sem("recip_ready"), sem("out_ready")
        out_stored = [sem(f"out_stored{c}") for c in range(2)]
        block = ctx.enter_context(nc.Block())

        s_bank = lambda c, kt, h: (HG * (upto(c) + kt) + h) % NS

        def bank_before(c, kt, h):
            at = HG * (upto(c) + kt) + h
            return at - NS if at >= NS else max(n for n in range(HG * STEPS) if n % NS == at % NS) - HG * STEPS

        upto = lambda c: 2 * c * (c + 1)
        STEPS = upto(NGRP)
        FILLS = 3 if second else 6
        QL = 16 * (6 if second else 4)
        KL = 16 * (3 if second else 4)
        KML = 16 * (2 if second else 4)
        EXP_CREDIT, PV_CREDIT, R_CREDIT = HG, 4, NR
        by_pool = lambda c, kt: c > 0 and kt % 4 != 3
        pool_adds = [by_pool(c, kt) and kt > 0 for c in range(NGRP) for kt in range(4 * c + 4)]
        ADDS = sum(pool_adds)

        def adds_before(at):
            return sum(pool_adds[:at]) if at >= 0 else -sum(pool_adds[at:])

        score_step = lambda g, c, kt: STEPS * g + upto(c) + kt
        first_query = lambda c, kt: max(0, P * (kt - 4 * c))

        def rows(c, tiles=range(NTILE)):
            return [("R", c, h, t, kc) for t in tiles for h in range(HG) for kc in range(c + 1)]

        def chain_up(*parts):
            side, late = [], []
            for part in parts:
                side += part[:3] + late + part[3:]
                c, h, t, kc = part[-1][1:]
                late = []
                if t == NTILE - 1:
                    side.append(("F", c))
                    late = [("M", c)]
            return side + late

        def order(side, scores, deferred=False):
            main = []
            for c in range(NGRP) if scores else ():
                for kt in range(4 * c + 4):
                    main += [[("S", c, kt, h)] for h in range(HG)]
                    if c or kt:
                        main[-1].append(("V", c, kt - 1) if kt else ("V", c - 1, 4 * c - 1))
                    if c and kt == 0:
                        main[-1].append(("E", c - 1))
            if scores:
                main.append([("V", NGRP - 1, 4 * NGRP - 1), ("E", NGRP - 1)])
                for c in range(0 if deferred else 1, NGRP):
                    at = HG * upto(c)
                    if not second:
                        main[at + 2 * HG].append(("O", c - 1))
                        continue
                    main[at + (HG + 3 if c else 0)].append(("Z", c - 1))
                    for n in range(NTILE):
                        main[at + (2 * HG + 2 * n if c else 1 + n)].append(("N", c - 1, n))
            cost = {"R": 612, "N": 1090, "O": 600, "M": 400, "F": 200}
            price = lambda x: 100 + P * (x[3] + 1) if x[0] == "R" and x[4] == x[1] else cost.get(x[0], 0)
            weights = [sum(GT - first_query(*x[1:3]) for x in items if x[0] == "S") for items in main]
            whole = sum(map(price, side)) + sum(price(x) for items in main for x in items)
            result, side, paid = [], list(side), 0
            for n, items in enumerate(main):
                result += items
                paid += sum(map(price, items))
                while side and paid + price(side[0]) <= whole * sum(weights[:n + 1]) / max(1, sum(weights)) + 1:
                    paid += price(side[0])
                    result.append(side.pop(0))
            return result + side

        first = order(chain_up(rows(0), rows(1), rows(2, (0, 1, 2))), False)
        side = chain_up(rows(2, (3,)), rows(3), rows(0), rows(1), rows(2, (0, 1, 2)))
        body0, body = order(side, True), order(side, True, True)
        of_next = lambda x: x[0] in "RFM" and (x[1] < 2 or x[0] == "R" and x[1] == 2 and x[3] < 3)
        final = [x for x in body if not of_next(x)]
        final += [("Z", NGRP - 1)] + [("N", NGRP - 1, n) for n in range(NTILE)] if second else [("O", NGRP - 1)]
        bank_uses = lambda items: sum(x[0] in "RMOK" for x in items)
        body = [("K",)] * (-bank_uses(body) % NR) + body
        R_FIRST, R_BODY = bank_uses(first), bank_uses(body)
        R_LOOP = R_FIRST + bank_uses(body0)
        bank_at_start = {id(first): 0, id(body0): R_FIRST % NR, id(body): R_LOOP % NR, id(final): R_LOOP % NR}

        def run(eng, work):
            work(first, -1, 0)
            work(body0, 0, R_FIRST)
            with eng.Fori(0, NG - 2) as k:
                work(body, k + 1, R_LOOP + k * R_BODY)
            work(final, NG - 1, R_LOOP + (NG - 2) * R_BODY)

        def max_count(items, g, c):
            return c if items is first else 4 * g + (c if c >= 2 else 4 + c)

        @block.sync
        def _(sp):
            def load_q(c, g):
                cols = slice(c * GT, (c + 1) * GT)
                if second:
                    for s in range(2):
                        for k in range(2):
                            v = d["q2"][bass.ds(g, 1), s, k, :, cols].rearrange("a (h r) t -> r (a h) t", h=HG)
                            at = 64 * s + 32 * k
                            sp.dma_start(q[0][at:at + 32, c].bitcast(FP32), v).then_inc(q_loaded[c], 16)
                            if s == 0:
                                sp.dma_start(q[1][at:at + 32, c].bitcast(FP32), v).then_inc(q_loaded[c], 16)
                else:
                    for n, s in enumerate((0, 0, 1, 1)):
                        v = d["qk1"][0, s, bass.ds(64 * g, 64), cols].rearrange("(h f) t -> f h t", h=HG)
                        sp.dma_start(q[0][16 * n:16 * n + 16, c].bitcast(FP32), v).then_inc(q_loaded[c], 16)

            def load_kmax(c, g, tile=kmax, signal=kmax_loaded):
                cols = slice(c * GT, (c + 1) * GT)
                if second:
                    sp.sem_inc(sp_passed, 1)
                    for n in range(2):
                        v = d["k2"][bass.ds(g // 4, 1), 0, :, cols].rearrange("a f t -> (a f) t")
                        sp.dma_start(tile[64 * n:64 * n + 64, 0, cols].bitcast(FP32), v).then_inc(signal[c], 16)
                else:
                    for n, s in enumerate((0, 1, 0, 1)):
                        v = d["qk1"][1, s, bass.ds(64 * g, 64), cols].rearrange("(h f) t -> f h t", h=HG)
                        sp.dma_start(tile[16 * n:16 * n + 16, :, cols].bitcast(FP32), v).then_inc(signal[c], 16)

            def load_k(c, g):
                cols = slice(c * GT, (c + 1) * GT)
                if second:
                    sp.sem_inc(sp_passed, 1)
                    for n, at, s in ((0, 0, 0), (0, 64, 0), (1, 0, 1)):
                        v = d["k2"][bass.ds(g // 4, 1), s, :, cols].rearrange("a f t -> (a f) t")
                        sp.dma_start(key[n][at:at + 64, 0, cols].bitcast(FP32), v).then_inc(key_loaded[c], 16)
                else:
                    for n, s in enumerate((0, 1, 0, 1)):
                        v = d["qk1"][1, s, bass.ds(64 * g, 64), cols].rearrange("(h f) t -> f h t", h=HG)
                        sp.dma_start(key[0][16 * n:16 * n + 16, :, cols].bitcast(FP32), v).then_inc(key_loaded[c], 16)

            def store_max(c, count):
                sp.wait_ge(neg_ready, count + 1)
                for row, half in ((96, neg_hi), (97, neg_lo)):
                    sp.dma_start(q[-1][row:row + 1, c].bitcast(FP32), half[:, :].bitcast(FP32)).then_inc(neg_stored, 16)

            def store_out(c, g):
                sp.wait_ge(out_ready, 4 * g + c + 1)
                cols = slice(c % NGRP * GT, (c % NGRP + 1) * GT)
                if second:
                    dst = d["o2"][bass.ds(g + min(c, 0), 1), :, cols].rearrange("a p t -> (a p) t")
                    sp.dma_start(dst, out[:, c % 2, :]).then_inc(out_stored[c % 2], 16)
                else:
                    dst = d["o1"][bass.ds(g + min(c, 0), 1), cols].rearrange("a (t p) f -> p (a t) f", p=P)
                    sp.dma_start(dst, out[:, c % 2].rearrange("p t h f -> p t (h f)")).then_inc(out_stored[c % 2], 16)

            load_kmax(0, 0, kmax_first, first_loaded)
            for c in range(3):
                load_q(c, 0)
                load_kmax(c, 0)
            load_kmax(3, 0)
            for c in range(NGRP):
                load_k(c, 0)
            sp.wait_ge(q_filled, 1)
            for c in range(2):
                store_max(c, c)

            def step(g, has_before, has_next):
                sp.wait_ge(s_psum, HG * STEPS * g)
                load_q(3, g)
                store_max(2, 4 * g + 2)
                if has_before:
                    load_k(3, g)
                    store_out(-1, g)
                if has_next:
                    sp.wait_ge(s_psum, HG * (STEPS * g + upto(1)))
                    load_q(0, g + 1)
                    load_kmax(0, g + 1, kmax_first, first_loaded)
                store_out(0, g)
                if has_next:
                    sp.wait_ge(s_psum, HG * (STEPS * g + upto(2)))
                    load_q(1, g + 1)
                store_out(1, g)
                store_max(3, 4 * g + 3)
                if has_next:
                    for c in range(NGRP):
                        load_kmax(c, g + 1)
                    sp.wait_ge(s_psum, HG * (STEPS * g + upto(3)))
                    load_q(2, g + 1)
                store_out(2, g)
                if has_next:
                    for c in range(3):
                        sp.wait_ge(s_psum, HG * (STEPS * g + upto(3) + 4 * c + 4))
                        load_k(c, g + 1)
                        if c < 2:
                            store_max(c, 4 * g + 4 + c)

            if second:
                for src, place in m.expert_loads:
                    sp.dma_start(place, src).then_inc(experts_loaded, 16)
            step(0, False, True)
            with sp.Fori(0, NG - 2) as k:
                step(k + 1, True, True)
            step(NG - 1, True, False)
            store_out(NGRP - 1, NG - 1)
            if second:
                sp.wait_ge(experts_loaded, 16 * len(m.expert_loads))
            for r in range(2):
                sp.wait_ge(out_stored[r], 16 * 2 * NG)

        @block.gpsimd
        def _(pool):
            fills = [(t[64:P].bitcast(FP32), 0.0) for t in ((key[1],) if second else (kmax, kmax_first, key[0]))]
            fills += [(ones[:, :], 1.0)] if second else [(val[:, :, :, 16:32], 0.0), (val[:, :, :, 16:17], 1.0)]
            fills += [(key[-1][96:98].bitcast(FP32), 1.0)]
            for n, (place, value) in enumerate(fills):
                if n:
                    pool.wait_ge(filled, n)
                pool.memset(place, value).then_inc(filled, 1)
            pool.wait_ge(filled, FILLS)

            def values(c, g):
                if second:
                    src = m.lat[:, bass.ds((g // 4) * (T // P) + 4 * c, 4), :]
                    pool.tensor_copy(val[:, 4 * c:4 * c + 4, 0, :], src).then_inc(val_ready, 1)
                else:
                    src = m.v1[:, bass.ds(g, 1), 4 * c:4 * c + 4, :].rearrange("p a t (h f) -> p (a t) h f", h=HG)
                    pool.tensor_copy(val[:, 4 * c:4 * c + 4, :, 0:16], src).then_inc(val_ready, 1)

            if second:
                pool.sem_inc(z_added, EXP_CREDIT)

            def work(items, g, r):
                for item in items:
                    if item[0] == "V" and second and by_pool(*item[1:]) and item[2] > 0:
                        _, c, kt = item
                        n = score_step(g, c, kt)
                        at = first_query(c, kt)
                        pool.wait_ge(exp_ready, EXP_CREDIT + HG * n + HG)
                        before = EXP_CREDIT + ADDS * g + adds_before(upto(c) + kt)
                        if kt == 1:
                            pool.wait_ge(z_psum, 4 * g + c)
                            pool.tensor_tensor(zsum[:, :, :], prob[:, 0, :, :], prob[:, 1, :, :], ALU.add).then_inc(z_added, 1)
                        else:
                            pool.wait_ge(z_added, before)
                            pool.tensor_tensor(zsum[:, :, at:GT], zsum[:, :, at:GT], prob[:, kt % 4, :, at:GT], ALU.add).then_inc(z_added, 1)
                    if item[0] == "V" and item[1] == 3 and item[2] % 4 == 3 and items is not final:
                        pool.wait_ge(pv_done, PV_CREDIT + score_step(g, 3, item[2]) + 1)
                        values(item[2] // 4, g + 1)

            for c in range(NGRP):
                values(c, 0)
            run(pool, work)

        @block.scalar
        def _(act):
            act.sem_inc(exp_ready, EXP_CREDIT)

            def work(items, g, r):
                for item in items:
                    if item[0] == "S":
                        _, c, kt, h = item
                        n = score_step(g, c, kt)
                        at = first_query(c, kt)
                        if h == 0:
                            act.wait_ge(pv_done, n + 1)
                            if second:
                                done = upto(c) + kt - (2 if c and kt == 4 else 3)
                                act.wait_ge(z_added, EXP_CREDIT + ADDS * g + adds_before(done))
                        act.wait_ge(s_psum, HG * n + h + 1)
                        act.activation(prob[:, kt % 4, h, at:GT], pS[:, s_bank(c, kt, h), at:GT], ACT.Exp, scale=SCALE).then_inc(exp_ready, 1)
                    if item[0] == "E":
                        c = item[1]
                        act.wait_ge(pv_done, PV_CREDIT + score_step(g, c, 4 * c + 4))
                        act.wait_ge(out_ready, 4 * g + c)
                        act.activation(oT[:, :], pO[:, :], ACT.Copy).then_inc(o_copied, 1)
            run(act, work)

        @block.vector
        def _(dve):
            dve.memset(q[-1][64:P].bitcast(FP32), 0.0).then_inc(q_filled, 1)
            dve.sem_inc(r_read, R_CREDIT)

            def work(items, g, r0):
                bank0 = bank_at_start[id(items)]
                used = 0
                for item in items:
                    r, bank = r0 + used, (bank0 + used) % NR
                    if item[0] == "R":
                        _, c, h, t, kc = item
                        used += 1
                        dve.wait_ge(r_psum, r + 1)
                        if kc < c:
                            dve.tensor_reduce(rowmax[:, c % 2, h, t, kc:kc + 1], pR[:, bank, :], axis=AX.X, op=ALU.max).then_inc(r_read, 1)
                        else:
                            n = P * (t + 1)
                            dve.sem_inc(dve_passed, 1)
                            dve.tensor_tensor_reduce(out=pR[:, bank, 0:n], in0=pR[:, bank, 0:n], in1=m.causal[:, GT - n:GT],
                                                     scale=1.0, scalar=-3e38, op0=ALU.add, op1=ALU.max,
                                                     accum_out=rowmax[:, c % 2, h, t, kc:kc + 1]).then_inc(r_read, 1)
                    if item[0] == "K":
                        used += 1
                        dve.wait_ge(r_read, R_CREDIT + r)
                        dve.sem_inc(r_read, 1)
                    if item[0] == "F":
                        c = item[1]
                        dve.wait_ge(r_read, R_CREDIT + r)
                        dve.tensor_reduce(fullmax[:, :], rowmax[:, c % 2, :, :, 0:c + 1].rearrange("p h t k -> p (h t) k"),
                                          axis=AX.X, op=ALU.max).then_inc(fullmax_ready, 1)
                    if item[0] == "M":
                        used += 1
                        count = max_count(items, g, item[1])
                        dve.wait_ge(r_psum, r + 1)
                        dve.wait_ge(neg_stored, 32 * count)
                        dve.tensor_scalar(neg_hi[:, :], pR[0:HG * NTILE, bank, 0:P], -1.0, None, ALU.mult).then_inc(neg_hi_ready, 1)
                        dve.wait_ge(neg_hi_ready, count + 1)
                        dve.scalar_tensor_tensor(out=neg_lo[:, :], in0=pR[0:HG * NTILE, bank, 0:P], scalar=-1.0, in1=neg_hi[:, :],
                                                 op0=ALU.mult, op1=ALU.subtract).then_inc(neg_ready, 1)
                        dve.wait_ge(neg_ready, count + 1)
                        dve.sem_inc(r_read, 1)
                    if item[0] == "O":
                        c = item[1]
                        used += 1
                        n = 4 * g + c
                        dve.wait_ge(r_psum, r + 1)
                        o = pR[:, bank, :].rearrange("p (t h f) -> p t h f", t=NTILE, h=HG)
                        dve.reciprocal(recip[:, :, :], o[:, :, :, HD1]).then_inc(recip_ready, 1)
                        dve.wait_ge(recip_ready, n + 1)
                        dve.wait_ge(out_stored[c % 2], 16 * (2 * g + c // 2))
                        dve.tensor_tensor(out[:, c % 2], o[:, :, :, 0:HD1],
                                          recip[:, :, :].unsqueeze(3).broadcast_to([P, NTILE, HG, HD1]), ALU.mult).then_inc(out_ready, 1)
                        dve.wait_ge(out_ready, n + 1)
                        dve.sem_inc(r_read, 1)
                    if item[0] == "N":
                        _, c, n = item
                        piece = slice(P * n, P * n + P)
                        if n == 0:
                            dve.wait_ge(z_psum, 4 * g + c + 1)
                            dve.wait_ge(o_copied, 4 * g + c + 1)
                            dve.wait_ge(out_stored[c % 2], 16 * (2 * g + c // 2))
                        dve.reciprocal(recip[:, piece], pZ[:, piece]).then_inc(recip_ready, 1)
                        dve.wait_ge(recip_ready, 4 * (4 * g + c) + n + 1)
                        ins = dve.tensor_tensor(out[:, c % 2, piece], oT[:, piece], recip[:, piece], ALU.mult)
                        if n == NTILE - 1:
                            ins.then_inc(out_ready, 1)
            run(dve, work)

        @block.tensor
        def _(pe):
            pe.sem_inc(pv_done, PV_CREDIT)
            pe.wait_ge(filled, FILLS)
            pe.wait_ge(q_filled, 1)

            def work(items, g, r0):
                bank0 = bank_at_start[id(items)]
                used = 0
                for item in items:
                    r, bank = r0 + used, (bank0 + used) % NR
                    if item[0] == "R":
                        _, c, h, t, kc = item
                        used += 1
                        step = g if c == 3 else g + 1
                        if h == 0 and t == 0:
                            if kc == 0:
                                pe.wait_ge(q_loaded[c], QL * (step + 1))
                            pe.wait_ge((kmax_loaded if c else first_loaded)[kc], KML * (step + 1))
                        pe.wait_ge(r_read, r + 1)
                        n = GT if kc < c else P * (t + 1)
                        pe.matmul(pR[:, bank, 0:n], q[0][0:MAX_ROWS, c, h, P * t:P * t + P],
                                  (kmax if c else kmax_first)[0:MAX_ROWS, h % KH, GT * kc:GT * kc + n], start=True, stop=True).then_inc(r_psum, 1)
                    if item[0] == "M":
                        used += 1
                        pe.wait_ge(r_read, r + 1)
                        pe.wait_ge(fullmax_ready, max_count(items, g, item[1]) + 1)
                        pe.transpose(pR[0:HG * NTILE, bank, 0:P], fullmax[:, :], m.eye[:, :]).then_inc(r_psum, 1)
                    if item[0] == "S":
                        _, c, kt, h = item
                        n = score_step(g, c, kt)
                        at = first_query(c, kt)
                        if kt == 0 and h == 0:
                            pe.wait_ge(neg_stored, 32 * (4 * g + 4 if c == 3 else 4 * g + c + 1))
                            pe.wait_ge(q_loaded[c], QL * (g + 1))
                        if kt >= 4 * c and kt % 4 == 0 and h == 0:
                            pe.wait_ge(key_loaded[kt // 4], KL * (g + 1))
                        diagonal = kt >= 4 * c
                        pe.wait_ge(exp_ready, EXP_CREDIT + HG * STEPS * g + bank_before(c, kt, h) + 1)
                        bank_s = s_bank(c, kt, h)
                        for s in range(STACKS):
                            mm = pe.matmul(pS[:, bank_s, at:GT], key[s][0:rows_exp[s], h % KH, P * kt:P * kt + P],
                                           q[s][0:rows_exp[s], c, h, at:GT], start=(s == 0), stop=(s == STACKS - 1 and not diagonal))
                        if diagonal:
                            mm = pe.matmul(pS[:, bank_s, at:at + P], m.after16[:, :], m.eye16[:, :], start=False, stop=True)
                        mm.then_inc(s_psum, 1)
                    if item[0] == "V":
                        _, c, kt = item
                        n = score_step(g, c, kt)
                        at = first_query(c, kt)
                        pe.wait_ge(exp_ready, EXP_CREDIT + HG * n + HG)
                        if kt >= 4 * c:
                            if kt % 4 == 0:
                                pe.wait_ge(val_ready, 4 * g + kt // 4 + 1)
                        if kt == 0:
                            pe.wait_ge(o_copied, 4 * g + c)
                        ends = kt == 4 * c + 3
                        for h in range(HG):
                            mm = pe.matmul(pO[32 * h:32 * h + 32, at:GT], val[:, kt, h % KH, :], prob[:, kt % 4, h, at:GT],
                                           start=(kt == 0), stop=ends)
                        if second and not by_pool(c, kt):
                            begins = kt == (3 if c else 0)
                            if begins:
                                pe.wait_ge(recip_ready, 4 * (4 * g + c))
                            for h in range(HG):
                                mm = pe.matmul(pZ[32 * h:32 * h + 32, at:GT], ones[:, :], prob[:, kt % 4, h, at:GT],
                                               start=begins, stop=(c == 0 and kt == 3))
                        mm.then_inc(pv_done, 1)
                    if item[0] == "Z":
                        c = item[1]
                        pe.wait_ge(z_added, EXP_CREDIT + ADDS * g + adds_before(upto(c + 1)))
                        if c == 0:
                            pe.wait_ge(pv_done, PV_CREDIT + score_step(g, 0, 4))
                            pe.sem_inc(z_psum, 1)
                            continue
                        for h in range(HG):
                            mm = pe.matmul(pZ[32 * h:32 * h + 32, :], ones[:, :], zsum[:, h, :], start=False, stop=True)
                        mm.then_inc(z_psum, 1)
                    if item[0] == "O":
                        used += 1
                        pe.wait_ge(r_read, r + 1)
                        pe.wait_ge(o_copied, 4 * g + item[1] + 1)
                        for t in range(NTILE):
                            mm = pe.transpose(pR[:, bank, P * t:P * t + P], oT[:, P * t:P * t + P], m.eye[:, :])
                        mm.then_inc(r_psum, 1)
                    if item[0] == "K":
                        used += 1
                        pe.wait_ge(r_psum, r)
                        pe.sem_inc(r_psum, 1)
            run(pe, work)


def project2(nc, d, m):
    with ExitStack() as ctx:
        sb = lambda n, s, t=FP32: ctx.enter_context(nc.sbuf_tensor("p2_" + n, s, t))
        sem = lambda n: nc.alloc_semaphore("p2_" + n)
        sems = lambda n: [sem(f"{n}{b}") for b in range(2)]
        G = HEADS // HG
        wq_hi, wq_lo = sb("wq_hi", [P, KT, 3, G, P], F32R), sb("wq_lo", [P, KT, 3, G, P], F32R)
        wk_hi, wk_lo = sb("wk_hi", [P, KT, 2, P], F32R), sb("wk_lo", [P, KT, 2, P], F32R)
        cos, sin = sb("cos", [P, 2, T]), sb("sin", [P, 2, T])
        with ExitStack() as inner:
            st = lambda n, s, t=FP32: inner.enter_context(nc.sbuf_tensor("p2_" + n, s, t))
            wr_st, wk_st = st("wr_st", [P, KT, 2, G, P]), st("wk_st", [P, KT, 2, P])
            wqn, kvb = st("wqn", [P, G, C]), st("kvb", [P, G, P])
            fold_weights(nc, "p2_fold", d, kvb,
                         [(wqn[:, :, :], d["wqnT"].rearrange("(g p) f -> p g f", p=P))],
                         [(wqn[:, g, P * k:P * k + P], kvb[:, g, :], wq_hi[:, k, 0, g, :], wq_lo[:, k, 0, g, :])
                          for g in range(G) for k in range(KT)])
            split_weights(nc, "p2_w", [
                ([(d["wqr"].rearrange("(k p) (s g n) -> p k s g n", p=P, s=2, g=G)[:, k], wr_st[:, k]) for k in range(KT)],
                 wr_st[:, :, :, :, :], wq_hi[:, :, 1:3], wq_lo[:, :, 1:3]),
                ([(d["wk"].rearrange("(k p) (s n) -> p k s n", p=P, s=2), wk_st[:, :, :, :])], wk_st[:, :, :, :], wk_hi[:, :, :, :], wk_lo[:, :, :, :])])
        u, o = sb("u", [P, B, NTILE, C]), sb("o", [P, B, NTILE, C])
        x1, xin = sb("x1", [P, B, NTILE, C]), sb("xin", [P, B, NTILE, C])
        xn = sb("xn", [P, B, NTILE, C])
        stats, mv = sb("stats", [P, B, NTILE, 6]), sb("mv", [P, B, NTILE, 2])
        ssq, sd, rstd = sb("ssq", [P, B, NTILE]), sb("sd", [P, B, NTILE]), sb("rstd", [P, B, NTILE])
        rsd, rrms = sb("rsd", [P, B, NTILE]), sb("rrms", [P, B, NTILE])
        squares = sb("squares", [P, NTILE, C])
        xT_hi, xT_lo = sb("xT_hi", [P, B, KT, GT], F32R), sb("xT_lo", [P, B, KT, GT], F32R)
        n_hi, n_lo = sb("n_hi", [P, 2, GT], F32R), sb("n_lo", [P, 2, GT], F32R)
        r_hi, r_lo = sb("r_hi", [P, 2, GT], F32R), sb("r_lo", [P, 2, GT], F32R)
        by_cos, by_sin, turned = sb("by_cos", [P, 2, GT]), sb("by_sin", [P, 2, GT]), sb("turned", [P, 2, GT])
        pT = ctx.enter_context(nc.psum_tensor("p2_pT", [P, KT, GT], FP32))
        pN = ctx.enter_context(nc.psum_tensor("p2_pN", [P, 2, GT], FP32))
        pR = ctx.enter_context(nc.psum_tensor("p2_pR", [P, 2, 2, GT], FP32))
        pL = pT[:, 0, 0:NTILE * LAT].rearrange("p (t r) -> p t r", t=NTILE)
        loaded, stored = sems("loaded"), sems("stored")
        gated, x1_ready, var_ready, sd_ready, rstd_ready, unit_ready, scaled, xin_ready = (
            sem(n) for n in ("gated", "x1_ready", "var_ready", "sd_ready", "rstd_ready", "unit_ready", "scaled", "xin_ready"))
        ssq_ready, ms_ready, rms_ready, rrms_ready, xn_ready = (
            sem(n) for n in ("ssq_ready", "ms_ready", "rms_ready", "rrms_ready", "xn_ready"))
        t_psum, hi_ready, lo_ready = sem("t_psum"), sem("hi_ready"), sem("lo_ready")
        n_psum, n_hi_ready, n_lo_ready, n_stored = sem("n_psum"), sem("n_hi_ready"), sem("n_lo_ready"), sems("n_stored")
        r_psum, r_read, turned_ready = sem("r_psum"), sem("r_read"), sem("turned_ready")
        r_hi_ready, r_lo_ready, r_stored = sem("r_hi_ready"), sem("r_lo_ready"), sems("r_stored")
        l_psum, l_read = sem("l_psum"), sem("l_read")
        stats_ready, passed, sp_passed = sem("stats_ready"), sem("passed"), sem("sp_passed")
        tables_loaded, pe_passed = sem("tables_loaded"), sem("pe_passed")
        block = ctx.enter_context(nc.Block())
        RING = 2
        tok = lambda name: d[name].rearrange("b (i t p) c -> b i p t c", t=NTILE, p=P)
        spread = lambda b, v: m.mod[:, b, v, :].unsqueeze(1).broadcast_to([P, NTILE, C])
        PIECES = G + 1

        def order(products, front):
            after = {0: "B", 1: "CD", 2: "S", 3: "M", 4: "T"}
            items = [("A", 0)] if front else []
            for p in range(PIECES) if products else ():
                items += [("N", p - 1)] * (p > 0) + [("Q", p)] + [("L", 0)] * (p == 1) + [(x, 0) for x in (after[p] if front else "")]
            return items if products else [(x, 0) for x in "ABCDSMT"]

        def run(eng, work):
            work(order(False, True), -1, 1, 0, 0)
            with eng.Fori(0, NGRP - 1) as i:
                for b in range(B):
                    work(order(True, True), i, b, i + b, 1 - b)
            work(order(True, True), NGRP - 1, 0, NGRP - 1, 1)
            work(order(True, False), NGRP - 1, 1, 0, 0)

        @block.sync
        def _(sp):
            def load(i, b):
                sp.dma_start(u[:, b], tok("u1")[b, bass.ds(i, 1)].rearrange("a p t c -> (a p) t c")).then_inc(loaded[b], 16)
                for g in range(G):
                    src = d["o1"][4 * b + g, bass.ds(i * GT, GT)].rearrange("(t p) f -> p t f", p=P)
                    sp.dma_start(o[:, b, :, 64 * g:64 * g + 64], src).then_inc(loaded[b], 16)

            def work(items, i, b, fi, fb):
                n, fn = 2 * i + b, 2 * fi + fb
                for step, g in items:
                    if step == "A":
                        if ("Q", 0) not in items:
                            load(0, 0)
                            load(0, 1)
                    if step == "D":
                        sp.wait_ge(xin_ready, fn + 1)
                        sp.dma_start(tok("xin")[fb, bass.ds(fi, 1)].rearrange("a p t c -> (a p) t c"), xin[:, fb]).then_inc(stored[fb], 16)
                        sp.dma_start(tok("x1")[fb, bass.ds(fi, 1)].rearrange("a p t c -> (a p) t c"), x1[:, fb]).then_inc(stored[fb], 16)
                    cols = bass.ds(i * GT, GT)
                    if step == "N":
                        sp.wait_ge(n_lo_ready, RING + G * n + g + 1)
                        sp.sem_inc(sp_passed, 1)
                        for s, half in enumerate((n_hi, n_lo)):
                            sp.dma_start(d["q2"][4 * b + g, s, 0, :, cols], half[:, g % 2, :].bitcast(FP32)).then_inc(n_stored[g % 2], 16)
                    if step == "Q":
                        ring = (b + g) % 2
                        sp.wait_ge(r_lo_ready, PIECES * n + g + 1)
                        sp.sem_inc(sp_passed, 1)
                        for s, half in enumerate((r_hi, r_lo)):
                            dst, rows = (d["q2"][4 * b + g - 1, s, 1, :, cols], P) if g else (d["k2"][b, s, :, cols], LAT + ROPE)
                            sp.dma_start(dst, half[0:rows, ring, :].bitcast(FP32)).then_inc(r_stored[ring], 16)

            work(order(False, True), -1, 1, 0, 0)
            with sp.Fori(0, NGRP - 1) as i:
                for b in range(B):
                    sp.wait_ge(x1_ready, 2 * i + b + 1)
                    sp.sem_inc(sp_passed, 1)
                    load(i + 1, b)
                    work(order(True, True), i, b, i + b, 1 - b)
            work(order(True, True), NGRP - 1, 0, NGRP - 1, 1)
            work(order(True, False), NGRP - 1, 1, 0, 0)
            for b in range(B):
                sp.wait_ge(stored[b], 32 * NGRP)
                sp.wait_ge(n_stored[b], 16 * G * B * NGRP)
                sp.wait_ge(r_stored[b], 16 * PIECES * B * NGRP)

        @block.gpsimd
        def _(pool):
            pool.sem_inc(turned_ready, RING)

            def work(items, i, b, fi, fb):
                n, fn = 2 * i + b, 2 * fi + fb
                for step, g in items:
                    if step == "A":
                        pool.wait_ge(loaded[fb], 16 * (G + 1) * (fi + 1))
                        pool.wait_ge(stored[fb], 32 * fi)
                        pool.tensor_tensor(x1[:, fb], o[:, fb], spread(fb, 2), ALU.mult).then_inc(gated, 1)
                        pool.wait_ge(gated, fn + 1)
                        pool.tensor_tensor(x1[:, fb], x1[:, fb], u[:, fb], ALU.add).then_inc(x1_ready, 1)
                    if step == "D":
                        pool.wait_ge(unit_ready, fn + 1)
                        pool.tensor_tensor(xin[:, fb], xin[:, fb], spread(fb, 4), ALU.mult).then_inc(scaled, 1)
                        pool.wait_ge(scaled, fn + 1)
                        pool.tensor_tensor(xin[:, fb], xin[:, fb], spread(fb, 3), ALU.add).then_inc(xin_ready, 1)
                    if step == "Q":
                        ring = (b + g) % 2
                        piece = PIECES * n + g
                        pool.wait_ge(r_read, RING + piece + 1)
                        if g == 2:
                            pool.wait_ge(l_psum, n + 1)
                        pool.tensor_tensor(turned[:, ring, :], by_cos[:, ring, :], by_sin[:, ring, :], ALU.add).then_inc(turned_ready, 1)
            run(pool, work)

        @block.scalar
        def _(act):
            act.dma_start(cos[:, :, :], d["cos"]).then_inc(tables_loaded, 16)
            act.dma_start(sin[:, :, :], d["sin"]).then_inc(tables_loaded, 16)

            def work(items, i, b, fi, fb):
                n, fn = 2 * i + b, 2 * fi + fb
                for step, g in items:
                    if step == "B":
                        act.wait_ge(var_ready, fn + 1)
                        act.activation(sd[:, fb], mv[:, fb, :, 1], ACT.Sqrt).then_inc(sd_ready, 1)
                    if step == "S":
                        act.wait_ge(xin_ready, fn + 1)
                        for t in range(NTILE):
                            last = act.activation(squares[:, t, :], xin[:, fb, t, :], ACT.Square, accum_out=ssq[:, fb, t:t + 1])
                        last.then_inc(ssq_ready, 1)
                    if step == "M":
                        act.wait_ge(ms_ready, fn + 1)
                        act.activation(rsd[:, fb], ssq[:, fb], ACT.Sqrt).then_inc(rms_ready, 1)
                    if step == "T":
                        for k in range(KT):
                            act.wait_ge(t_psum, KT * fn + k + 1)
                            act.activation(xT_hi[:, fb, k, :], pT[:, k, :], ACT.Copy, scale=m.wln[:, 0, k:k + 1]).then_inc(hi_ready, 1)
                    if step == "N":
                        act.wait_ge(n_psum, G * n + g + 1)
                        act.wait_ge(n_stored[g % 2], 32 * (2 * n + g // 2))
                        act.activation(n_hi[:, g % 2, :], pN[:, g % 2, :], ACT.Copy).then_inc(n_hi_ready, 1)
                    for piece in ([g] if step == "N" else [G] if step == "Q" and g == G else []):
                        ring = (b + piece) % 2
                        act.wait_ge(turned_ready, RING + PIECES * n + piece + 1)
                        act.wait_ge(r_stored[ring], 32 * (PIECES * i + (PIECES * b + piece) // 2))
                        act.activation(r_hi[:, ring, :], turned[:, ring, :], ACT.Copy).then_inc(r_hi_ready, 1)
            run(act, work)

        @block.vector
        def _(dve):
            dve.sem_inc(r_read, RING)
            dve.sem_inc(n_lo_ready, RING)

            def split_turned(n, b, g):
                ring = (b + g) % 2
                dve.wait_ge(r_hi_ready, PIECES * n + g + 1)
                dve.tensor_tensor(r_lo[:, ring, :], turned[:, ring, :], r_hi[:, ring, :], ALU.subtract).then_inc(r_lo_ready, 1)

            def work(items, i, b, fi, fb):
                n, fn = 2 * i + b, 2 * fi + fb
                for step, g in items:
                    if step == "B":
                        dve.wait_ge(x1_ready, fn + 1)
                        for t in range(NTILE):
                            last = dve.bn_stats(stats[:, fb, t, :], x1[:, fb, t, :])
                        last.then_inc(stats_ready, 1)
                        dve.wait_ge(stats_ready, 2 * fn + 1)
                        dve.sem_inc(passed, 1)
                        for t in range(NTILE):
                            last = dve.bn_aggr(mv[:, fb, t, :], stats[:, fb, t, :])
                        last.then_inc(stats_ready, 1)
                        dve.wait_ge(stats_ready, 2 * fn + 2)
                        dve.tensor_scalar(mv[:, fb, :, 1], mv[:, fb, :, 1], EPS, None, ALU.add).then_inc(var_ready, 1)
                    if step == "C":
                        dve.wait_ge(sd_ready, fn + 1)
                        dve.reciprocal(rstd[:, fb], sd[:, fb]).then_inc(rstd_ready, 1)
                        dve.wait_ge(rstd_ready, fn + 1)
                        dve.wait_ge(stored[fb], 32 * fi)
                        for t in range(NTILE):
                            last = dve.tensor_scalar(xin[:, fb, t, :], x1[:, fb, t, :], mv[:, fb, t, 0:1], rstd[:, fb, t:t + 1],
                                                     ALU.subtract, ALU.mult)
                        last.then_inc(unit_ready, 1)
                    if step == "M":
                        dve.wait_ge(ssq_ready, fn + 1)
                        dve.tensor_scalar(ssq[:, fb], ssq[:, fb], 1.0 / C, EPS, ALU.mult, ALU.add).then_inc(ms_ready, 1)
                        dve.wait_ge(rms_ready, fn + 1)
                        dve.reciprocal(rrms[:, fb], rsd[:, fb]).then_inc(rrms_ready, 1)
                        dve.wait_ge(rrms_ready, fn + 1)
                        for t in range(NTILE):
                            last = dve.tensor_scalar(xn[:, fb, t, :], xin[:, fb, t, :], rrms[:, fb, t:t + 1], None, ALU.mult)
                        last.then_inc(xn_ready, 1)
                    if step == "T":
                        for k in range(KT):
                            dve.wait_ge(hi_ready, KT * fn + k + 1)
                            dve.scalar_tensor_tensor(out=xT_lo[:, fb, k, :], in0=pT[:, k, :], scalar=m.wln[:, 0, k:k + 1],
                                                     in1=xT_hi[:, fb, k, :], op0=ALU.mult, op1=ALU.subtract).then_inc(lo_ready, 1)
                    if step == "L":
                        dve.wait_ge(l_psum, n + 1)
                        dve.tensor_copy(m.lat[:, bass.ds(i * NTILE + b * (T // P), NTILE), :], pL).then_inc(l_read, 1)
                    if step == "N":
                        dve.wait_ge(n_hi_ready, G * n + g + 1)
                        dve.tensor_tensor(n_lo[:, g % 2, :], pN[:, g % 2, :], n_hi[:, g % 2, :], ALU.subtract).then_inc(n_lo_ready, 1)
                    if step == "Q":
                        ring, table = (b + g) % 2, int(g == 0)
                        piece = PIECES * n + g
                        cols = bass.ds(i * GT, GT)
                        dve.wait_ge(r_psum, piece + 1)
                        dve.wait_ge(turned_ready, piece + 1)
                        dve.wait_ge(tables_loaded, 32)
                        dve.tensor_tensor(by_cos[:, ring, :], pR[:, ring, 0, :], cos[:, table, cols], ALU.mult)
                        dve.tensor_tensor(by_sin[:, ring, :], pR[:, ring, 1, :], sin[:, table, cols], ALU.mult).then_inc(r_read, 1)
                        if g:
                            split_turned(n, b, g - 1)
                        if g == G:
                            split_turned(n, b, g)
            run(dve, work)

        @block.tensor
        def _(pe):
            def work(items, i, b, fi, fb):
                n, fn = 2 * i + b, 2 * fi + fb
                for step, g in items:
                    if step == "T":
                        pe.wait_ge(xn_ready, fn + 1)
                        pe.wait_ge(l_read, fn)
                        for k in range(KT):
                            for t in range(NTILE):
                                mm = pe.transpose(pT[:, k, P * t:P * t + P], xn[:, fb, t, P * k:P * k + P], m.eye[:, :])
                            mm.then_inc(t_psum, 1)
                    if step == "L":
                        pe.wait_ge(turned_ready, RING + PIECES * n + 1)
                        pe.sem_inc(pe_passed, 1)
                        for t in range(NTILE):
                            mm = pe.transpose(pT[:, 0, LAT * t:LAT * t + LAT], turned[0:LAT, b, P * t:P * t + P], m.eye[0:LAT, 0:LAT])
                        mm.then_inc(l_psum, 1)
                    if step == "N":
                        pe.wait_ge(n_lo_ready, G * n + g + 1)
                        for k in range(KT):
                            mm = product3(pe, pN[:, g % 2, :], wq_hi[:, k, 0, g, :], wq_lo[:, k, 0, g, :],
                                          xT_hi[:, b, k, :], xT_lo[:, b, k, :], k == 0, k == KT - 1)
                        mm.then_inc(n_psum, 1)
                    if step == "Q":
                        ring = (b + g) % 2
                        if g == 0:
                            pe.wait_ge(lo_ready, KT * n + KT)
                        pe.wait_ge(r_read, PIECES * n + g + 1)
                        for s in range(2):
                            for k in range(KT):
                                hi, lo = ((wq_hi[:, k, 1 + s, g - 1, :], wq_lo[:, k, 1 + s, g - 1, :]) if g
                                          else (wk_hi[:, k, s, :], wk_lo[:, k, s, :]))
                                mm = product3(pe, pR[:, ring, s, :], hi, lo, xT_hi[:, b, k, :], xT_lo[:, b, k, :], k == 0, k == KT - 1)
                        mm.then_inc(r_psum, 1)
            run(pe, work)


def fold_weights(nc, name, d, kvb, loads, jobs):
    with ExitStack() as ctx:
        sem = lambda n: nc.alloc_semaphore(name + n)
        ps = ctx.enter_context(nc.psum_tensor(name + "_ps", [P, 2, GT], FP32))
        zeroed, loaded, product, high, low = (sem(n) for n in ("_zeroed", "_loaded", "_product", "_high", "_low"))
        block = ctx.enter_context(nc.Block())

        @block.gpsimd
        def _(pool):
            pool.memset(kvb[:, :, :], 0.0).then_inc(zeroed, 1)

        @block.sync
        def _(sp):
            sp.wait_ge(zeroed, 1)
            src = d["wkvbT"].rearrange("(g j n) r -> j n g r", j=HG, n=32)
            for j in range(HG):
                sp.dma_start(kvb[32 * j:32 * j + 32, :, 32 * j:32 * j + 32], src[j]).then_inc(loaded, 16)
            for dst, src in loads:
                sp.dma_start(dst, src).then_inc(loaded, 16)

        @block.tensor
        def _(pe):
            pe.wait_ge(loaded, 16 * (HG + len(loads)))
            for n, (left, right, hi, lo) in enumerate(jobs):
                if n >= 2:
                    pe.wait_ge(low, n - 1)
                pe.matmul(ps[:, n % 2, 0:right.shape[-1]], left, right, start=True, stop=True).then_inc(product, 1)

        @block.scalar
        def _(act):
            for n, (left, right, hi, lo) in enumerate(jobs):
                act.wait_ge(product, n + 1)
                act.activation(hi, ps[:, n % 2, 0:right.shape[-1]], ACT.Copy).then_inc(high, 1)

        @block.vector
        def _(dve):
            for n, (left, right, hi, lo) in enumerate(jobs):
                dve.wait_ge(high, n + 1)
                dve.tensor_tensor(lo, ps[:, n % 2, 0:right.shape[-1]], hi, ALU.subtract).then_inc(low, 1)


def experts(nc, d, m):
    with ExitStack() as ctx:
        sb = lambda n, s, t=FP32: ctx.enter_context(nc.sbuf_tensor("e_" + n, s, t))
        sem = lambda n: nc.alloc_semaphore("e_" + n)
        sems = lambda n: [sem(f"{n}{b}") for b in range(2)]
        G, EX = HEADS // HG, E + 1
        wo_hi, wo_lo = sb("wo_hi", [P, G, C], F32R), sb("wo_lo", [P, G, C], F32R)
        wg_hi, wg_lo = sb("wg_hi", [P, KT, EX, I], F32R), sb("wg_lo", [P, KT, EX, I], F32R)
        wu_hi, wu_lo = sb("wu_hi", [P, KT, EX, I], F32R), sb("wu_lo", [P, KT, EX, I], F32R)
        wd_hi, wd_lo = sb("wd_hi", [P, EX, C], F32R), sb("wd_lo", [P, EX, C], F32R)
        gate_hi, gate_lo = sb("gate_hi", [P, KT, E], F32R), sb("gate_lo", [P, KT, E], F32R)
        sel_st = sb("sel_st", [64, E, P])
        sel = sb("sel", [64, E, P], F32R)
        rank = sb("rank", [P, E])
        with ExitStack() as inner:
            st = lambda n, s, t=FP32: inner.enter_context(nc.sbuf_tensor("e_" + n, s, t))
            wo, kvb = st("wo", [P, G, C]), st("kvb", [P, G, P])
            fold_weights(nc, "e_fold", d, kvb,
                         [(wo[32 * j:32 * j + 32, :, :], d["Wo"].rearrange("(g j n) c -> j n g c", j=HG, n=HD2)[j, 0:32])
                          for j in range(HG)] + [(sel_st[:, :, :], d["sel"].rearrange("k (e p) -> k e p", e=E)),
                                                 (rank[:, :], d["rank"].rearrange("(a n) -> a n", a=1).broadcast_to([P, E]))],
                         [(kvb[:, g, :], wo[:, g, :], wo_hi[:, g, :], wo_lo[:, g, :]) for g in range(G)])
        split_weights(nc, "e_w", [([], m.wg[:, :, :, :], wg_hi[:, :, :, :], wg_lo[:, :, :, :]),
                                  ([], m.wu[:, :, :, :], wu_hi[:, :, :, :], wu_lo[:, :, :, :]),
                                  ([], m.wd[:, :, :], wd_hi[:, :, :], wd_lo[:, :, :]),
                                  ([], m.gate[:, :, :], gate_hi[:, :, :], gate_lo[:, :, :])])
        o_st = m.wg[:, :, :, :].rearrange("p k e i -> p (k e i)")[:, 0:G * GT].rearrange("p (g t) -> p g t", g=G)
        y = m.wu[:, :, :, :].rearrange("p k e i -> p (k e i)")[:, 0:B * NTILE * C].rearrange("p (b t c) -> p b t c", b=B, t=NTILE)
        o_hi, o_lo = sb("o_hi", [P, G, GT], F32R), sb("o_lo", [P, G, GT], F32R)
        xin, x1, x2 = sb("xin", [P, B, NTILE, C]), sb("x1", [P, B, NTILE, C]), sb("x2", [P, B, NTILE, C])
        xn, squares = sb("xn", [P, NTILE, C]), sb("squares", [P, NTILE, C])
        ssq, rms, rrms = sb("ssq", [P, NTILE]), sb("rms", [P, NTILE]), sb("rrms", [P, NTILE])
        xT_hi, xT_lo = sb("xT_hi", [P, B, KT, GT], F32R), sb("xT_lo", [P, B, KT, GT], F32R)
        logit, pick1, pick2 = sb("logit", [P, NTILE, E]), sb("pick1", [P, NTILE, E]), sb("pick2", [P, NTILE, E])
        top, best = sb("top", [P, 2, NTILE]), sb("best", [P, NTILE])
        gap, weight = sb("gap", [P, 2, NTILE]), sb("weight", [P, 2, NTILE])
        comb = sb("comb", [P, NTILE, E])
        combT = sb("combT", [64, B, GT], F32R)
        silu, prod = sb("silu", [P, 2, GT]), sb("prod", [P, 2, GT])
        p_hi, p_lo = sb("p_hi", [P, 2, GT], F32R), sb("p_lo", [P, 2, GT], F32R)
        pPair = ctx.enter_context(nc.psum_tensor("e_pPair", [P, 2, 2, GT], FP32))
        pD = ctx.enter_context(nc.psum_tensor("e_pD", [P, NTILE, C], FP32))
        pB = ctx.enter_context(nc.psum_tensor("e_pB", [P, GT], FP32))
        pG = ctx.enter_context(nc.psum_tensor("e_pG", [P, GT], FP32))

        filled, sel_ready, sp_passed = sem("filled"), sem("sel_ready"), sem("sp_passed")
        o_loaded, x_loaded, out_stored = sem("o_loaded"), sems("x_loaded"), sems("out_stored")
        x1_loaded, gate_psum = sems("x1_loaded"), sem("gate_psum")
        o_hi_ready, o_lo_ready = sem("o_hi_ready"), sem("o_lo_ready")
        pair_psum, pair_read = sem("pair_psum"), sem("pair_read")
        x2_ready, ssq_ready, ms_ready, rms_ready, xn_ready = sem("x2_ready"), sem("ssq_ready"), sem("ms_ready"), sem("rms_ready"), sem("xn_ready")
        xT_hi_ready, xT_ready = sem("xT_hi_ready"), sem("xT_ready")
        g_psum, g_read, chain = sem("g_psum"), sem("g_read"), sem("chain")
        gap_ready, weight_ready, comb_ready, combT_hi_ready, combT_ready = (
            sem("gap_ready"), sem("weight_ready"), sem("comb_ready"), sem("combT_hi_ready"), sem("combT_ready"))
        b_psum, b_read = sem("b_psum"), sem("b_read")
        silu_ready, prod_ready, p_hi_ready, p_lo_ready = sem("silu_ready"), sem("prod_ready"), sem("p_hi_ready"), sem("p_lo_ready")
        down_done, y_sum, y_scaled, y_ready = sem("down_done"), sem("y_sum"), sem("y_scaled"), sem("y_ready")
        block = ctx.enter_context(nc.Block())
        RING = 2

        FRONT = ("P", "A", "N", "R", "X", "L", "W", "C")

        def order(experts_too, front):
            after = {0: "P", 2: "A", 3: "NR", 4: "X", 5: "L", 6: "W", 7: "C"}
            if not experts_too:
                return [(s, 0) for s in FRONT]
            items = []
            for j in range(EX):
                items.append(("G", j))
                if j < E:
                    items.append(("B", j))
                items.append(("U", j))
                if j:
                    items.append(("D", j - 1))
                if front:
                    items += [(s, 0) for s in after.get(j, "")]
            return items + [("D", E), ("Y", 0)]

        PAIRS = EX + 2

        def run(eng, work):
            work(order(False, True), -1, 1, 0, 0, 0, 0)
            with eng.Fori(0, NGRP - 1) as i:
                for b in range(B):
                    work(order(True, True), i, b, i + b, 1 - b, 2 + PAIRS * (2 * i + b), b)
            i = NGRP - 1
            work(order(True, True), i, 0, i, 1, 2 + PAIRS * 2 * i, 0)
            work(order(True, False), i, 1, 0, 0, 2 + PAIRS * (2 * i + 1), 1)

        tok = lambda name, b, i: d[name].rearrange("b (i t p) c -> b i p t c", t=NTILE, p=P)[b, bass.ds(i, 1)].rearrange("a p t c -> (a p) t c")

        @block.sync
        def _(sp):
            def work(items, i, b, fi, fb, pair, parity):
                if ("P", 0) in items:
                    fn = 2 * fi + fb
                    sp.wait_ge(o_lo_ready, fn)
                    sp.sem_inc(sp_passed, 1)
                    sp.dma_start(o_st[:, :, :], d["o2"][4 * fb:4 * fb + 4, :, bass.ds(fi * GT, GT)].rearrange("g p t -> p g t")).then_inc(o_loaded, 16)
                    if ("Y", 0) in items:
                        sp.wait_ge(x2_ready, 2 * i + b)
                        sp.sem_inc(sp_passed, 1)
                    sp.dma_start(xin[:, fb], tok("xin", fb, fi)).then_inc(x_loaded[fb], 16)
                    if ("Y", 0) in items:
                        sp.wait_ge(y_ready, 2 * i + b)
                        sp.sem_inc(sp_passed, 1)
                    sp.dma_start(x1[:, fb], tok("x1", fb, fi)).then_inc(x1_loaded[fb], 16)
                if ("Y", 0) in items:
                    sp.wait_ge(y_ready, 2 * i + b + 1)
                    sp.sem_inc(sp_passed, 1)
                    sp.dma_start(tok("out", b, i), y[:, b]).then_inc(out_stored[b], 16)
            run(sp, work)
            for b in range(B):
                sp.wait_ge(out_stored[b], 16 * NGRP)

        @block.gpsimd
        def _(pool):
            pool.memset(combT[:, :, :].bitcast(FP32), 0.0).then_inc(filled, 1)

            def work(items, i, b, fi, fb, pair, parity):
                n, fn = 2 * i + b, 2 * fi + fb
                for step, j in items:
                    if step == "P":
                        pool.wait_ge(o_hi_ready, fn + 1)
                        pool.tensor_tensor(o_lo[:, :, :], o_st[:, :, :], o_hi[:, :, :], ALU.subtract).then_inc(o_lo_ready, 1)
                    if step == "Y":
                        pool.wait_ge(y_sum, n + 1)
                        pool.tensor_tensor(y[:, b], y[:, b], m.mod[:, b, 5, :].unsqueeze(1).broadcast_to([P, NTILE, C]),
                                           ALU.mult).then_inc(y_scaled, 1)
                        pool.wait_ge(y_scaled, n + 1)
                        pool.wait_ge(x1_loaded[b], 16 * (i + 1))
                        pool.tensor_tensor(y[:, b], y[:, b], x1[:, b], ALU.add).then_inc(y_ready, 1)
            run(pool, work)

        @block.scalar
        def _(act):
            act.activation(sel[:, :, :], sel_st[:, :, :], ACT.Copy).then_inc(sel_ready, 1)

            def work(items, i, b, fi, fb, pair, parity):
                n, fn = 2 * i + b, 2 * fi + fb
                used = 0
                for step, j in items:
                    use, s = EX * n + j, (b + j) % 2
                    if step == "P":
                        act.wait_ge(o_loaded, 16 * (fn + 1))
                        act.wait_ge(x2_ready, fn)
                        act.activation(o_hi[:, :, :], o_st[:, :, :], ACT.Copy).then_inc(o_hi_ready, 1)
                    if step == "N":
                        act.wait_ge(x2_ready, fn + 1)
                        for t in range(NTILE):
                            last = act.activation(squares[:, t, :], x2[:, fb, t, :], ACT.Square, accum_out=ssq[:, t:t + 1])
                        last.then_inc(ssq_ready, 1)
                    if step == "R":
                        act.wait_ge(ms_ready, fn + 1)
                        act.activation(rms[:, :], ssq[:, :], ACT.Sqrt).then_inc(rms_ready, 1)
                    if step == "X":
                        act.wait_ge(pair_psum, pair + used + 1)
                        for k in range(KT):
                            last = act.activation(xT_hi[:, fb, k, :], pPair[:, (parity + used) % 2, k, :], ACT.Copy, scale=m.wln[:, 1, k:k + 1])
                        last.then_inc(xT_hi_ready, 1)
                    if step == "W":
                        act.wait_ge(gap_ready, fn + 1)
                        act.activation(weight[:, :, :], gap[:, :, :], ACT.Sigmoid).then_inc(weight_ready, 1)
                    if step == "C":
                        act.wait_ge(g_psum, 2 * fn + 2)
                        act.activation(combT[0:E, fb, :], pG[0:E, :], ACT.Copy).then_inc(combT_hi_ready, 1)
                    if step == "G":
                        act.wait_ge(gate_psum, use + 1)
                        act.wait_ge(prod_ready, use + 1)
                        act.activation(silu[:, s, :], pPair[:, (parity + used) % 2, 0, :], ACT.Silu).then_inc(silu_ready, 1)
                    if step == "U":
                        act.wait_ge(prod_ready, RING + use + 1)
                        act.wait_ge(down_done, use + 1)
                        act.activation(p_hi[:, s, :], prod[:, s, :], ACT.Copy).then_inc(p_hi_ready, 1)
                    used += step in "UAX"
            run(act, work)

        @block.vector
        def _(dve):
            dve.sem_inc(prod_ready, RING)
            dve.sem_inc(p_lo_ready, RING)
            dve.sem_inc(pair_read, RING)
            dve.sem_inc(g_read, 1)
            dve.sem_inc(b_read, 1)
            LINKS = 11

            def work(items, i, b, fi, fb, pair, parity):
                n, fn = 2 * i + b, 2 * fi + fb
                used, links = 0, 0
                per_token = lambda t: t.unsqueeze(2).broadcast_to([P, NTILE, E])

                def low_half(n, b, j):
                    use, s = EX * n + j, (b + j) % 2
                    dve.wait_ge(p_hi_ready, use + 1)
                    dve.wait_ge(down_done, use + 1)
                    dve.tensor_tensor(p_lo[:, s, :], prod[:, s, :], p_hi[:, s, :], ALU.subtract).then_inc(p_lo_ready, 1)

                for step, j in items:
                    use, s = EX * n + j, (b + j) % 2
                    q = (parity + used) % 2
                    if step == "A":
                        dve.wait_ge(pair_psum, pair + used + 1)
                        dve.wait_ge(x_loaded[fb], 16 * (fi + 1))
                        dve.tensor_tensor(x2[:, fb], xin[:, fb], pPair[:, q, :, :].rearrange("p k (t c) -> p (k t) c", c=C),
                                          ALU.add).then_inc(x2_ready, 1)
                        dve.wait_ge(x2_ready, fn + 1)
                        dve.sem_inc(pair_read, 1)
                    if step == "R":
                        dve.wait_ge(ssq_ready, fn + 1)
                        dve.tensor_scalar(ssq[:, :], ssq[:, :], 1.0 / C, EPS, ALU.mult, ALU.add).then_inc(ms_ready, 1)
                        dve.wait_ge(rms_ready, fn + 1)
                        dve.reciprocal(rrms[:, :], rms[:, :]).then_inc(chain, 1)
                        dve.wait_ge(chain, LINKS * fn + 1)
                        for t in range(NTILE):
                            last = dve.tensor_scalar(xn[:, t, :], x2[:, fb, t, :], rrms[:, t:t + 1], None, ALU.mult)
                        last.then_inc(xn_ready, 1)
                    if step == "X":
                        dve.wait_ge(xT_hi_ready, fn + 1)
                        for k in range(KT):
                            last = dve.scalar_tensor_tensor(out=xT_lo[:, fb, k, :], in0=pPair[:, q, k, :], scalar=m.wln[:, 1, k:k + 1],
                                                            in1=xT_hi[:, fb, k, :], op0=ALU.mult, op1=ALU.subtract)
                        last.then_inc(xT_ready, 1)
                        dve.wait_ge(xT_ready, fn + 1)
                        dve.sem_inc(pair_read, 1)
                    if step == "L":
                        links = 1

                        def link(ins):
                            nonlocal links
                            links += 1
                            ins.then_inc(chain, 1)
                            dve.wait_ge(chain, LINKS * fn + links)

                        dve.wait_ge(g_psum, 2 * fn + 1)
                        dve.tensor_tensor(logit[:, :, :], pG[:, 0:NTILE * E].rearrange("p (t e) -> p t e", e=E),
                                          m.ebias[:, :].unsqueeze(1).broadcast_to([P, NTILE, E]), ALU.add).then_inc(g_read, 1)
                        dve.wait_ge(g_read, 1 + 2 * fn + 1)
                        for c, pick in enumerate((pick1, pick2)):
                            link(dve.tensor_reduce(top[:, c, :], logit[:, :, :], axis=AX.X, op=ALU.max))
                            link(dve.tensor_tensor(pick[:, :, :], logit[:, :, :], per_token(top[:, c, :]), ALU.is_equal))
                            link(dve.tensor_tensor(pick[:, :, :], pick[:, :, :], rank[:, :].unsqueeze(1).broadcast_to([P, NTILE, E]), ALU.mult))
                            link(dve.tensor_reduce(best[:, :], pick[:, :, :], axis=AX.X, op=ALU.max))
                            if c == 0:
                                link(dve.tensor_tensor(pick[:, :, :], pick[:, :, :], per_token(best[:, :]), ALU.is_equal))
                                link(dve.scalar_tensor_tensor(out=logit[:, :, :], in0=pick[:, :, :], scalar=NEG, in1=logit[:, :, :],
                                                              op0=ALU.mult, op1=ALU.add))
                            else:
                                dve.tensor_tensor(pick[:, :, :], pick[:, :, :], per_token(best[:, :]), ALU.is_equal)
                        dve.tensor_tensor(gap[:, 0, :], top[:, 0, :], top[:, 1, :], ALU.subtract)
                        dve.tensor_tensor(gap[:, 1, :], top[:, 1, :], top[:, 0, :], ALU.subtract).then_inc(gap_ready, 1)
                        assert links == LINKS
                    if step == "W":
                        dve.wait_ge(weight_ready, fn + 1)
                        dve.tensor_tensor(pick1[:, :, :], pick1[:, :, :], per_token(weight[:, 0, :]), ALU.mult)
                        dve.tensor_tensor(pick2[:, :, :], pick2[:, :, :], per_token(weight[:, 1, :]), ALU.mult).then_inc(comb_ready, 1)
                        dve.wait_ge(comb_ready, 2 * fn + 1)
                        dve.tensor_tensor(comb[:, :, :], pick1[:, :, :], pick2[:, :, :], ALU.add).then_inc(comb_ready, 1)
                    if step == "C":
                        dve.wait_ge(combT_hi_ready, fn + 1)
                        dve.tensor_tensor(combT[32:32 + E, fb, :], pG[0:E, :], combT[0:E, fb, :], ALU.subtract).then_inc(combT_ready, 1)
                        dve.wait_ge(combT_ready, fn + 1)
                        dve.sem_inc(g_read, 1)
                    if step in "BU" and j and (step == "B" or j == E):
                        low_half(n, b, j - 1)
                    if step == "B":
                        dve.wait_ge(silu_ready, use + 1)
                        dve.wait_ge(b_psum, E * n + j + 1)
                        dve.wait_ge(p_lo_ready, use + 1)
                        dve.tensor_tensor(prod[:, s, :], silu[:, s, :], pB[:, :], ALU.mult).then_inc(b_read, 1)
                    if step == "U":
                        if j == E:
                            dve.wait_ge(silu_ready, use + 1)
                            dve.wait_ge(p_lo_ready, use + 1)
                        else:
                            dve.wait_ge(b_read, 1 + E * n + j + 1)
                        dve.wait_ge(pair_psum, pair + used + 1)
                        dve.tensor_tensor(prod[:, s, :], pPair[:, q, 1, :], (silu if j == E else prod)[:, s, :], ALU.mult).then_inc(prod_ready, 1)
                        dve.wait_ge(prod_ready, RING + use + 1)
                        dve.sem_inc(pair_read, 1)
                        if j == E:
                            low_half(n, b, j)
                    if step == "Y":
                        dve.wait_ge(down_done, RING + EX * (n + 1))
                        dve.wait_ge(out_stored[b], 16 * i)
                        dve.tensor_tensor(y[:, b], x2[:, b], pD[:, :, :], ALU.add).then_inc(y_sum, 1)
                    used += step in "UAX"
            run(dve, work)

        @block.tensor
        def _(pe):
            pe.sem_inc(down_done, RING)
            pe.wait_ge(filled, 1)
            pe.wait_ge(sel_ready, 1)

            def work(items, i, b, fi, fb, pair, parity):
                n, fn = 2 * i + b, 2 * fi + fb
                used = 0
                for step, j in items:
                    use, s = EX * n + j, (b + j) % 2
                    q = (parity + used) % 2
                    if step in "GAX":
                        pe.wait_ge(pair_read, pair + used + 1)
                    used += step in "UAX"
                    if step == "A":
                        pe.wait_ge(o_lo_ready, fn + 1)
                        for t in range(NTILE):
                            at = slice(P * t, P * t + P)
                            for g in range(G):
                                mm = product3(pe, pPair[:, q, t // 2, C * (t % 2):C * (t % 2) + C], o_hi[:, g, at], o_lo[:, g, at],
                                              wo_hi[:, g, :], wo_lo[:, g, :], g == 0, g == G - 1)
                        mm.then_inc(pair_psum, 1)
                    if step == "X":
                        pe.wait_ge(xn_ready, fn + 1)
                        for k in range(KT):
                            for t in range(NTILE):
                                mm = pe.transpose(pPair[:, q, k, P * t:P * t + P], xn[:, t, P * k:P * k + P], m.eye[:, :])
                        mm.then_inc(pair_psum, 1)
                    if step == "L":
                        pe.wait_ge(xT_ready, fn + 1)
                        pe.wait_ge(g_read, 2 * fn + 1)
                        for t in range(NTILE):
                            at = slice(P * t, P * t + P)
                            for k in range(KT):
                                mm = product3(pe, pG[:, E * t:E * t + E], xT_hi[:, fb, k, at], xT_lo[:, fb, k, at],
                                              gate_hi[:, k, :], gate_lo[:, k, :], k == 0, k == KT - 1)
                        mm.then_inc(g_psum, 1)
                    if step == "C":
                        pe.wait_ge(comb_ready, 2 * fn + 2)
                        for t in range(NTILE):
                            mm = pe.transpose(pG[0:E, P * t:P * t + P], comb[:, t, :], m.eye[:, :])
                        mm.then_inc(g_psum, 1)
                    if step in "GU":
                        half, hi, lo, done = (0, wg_hi, wg_lo, gate_psum) if step == "G" else (1, wu_hi, wu_lo, pair_psum)
                        for k in range(KT):
                            mm = product3(pe, pPair[:, q, half, :], hi[:, k, j, :], lo[:, k, j, :],
                                          xT_hi[:, b, k, :], xT_lo[:, b, k, :], k == 0, k == KT - 1)
                        mm.then_inc(done, 1)
                    if step == "B":
                        if j == 0:
                            pe.wait_ge(combT_ready, n + 1)
                        pe.wait_ge(b_read, E * n + j + 1)
                        pe.matmul(pB[:, :], sel[:, j, :], combT[:, b, :], start=True, stop=True).then_inc(b_psum, 1)
                    if step == "D":
                        if j == 0:
                            pe.wait_ge(y_sum, n)
                        pe.wait_ge(p_lo_ready, RING + use + 1)
                        for t in range(NTILE):
                            at = slice(P * t, P * t + P)
                            mm = product3(pe, pD[:, t, :], p_hi[:, s, at], p_lo[:, s, at], wd_hi[:, j, :], wd_lo[:, j, :],
                                          j == 0 and t % 2 == 0, j == E, skip_group_check=True)
                        mm.then_inc(down_done, 1)
            run(pe, work)


class Resident:
    pass


def adaln_moe_kernel(nc, d):
    for name, shape in (("u1", (B, T, C)), ("qk1", (2, 2, B * C, T)), ("o1", (NG, T, HG * HD1)), ("x1", (B, T, C)),
                        ("xin", (B, T, C)), ("q2", (NG, 2, 2, P, T)), ("k2", (B, 2, LAT + ROPE, T)), ("o2", (NG, P, T))):
        d[name] = nc.dram_tensor("mid_" + name, shape, FP32, kind="Internal").ap()
    m = Resident()
    with ExitStack() as ctx:
        sb = lambda n, s, t=FP32: ctx.enter_context(nc.sbuf_tensor(n, s, t))
        m.eye, m.causal = sb("eye", [P, P]), sb("causal", [P, GT])
        m.bqk, m.bv = sb("bqk", [P, 2 * KT]), sb("bv", [P, C])
        m.wln, m.ebias = sb("wln", [P, 2, KT]), sb("ebias", [P, E])
        m.eye16, m.after16 = sb("eye16", [P, P], BF16), sb("after16", [P, P], BF16)
        m.mod = sb("mod", [P, B, 6, C])
        with nc.cleanup_on_exit():
            modulation(nc, d, m)
        with ExitStack() as inner:
            m.v1 = inner.enter_context(nc.sbuf_tensor("v1", [P, NG, T // P, HG * HD1], FP32))
            with nc.cleanup_on_exit():
                project1(nc, d, m)
            with nc.cleanup_on_exit():
                attention(nc, d, m, False)
        with ExitStack() as inner:
            m.lat = inner.enter_context(nc.sbuf_tensor("lat", [P, B * T // P, LAT], FP32))
            with nc.cleanup_on_exit():
                project2(nc, d, m)
            m.wg, m.wu = (inner.enter_context(nc.sbuf_tensor(n, [P, KT, E + 1, I], FP32)) for n in ("wg", "wu"))
            m.wd = inner.enter_context(nc.sbuf_tensor("wd", [P, E + 1, C], FP32))
            m.gate = inner.enter_context(nc.sbuf_tensor("gate", [P, KT, E], FP32))
            up = lambda name: d[name].rearrange("e (k p) n -> p k e n", p=P)
            m.expert_loads = [(d["Wd"].rearrange("e p n -> p e n"), m.wd[:, 0:E, :]), (d["sWd"].rearrange("e p n -> p e n"), m.wd[:, E:, :]),
                              (d["Wgate"].rearrange("(k p) n -> p k n", p=P), m.gate[:, :, :])]
            for name, tile in (("Wg", m.wg), ("Wu", m.wu)):
                for k in range(KT):
                    m.expert_loads += [(up(name)[:, k], tile[:, k, 0:E]), (up("s" + name)[:, k], tile[:, k, E:])]
            with nc.cleanup_on_exit():
                attention(nc, d, m, True)
            with nc.cleanup_on_exit():
                experts(nc, d, m)


def kernel(**inputs):
    import numpy as _np
    import concourse.bacc as _bacc
    from concourse import mybir as _mybir
    from concourse.bass_utils import run_bass_kernel_spmd as _run

    f = {name: _np.asarray(value) for name, value in inputs.items()}
    wq = f["L0_ffn_Wq"].reshape(C, HEADS, HD2)
    turn = _np.concatenate([_np.arange(0, ROPE, 2), _np.arange(1, ROPE, 2)])
    swap = _np.concatenate([turn[ROPE // 2:], turn[:ROPE // 2]])
    wkva = f["L0_ffn_Wkva"]
    latent = wkva[:, :LAT]
    cos, sin = rope_tables()
    causal = _np.zeros((P, GT), _np.float32)
    causal[:, GT - P:] = _np.where(_np.arange(P)[None, :] > _np.arange(P)[:, None], _np.float32(NEG), _np.float32(0))
    sel = _np.zeros((64, E, P), _np.float32)
    for e in range(E):
        sel[e, e] = sel[32 + e, e] = 1
    data = {
        "x": f["L0_attn_x"], "wT": f["L0_attn_W"].T, "bqk": f["L0_attn_b"][:2 * C].reshape(-1, P).T,
        "bv": f["L0_attn_b"][2 * C:], "cT": f["L0_c"].T, "wmod": f["L0_wmod"],
        "wln": _np.stack([f["L0_ffn_w_ln1"].reshape(KT, P).T, f["L0_ffn_w_ln2"].reshape(KT, P).T], axis=1), "ebias": f["L0_ffn_expert_bias"],
        "wqnT": wq[:, :, :HD2 - ROPE].transpose(1, 2, 0).reshape(-1, C), "wkvbT": f["L0_ffn_Wkvb"].T,
        "wqr": _np.stack([wq[:, :, ROPE:][:, :, turn], wq[:, :, ROPE:][:, :, swap]], axis=1).reshape(C, -1),
        "wk": _np.concatenate([latent, wkva[:, LAT:][:, turn], latent, wkva[:, LAT:][:, turn]] + [wkva[:, LAT:][:, swap]] * 4, axis=1),
        "Wo": f["L0_ffn_Wo"], "Wgate": f["L0_ffn_Wgate"], "Wg": f["L0_ffn_Wg"], "Wu": f["L0_ffn_Wu"], "Wd": f["L0_ffn_Wd"],
        "sWg": f["L0_ffn_sWg"], "sWu": f["L0_ffn_sWu"], "sWd": f["L0_ffn_sWd"],
        "eye": _np.eye(P, dtype=_np.float32), "causal": causal, 
        "cos": _np.stack([_np.tile(cos, (4, 1)), _np.tile(_np.concatenate([_np.ones_like(cos), cos]), (2, 1))], axis=1),
        "sin": _np.stack([_np.tile(sin, (4, 1)), _np.tile(_np.concatenate([_np.zeros_like(sin), sin]), (2, 1))], axis=1),
        "sel": sel.reshape(64, -1), "rank": _np.arange(E, 0, -1).astype(_np.float32),
    }
    nc = _bacc.Bacc("TRN2", target_bir_lowering=False, num_devices=1)
    arrays, d = {}, {}
    for name, a in data.items():
        a = _np.ascontiguousarray(a)
        arrays[f"in_{name}_dram"] = a
        d[name] = nc.dram_tensor(f"in_{name}_dram", a.shape, _mybir.dt.from_np(a.dtype), kind="ExternalInput").ap()
    d["out"] = nc.dram_tensor("out_0_dram", (B, T, C), _mybir.dt.from_np(_np.dtype("float32")), kind="ExternalOutput").ap()
    adaln_moe_kernel(nc, d)
    r = _run(nc, [arrays], core_ids=[0])
    return r.results[0]["out_0_dram"]
```
